# Optimizing a Trainium2 kernel written in Bass

```python
import numpy as np
import jax
import jax.numpy as jnp

def _softmax(x, axis=-1):
    return jax.nn.softmax(x, axis=axis)

def _gelu(x):
    return jax.nn.gelu(x, approximate=True)

def _silu(x):
    return jax.nn.silu(x)

def _sigmoid(x):
    return jax.nn.sigmoid(x)

def _layernorm(x, axis=-1, eps=1e-05):
    m = jnp.mean(x, axis=axis, keepdims=True)
    v = jnp.var(x, axis=axis, keepdims=True)
    return (x - m) / jnp.sqrt(v + eps)

def _scatter_add(tgt, idx, src, axis=0):
    return tgt.at[idx].add(src)

def _segment_sum(src, seg, n):
    return jax.ops.segment_sum(src, seg, n)
kernel_name = 'mk_gnn_preln_d4_gnn_r16_04ef42'

def setup_inputs(seed: int=0):
    np.random.seed(seed)
    _w = jnp.asarray

    def _rec_inputs():
        import jax
        import jax.numpy as jnp
        _gk = jax.random.key(seed)
        x = -0.0005121 + 1.001 * jax.random.normal(jax.random.fold_in(_gk, 1), (3125, 64), jnp.float32)
        src = jax.random.randint(jax.random.fold_in(_gk, 2), (100000,), 0, 3125, jnp.int32)
        dst = jax.random.randint(jax.random.fold_in(_gk, 3), (100000,), 0, 3125, jnp.int32)
        _o = jnp.argsort(dst, stable=True)
        src = src[_o]
        dst = dst[_o]
        edge_attr_64 = -8.16379e-05 + 0.999858 * jax.random.normal(jax.random.fold_in(_gk, 12), (100000, 64), jnp.float32)
        return (x, src, dst, edge_attr_64)
    x, src, dst, edge_attr_64 = _rec_inputs()

    def _L0_gnn_setup():
        import jax, jax.numpy as jnp
        import numpy as np
        N = 3125
        E = 50000
        DIN = 64
        DEMB = 64
        H = 4
        DH = DEMB // H
        DFFN = DIN
        SLOPE = 0.2
        key = jax.random.key(seed)
        ks = jax.random.split(key, 9)
        s = 0.05
        return {'node_attr': jax.random.normal(ks[0], (N, DIN), jnp.float32), 'edge_index': jax.random.randint(ks[1], (E, 2), 0, N, dtype=jnp.int32), 'Wl': jax.random.normal(ks[2], (DEMB, DIN), jnp.float32) * s, 'Wr': jax.random.normal(ks[3], (DEMB, DIN), jnp.float32) * s, 'att': jax.random.normal(ks[4], (1, H, DH), jnp.float32) * s, 'W1': jax.random.normal(ks[5], (DFFN, DEMB + DIN), jnp.float32) * s, 'b1': jnp.zeros((DFFN,), jnp.float32), 'W2': jax.random.normal(ks[6], (DEMB, DFFN), jnp.float32) * s, 'b2': jnp.zeros((DEMB,), jnp.float32)}
    _L0_gnn_all = _L0_gnn_setup()
    _L0_gnn_in = {k: v for k, v in _L0_gnn_all.items() if k in ('Wl', 'Wr', 'att', 'W1', 'b1', 'W2', 'b2')}
    del _L0_gnn_all

    def _L1_gnn_setup():
        import jax, jax.numpy as jnp
        import numpy as np
        N = 6250
        E = 100000
        D = 64
        key = jax.random.key(seed)
        ks = jax.random.split(key, 6)
        scale = 1.0 / np.sqrt(3 * D)
        return {'h_e': jax.random.normal(ks[0], (N, D), dtype=jnp.float32), 'h_r': jax.random.normal(ks[1], (E, D), dtype=jnp.float32), 'W1': jax.random.normal(ks[2], (3 * D, D), dtype=jnp.float32) * scale, 'b1': jnp.zeros((D,), dtype=jnp.float32), 'W2': jax.random.normal(ks[3], (3 * D, D), dtype=jnp.float32) * scale, 'b2': jnp.zeros((D,), dtype=jnp.float32), 'edge_index': jax.random.randint(ks[4], (2, E), 0, N, dtype=jnp.int64)}
    _L1_gnn_all = _L1_gnn_setup()
    _L1_gnn_in = {k: v for k, v in _L1_gnn_all.items() if k in ('W1', 'b1', 'W2', 'b2')}
    del _L1_gnn_all

    def _L2_gnn_setup():
        import jax, jax.numpy as jnp
        import numpy as np
        V = 6250
        E = 100000
        C_IN = 64
        C_OUT = 64
        key = jax.random.key(seed)
        k1, k2, k3, k4, k5 = jax.random.split(key, 5)
        features = jax.random.normal(k1, (V, C_IN), dtype=jnp.float32)
        src = jax.random.randint(k2, (E,), 0, V, dtype=jnp.int32)
        tgt = jnp.sort(jax.random.randint(k3, (E,), 0, V, dtype=jnp.int32))
        W = jax.random.normal(k4, (C_OUT, 2 * C_IN), dtype=jnp.float32) * (1.0 / np.sqrt(2 * C_IN))
        b = jax.random.normal(k5, (C_OUT,), dtype=jnp.float32) * 0.01
        return {'features': features, 'src': src, 'tgt': tgt, 'W': W, 'b': b}
    _L2_gnn_all = _L2_gnn_setup()
    _L2_gnn_in = {k: v for k, v in _L2_gnn_all.items() if k in ('W', 'b')}
    del _L2_gnn_all

    def _L3_gnn_setup():
        import jax, jax.numpy as jnp
        import numpy as np
        N, E, D, H = (3125, 31250, 64, 8)
        LN_EPS = 1e-05
        SM_EPS = 1e-16
        SLOPE = 0.2

        def layer_norm(x, g, b):
            mu = jnp.mean(x, axis=-1, keepdims=True)
            var = jnp.mean((x - mu) ** 2, axis=-1, keepdims=True)
            return (x - mu) * jax.lax.rsqrt(var + LN_EPS) * g + b
        key = jax.random.key(seed)
        ks = jax.random.split(key, 12)
        glorot = lambda k, shape: jax.random.normal(k, shape, jnp.float32) * np.sqrt(2.0 / (shape[0] + shape[-1]))
        return {'x': jax.random.normal(ks[0], (N, D), jnp.float32), 'edge_index': jax.random.randint(ks[1], (2, E), 0, N, jnp.int64), 'W_att': glorot(ks[2], (D, H * D)), 'att_src': glorot(ks[3], (H, D)), 'att_dst': glorot(ks[4], (H, D)), 'bias_att': jnp.zeros((D,), jnp.float32), 'W1': glorot(ks[5], (D, 2 * D)), 'b1': jnp.zeros((2 * D,), jnp.float32), 'W2': glorot(ks[6], (2 * D, D)), 'b2': jnp.zeros((D,), jnp.float32), 'ln1_g': jnp.ones((D,), jnp.float32), 'ln1_b': jnp.zeros((D,), jnp.float32), 'ln2_g': jnp.ones((D,), jnp.float32), 'ln2_b': jnp.zeros((D,), jnp.float32)}
    _L3_gnn_all = _L3_gnn_setup()
    _L3_gnn_in = {k: v for k, v in _L3_gnn_all.items() if k in ('W_att', 'att_src', 'att_dst', 'bias_att', 'W1', 'b1', 'W2', 'b2', 'ln1_g', 'ln1_b', 'ln2_g', 'ln2_b')}
    del _L3_gnn_all
    return {'x': x, 'src': src, 'dst': dst, 'edge_attr_64': edge_attr_64, 'L0_gnn_Wl': _L0_gnn_in['Wl'], 'L0_gnn_Wr': _L0_gnn_in['Wr'], 'L0_gnn_att': _L0_gnn_in['att'], 'L0_gnn_W1': _L0_gnn_in['W1'], 'L0_gnn_b1': _L0_gnn_in['b1'], 'L0_gnn_W2': _L0_gnn_in['W2'], 'L0_gnn_b2': _L0_gnn_in['b2'], 'L1_gnn_W1': _L1_gnn_in['W1'], 'L1_gnn_b1': _L1_gnn_in['b1'], 'L1_gnn_W2': _L1_gnn_in['W2'], 'L1_gnn_b2': _L1_gnn_in['b2'], 'L2_gnn_W': _L2_gnn_in['W'], 'L2_gnn_b': _L2_gnn_in['b'], 'L3_gnn_W_att': _L3_gnn_in['W_att'], 'L3_gnn_att_src': _L3_gnn_in['att_src'], 'L3_gnn_att_dst': _L3_gnn_in['att_dst'], 'L3_gnn_bias_att': _L3_gnn_in['bias_att'], 'L3_gnn_W1': _L3_gnn_in['W1'], 'L3_gnn_b1': _L3_gnn_in['b1'], 'L3_gnn_W2': _L3_gnn_in['W2'], 'L3_gnn_b2': _L3_gnn_in['b2'], 'L3_gnn_ln1_g': _L3_gnn_in['ln1_g'], 'L3_gnn_ln1_b': _L3_gnn_in['ln1_b'], 'L3_gnn_ln2_g': _L3_gnn_in['ln2_g'], 'L3_gnn_ln2_b': _L3_gnn_in['ln2_b']}

def reference(x, src, dst, edge_attr_64, L0_gnn_Wl, L0_gnn_Wr, L0_gnn_att, L0_gnn_W1, L0_gnn_b1, L0_gnn_W2, L0_gnn_b2, L1_gnn_W1, L1_gnn_b1, L1_gnn_W2, L1_gnn_b2, L2_gnn_W, L2_gnn_b, L3_gnn_W_att, L3_gnn_att_src, L3_gnn_att_dst, L3_gnn_bias_att, L3_gnn_W1, L3_gnn_b1, L3_gnn_W2, L3_gnn_b2, L3_gnn_ln1_g, L3_gnn_ln1_b, L3_gnn_ln2_g, L3_gnn_ln2_b):
    import jax
    import jax.numpy as jnp

    def _L0_gnn_ref(node_attr, edge_index, Wl, Wr, att, W1, b1, W2, b2):
        import jax, jax.numpy as jnp
        import numpy as np
        N = 3125
        E = 50000
        DIN = 64
        DEMB = 64
        H = 4
        DH = DEMB // H
        DFFN = DIN
        SLOPE = 0.2
        ngl = (node_attr @ Wl.T).reshape(N, H, DH)
        ngr = (node_attr @ Wr.T).reshape(N, H, DH)
        idx = jnp.concatenate([edge_index, edge_index[:, ::-1]], axis=0)
        src, dst = (idx[:, 0], idx[:, 1])
        gl = ngl[src]
        gr = ngr[dst]
        score = (att * jax.nn.leaky_relu(gl + gr, SLOPE)).sum(-1)
        m = jax.ops.segment_max(score, src, num_segments=N)
        ex = jnp.exp(score - m[src])
        denom = jax.ops.segment_sum(ex, src, num_segments=N)
        alpha = ex / (denom[src] + 1e-16)
        out = jax.ops.segment_sum(gr * alpha[:, :, None], src, num_segments=N)
        out = out.reshape(N, H * DH)
        h = jnp.concatenate([out, node_attr], axis=1)
        h = jax.nn.gelu(h @ W1.T + b1, approximate=False)
        return h @ W2.T + b2

    def _L1_gnn_ref(h_e, h_r, W1, b1, W2, b2, edge_index):
        import jax, jax.numpy as jnp
        import numpy as np
        N = 6250
        E = 100000
        D = 64
        src = edge_index[0]
        dst = edge_index[1]
        n = h_e.shape[0]
        deg = jax.ops.segment_sum(jnp.ones((src.shape[0],), h_e.dtype), dst, num_segments=n)
        inv_deg = (1.0 / jnp.maximum(deg, 1.0))[:, None]
        nbr_r = jax.ops.segment_sum(h_r, dst, num_segments=n) * inv_deg

        def layer(h, W, b):
            nbr_x = jax.ops.segment_sum(h[src], dst, num_segments=n) * inv_deg
            z = jnp.concatenate([h, nbr_x, nbr_r], axis=1)
            return jax.nn.relu(z @ W + b)
        h = layer(h_e, W1, b1)
        h = layer(h, W2, b2)
        return h

    def _L2_gnn_ref(features, src, tgt, W, b):
        import jax, jax.numpy as jnp
        import numpy as np
        V = 6250
        E = 100000
        C_IN = 64
        C_OUT = 64
        num_v = features.shape[0]
        local = features[tgt]
        nbr = features[src]
        x = jnp.concatenate([local, nbr - local], axis=-1)
        y = jnp.einsum('ec,oc->eo', x, W) + b
        s = jax.ops.segment_sum(y, tgt, num_segments=num_v)
        cnt = jax.ops.segment_sum(jnp.ones((y.shape[0],), y.dtype), tgt, num_segments=num_v)
        cnt = cnt[:, None]
        return jnp.where(cnt > 0, s / jnp.maximum(cnt, 1.0), 0.0)

    def _L3_gnn_ref(x, edge_index, W_att, att_src, att_dst, bias_att, W1, b1, W2, b2, ln1_g, ln1_b, ln2_g, ln2_b):
        import jax, jax.numpy as jnp
        import numpy as np
        N, E, D, H = (3125, 31250, 64, 8)
        LN_EPS = 1e-05
        SM_EPS = 1e-16
        SLOPE = 0.2

        def layer_norm(x, g, b):
            mu = jnp.mean(x, axis=-1, keepdims=True)
            var = jnp.mean((x - mu) ** 2, axis=-1, keepdims=True)
            return (x - mu) * jax.lax.rsqrt(var + LN_EPS) * g + b
        n = x.shape[0]
        h = (x @ W_att).reshape(n, H, D)
        a_src = jnp.einsum('nhc,hc->nh', h, att_src)
        a_dst = jnp.einsum('nhc,hc->nh', h, att_dst)
        loops = jnp.arange(n, dtype=edge_index.dtype)
        src = jnp.concatenate([edge_index[0], loops])
        dst = jnp.concatenate([edge_index[1], loops])
        e = a_src[src] + a_dst[dst]
        e = jnp.where(e > 0, e, SLOPE * e)
        m = jax.ops.segment_max(e, dst, num_segments=n)
        e = jnp.exp(e - m[dst])
        s = jax.ops.segment_sum(e, dst, num_segments=n)
        alpha = e / (s[dst] + SM_EPS)
        msg = alpha[:, :, None] * h[src]
        out = jax.ops.segment_sum(msg, dst, num_segments=n)
        att_out = out.mean(axis=1) + bias_att
        x1 = layer_norm(att_out + x, ln1_g, ln1_b)
        ff = jax.nn.relu(x1 @ W1 + b1) @ W2 + b2
        return layer_norm(ff + x1, ln2_g, ln2_b)
    edge_index = jnp.stack([src, dst])
    edge_index_t = jnp.stack([src, dst], axis=1)
    h = jnp.maximum(_layernorm(x, axis=-1), 0.0)
    x = x + _L0_gnn_ref(h, edge_index_t, L0_gnn_Wl, L0_gnn_Wr, L0_gnn_att, L0_gnn_W1, L0_gnn_b1, L0_gnn_W2, L0_gnn_b2)
    h = jnp.maximum(_layernorm(x, axis=-1), 0.0)
    x = x + _L1_gnn_ref(h, edge_attr_64, L1_gnn_W1, L1_gnn_b1, L1_gnn_W2, L1_gnn_b2, edge_index)
    h = jnp.maximum(_layernorm(x, axis=-1), 0.0)
    x = x + _L2_gnn_ref(h, src, dst, L2_gnn_W, L2_gnn_b)
    h = jnp.maximum(_layernorm(x, axis=-1), 0.0)
    x = x + _L3_gnn_ref(h, edge_index, L3_gnn_W_att, L3_gnn_att_src, L3_gnn_att_dst, L3_gnn_bias_att, L3_gnn_W1, L3_gnn_b1, L3_gnn_W2, L3_gnn_b2, L3_gnn_ln1_g, L3_gnn_ln1_b, L3_gnn_ln2_g, L3_gnn_ln2_b)
    return x

_drawn_inputs = setup_inputs


def setup_inputs(seed=0):
    import zlib

    import numpy as np

    out = dict(_drawn_inputs(seed))
    spreads = {'L0_gnn_b1': (0.0, 0.353),
     'L0_gnn_b2': (0.0, 0.1),
     'L1_gnn_b1': (0.0, 0.299),
     'L1_gnn_b2': (0.0, 0.1),
     'L3_gnn_bias_att': (0.0, 0.1),
     'L3_gnn_b1': (0.0, 0.1),
     'L3_gnn_b2': (0.0, 0.1),
     'L3_gnn_ln1_g': (1.0, 0.2),
     'L3_gnn_ln1_b': (0.0, 0.1),
     'L3_gnn_ln2_g': (1.0, 0.2),
     'L3_gnn_ln2_b': (0.0, 0.1)}
    factors = {'L0_gnn_Wl': 8.0,
     'L0_gnn_Wr': 4.015,
     'L0_gnn_att': 8.0,
     'L2_gnn_b': 6.508,
     'L3_gnn_att_src': 8.0,
     'L3_gnn_att_dst': 8.0}
    for name, (base, spread) in spreads.items():
        noise = np.random.default_rng([zlib.crc32(name.encode()), seed]).standard_normal(out[name].shape)
        drawn = base * np.exp(spread * noise) if base else spread * noise
        out[name] = jnp.asarray(drawn.astype(out[name].dtype))
    for name, factor in factors.items():
        out[name] = (out[name] * factor).astype(out[name].dtype)
    return out
```

```python
import concourse.bass as bass
from concourse import mybir
from contextlib import ExitStack

N, D, E = 3125, 64, 100000
P = 128
NC = -(-N // P)
NF = N // P
NR = N - NF * P
NP = NC * P
EP = 125
EC = E // EP
NT = 816
assert NT * P >= E + NC * (P - 1)
GT = 8
PAIRS = NT // (2 * GT)
PAIRS0 = 2 * PAIRS
SG = EC // (2 * GT)
REC = D + 2
EPS = 1e-5
BIG = 1e30
H0, H3 = 4, 8


def build(nc, t, out):
    F, I, U = mybir.dt.float32, mybir.dt.int32, mybir.dt.uint32
    ALU, ACT, AX = mybir.AluOpType, mybir.ActivationFunctionType, mybir.AxisListType.X
    ctx = ExitStack()
    with ctx:
        def sb(name, shape, dt=F):
            return ctx.enter_context(nc.sbuf_tensor(name, shape, dt))

        def ps(name, shape):
            return ctx.enter_context(nc.psum_tensor(name, shape, F))

        def sem(name):
            return ctx.enter_context(nc.semaphore(name))

        rec = nc.dram_tensor("rec_dram", (P * NT, REC), F).ap()
        recv = rec.rearrange("(p t) f -> p t f", p=P)
        slist = nc.dram_tensor("slist_dram", (P * NT, 2), F).ap()
        slv = slist.rearrange("(p t) f -> p t f", p=P)
        tab = [nc.dram_tensor(f"tab{k}_dram", (NP, w), F).ap() for k, w in enumerate((D, D, D, D, D + H3))]
        stash = nc.dram_tensor("stash_dram", (P, 2 * NT, D + H3), F).ap()

        iota = sb("iota", [P, NT])
        iota1 = iota[:, 0:P]
        ones = sb("ones", [P, P])
        zrow = sb("zrow", [1, 512])
        tri = sb("tri", [P, P])
        triinc = sb("triinc", [P, P])
        ident = sb("ident", [P, P])

        jidx = sb("jidx", [P, 2 * NT], U)
        iloc = sb("iloc", [P, 2 * NT])
        ctab = sb("ctab", [1, 2 * NT], I)

        arena = sb("arena", [P, 13312])
        score = sb("score", [P, 2 * NT * H0])

        def cols(k, dt=F):
            v = arena[0:EP, k * EC:(k + 1) * EC]
            return v if dt == F else v.bitcast(dt)
        key_i = [cols(0, I), cols(1, I)]
        idf = [cols(2), cols(3)]
        lof = [cols(4), cols(5)]
        bkf = [cols(6), cols(7)]
        slot = [cols(8), cols(9)]
        mask = [cols(10), cols(11)]
        pos = [cols(12), cols(13)]
        sone = cols(14)
        low_i = cols(15, I)
        iota_i = score[:, 5 * NT:6 * NT].bitcast(I)
        gmat = score[0:NC, 0:2 * NT].rearrange("p (l t) -> p l t", l=2)
        rowidx = [score[0:EP, 2 * NT + l * EC:2 * NT + (l + 1) * EC].bitcast(U) for l in range(2)]
        blank = sb("blank", [P, GT, REC])
        slraw = sb("slraw", [P, NT, 2])
        cnt = [sb("cnt0", [EP, NC]), sb("cnt1", [EP, NC])]
        off = [sb("off0", [EP, NC]), sb("off1", [EP, NC])]
        tcol_i = sb("tcol_i", [NC, 2], I)
        tcol = sb("tcol", [NC, 2])
        t128 = sb("t128", [NC, 2, EP])
        endc = sb("endc", [NC, 2])

        recst = sb("recst", [EP, 2, GT, REC])
        sst = sb("sst", [EP, 2, GT, 2])
        rowst = sb("rowst", [EP, 2, GT], U)
        pdum = sb("pdum", [P, 2])
        vdum = sb("vdum", [1, 1])

        G = sb("G", [P, 2, GT, D + H3])
        oh = sb("oh", [P, 2, GT, P])
        ohT = sb("ohT", [P, 2, GT, P])
        pen = sb("pen", [P, 2, GT, P])
        jst = sb("jst", [P, 2, GT], U)
        work = sb("work", [P, GT, D])
        scst = sb("scst", [P, 2, GT, H0])
        mx = sb("mx", [P, GT, H3])
        w = sb("w", [P, 2, GT, H3])
        V0 = sb("V0", [P, 2, GT, D])
        junk = sb("junk", [P, H3, P])

        X = sb("X", [P, NC, D])
        Hn = sb("Hn", [P, NC, D])
        M = sb("M", [P, NC * H3])
        AS = sb("AS", [P, NC, 2 * H3])
        es = sb("es", [P, NC, H3])
        rden = sb("rden", [P, NC, H3])
        w8 = sb("w8", [P, 2, GT, H3])
        b1c0 = sb("b1c0", [D, 1]); b1c3 = sb("b1c3", [2 * D, 1])
        BM = sb("BM", [P, NC, 2 * H3])
        st = sb("st", [P, 4, NC])
        invdeg = sb("invdeg", [P, NC])
        hasin = sb("hasin", [P, NC])
        nbr_r = sb("nbr_r", [P, NC, D])
        deg = sb("deg", [P, NC])

        def area(k, n=1):
            return arena[:, k * NC * D:(k + n) * NC * D]
        GL = area(0).rearrange("p (c d) -> p c d", d=D)
        GR = area(3).rearrange("p (c d) -> p c d", d=D)
        NRT = area(1, 2)[0:D, :]
        CAT = area(4, 2).rearrange("p (c d) -> p c d", d=2 * D)
        T = area(6, 2)
        XC = score[:, 3328:3328 + NC * D].rearrange("p (c d) -> p c d", d=D)
        SQ = score[:, 3328 + NC * D:3328 + 2 * NC * D].rearrange("p (c d) -> p c d", d=D)
        T2 = area(4, 2)
        TT = [ohT[:, q, 0:4, :].rearrange("p t n -> p (t n)") for q in range(2)]
        TB3 = arena[:, 0:NC * (D + H3)].rearrange("p (c d) -> p c d", d=D + H3)
        OUTN = XC
        acc3 = arena[:, 0:NC * H3 * D]

        wraw = sb("wraw", [D, 7 * D])
        WT = sb("WT", [P, 5, D])
        W1a = sb("W1a", [P, 2, D]); W1b = sb("W1b", [D, 2, D])
        Wp = sb("Wp", [P, 4, D])
        watt = V0[0:D].rearrange("p q t d -> p (q t d)")[:, 0:H3 * D]
        attsd = ohT[0:D].rearrange("p q t d -> p (q t d)")[:, 0:2 * H3 * D].rearrange("p (s f) -> p s f", s=2)
        Asd = sb("Asd", [D, 2, H3])
        F1 = sb("F1", [D, 2 * D]); F2 = sb("F2", [2 * D, D])
        attb = sb("attb", [P, D])
        bias = sb("bias", [1, 5, D])
        lnb = sb("lnb", [P, 5, D])

        acc = ps("acc", [P, 4 * 512])
        accw = ps("accw", [P, 512])
        pu = ps("pu", [P, 512])
        pt = ps("pt", [P, 1024])

        names = """iota rcp jdone const keys v cnt tot tcol end gm ct ctab rows blank fill attr0 attr1 recst pd scat0 scat1 sst
            sscat0 sscat1 rld0 rld1 roh rmm vl slist nbr x wts wtp wtc lnv lns tsrc tp tc lin ev tb up upc xp
            aj0 aj1 ag0 ag1 ast0 ast1 aoh atr aoht apen apu au ascc ab amx m0
            bld0 bld1 boh btr boht bpm bd bw bv bagg
            cj0 cj1 cg0 cg1 coh cmm
            dj0 dj1 dg0 dg1 dst0 dst1 doh dtr dpen db dmx bm
            eld0 eld1 eoh etr eoht epm ed ew ev3 ead emm
            es fac ftp ftc fmm out""".split()
        S = {x: sem("s_" + x) for x in names}

        attr_v = t["edge_attr_64"].rearrange("(p j) d -> p j d", p=EP)

        block = ctx.enter_context(nc.Block())

        def pairs(eng, n, body):
            for q in range(2):
                body(0, q, True)
            with eng.Fori(1, n) as i:
                for q in range(2):
                    body(i, q, False)

        def pipe(eng, n, step):
            step((0, 0, True), None)
            step((0, 1, True), (0, 0, True))
            step((1, 0, False), (0, 1, True))
            with eng.Fori(1, n - 1) as i:
                step((i, 1, False), (i, 0, False))
                step((i + 1, 0, False), (i, 1, False))
            step((n - 1, 1, False), (n - 1, 0, False))
            step(None, (n - 1, 1, False))

        @block.sync
        def _(sp):
            sp.dma_start(key_i[0], t["dst"].rearrange("(p j) -> p j", p=EP)).then_inc(S["keys"], 16)
            sp.dma_start(key_i[1], t["src"].rearrange("(p j) -> p j", p=EP)).then_inc(S["keys"], 16)
            sp.wait_ge(S["x"], 1)
            sp.dma_start(X[:, 0:NF, :], t["x"][0:NF * P, :].rearrange("(c p) d -> p c d", p=P)).then_inc(S["wts"], 16)
            sp.dma_start(X[0:NR, NF, :], t["x"][NF * P:N, :]).then_inc(S["wts"], 16)
            at = 0
            for name, wd in (("L0_gnn_Wl", D), ("L0_gnn_Wr", D), ("L0_gnn_W1", 2 * D), ("L0_gnn_W2", D), ("L2_gnn_W", 2 * D)):
                sp.dma_start(wraw[:, at:at + wd], t[name]).then_inc(S["wts"], 16)
                at += wd
            for k in range(2):
                sp.dma_start(W1a[:, k, :], t[f"L1_gnn_W{k + 1}"][0:2 * D, :]).then_inc(S["wts"], 16)
                sp.dma_start(W1b[:, k, :], t[f"L1_gnn_W{k + 1}"][2 * D:3 * D, :]).then_inc(S["wts"], 16)
                sp.dma_start(Wp[k * D:(k + 1) * D, :, :],
                             t["L3_gnn_W_att"].rearrange("d (q h c) -> h d q c", h=2, c=D)[k]).then_inc(S["wts"], 16)
                sp.dma_start(attsd[:, k, :], t["L3_gnn_att_" + ("src", "dst")[k]].rearrange("h c -> (h c)").unsqueeze(0)
                             .to_broadcast([D, H3 * D])).then_inc(S["wts"], 16)
            sp.dma_start(watt, t["L3_gnn_W_att"]).then_inc(S["wts"], 16)
            sp.dma_start(F1[:], t["L3_gnn_W1"]).then_inc(S["wts"], 16)
            sp.dma_start(F2[:], t["L3_gnn_W2"]).then_inc(S["wts"], 16)
            sp.dma_start(attb[:], t["L0_gnn_att"].rearrange("o h d -> o (h d)").to_broadcast([P, D])).then_inc(S["wts"], 16)
            for k, name in enumerate(("L0_gnn_b2", "L1_gnn_b1", "L1_gnn_b2", "L2_gnn_b", "L3_gnn_b2")):
                sp.dma_start(bias[:, k, :], t[name].unsqueeze(0)).then_inc(S["wts"], 16)
            for k, name in enumerate(("L3_gnn_bias_att", "L3_gnn_ln1_g", "L3_gnn_ln1_b", "L3_gnn_ln2_g", "L3_gnn_ln2_b")):
                sp.dma_start(lnb[:, k, :], t[name].unsqueeze(0).to_broadcast([P, D])).then_inc(S["wts"], 16)
            sp.dma_start(b1c0[:], t["L0_gnn_b1"].unsqueeze(1)).then_inc(S["wts"], 16)
            sp.dma_start(b1c3[:], t["L3_gnn_b1"].unsqueeze(1)).then_inc(S["wts"], 16)
            sp.wait_ge(S["blank"], 4)
            for k in range(NT // (GT * 6)):
                sp.dma_start(recv[:, k * 48:(k + 1) * 48, :].rearrange("p (a b) f -> p a (b f)", b=GT),
                             blank[:].rearrange("p b f -> p (b f)").unsqueeze(1).to_broadcast([P, 6, GT * REC])).then_inc(S["fill"], 16)
            sp.dma_start(slv, slraw[:]).then_inc(S["fill"], 16)

            def attrs(i, q, first):
                if not first:
                    sp.wait_ge(S[f"scat{q}"], i * 16 * GT)
                sp.dma_start(recst[:, q, :, 0:D], attr_v[:, bass.ds(i * 16 + q * 8, GT), :]).then_inc(S[f"attr{q}"], 16)
            pairs(sp, SG, attrs)

            for q in range(2):
                sp.wait_ge(S[f"scat{q}"], SG * 16 * GT)

            def recs(i, q, first):
                if not first:
                    sp.wait_ge(S["rmm"], i * 2 + q - 1)
                sp.dma_start(G[:, q, :, 0:REC], recv[:, bass.ds(i * 16 + q * 8, GT), :]).then_inc(S[f"rld{q}"], 16)
            pairs(sp, PAIRS, recs)
            for q in range(2):
                sp.wait_ge(S[f"sscat{q}"], SG * 16 * GT)
            sp.dma_start(slraw[:], slv).then_inc(S["slist"], 16)

            def table(k, n, src):
                sp.wait_ge(S["tsrc"], n)
                sp.dma_start(tab[k].rearrange("(c p) d -> p c d", p=P), src).then_inc(S["tb"], 16)

            def stage_gathers(x, npairs, R0, wd, stashed):
                def body(i, q, first):
                    t0 = bass.ds(i * 16 + q * 8, GT)
                    if not first or R0:
                        sp.wait_ge(S[f"{x}g{q}"], (R0 + i) * 16 * GT)
                    if stashed and not first:
                        sp.dma_start(stash[:, bass.ds(i * 16 + q * 8 - 16, GT), 0:wd], G[:, q, :, 0:wd]).then_inc(S[f"{x}st{q}"], 16)
                    sp.dma_start(jst[:, q, :], jidx[:, t0]).then_inc(S[f"{x}j{q}"], 16)
                pairs(sp, npairs, body)
                for q in range(2):
                    sp.wait_ge(S[f"{x}g{q}"], (R0 + npairs) * 16 * GT)
                    if stashed:
                        sp.dma_start(stash[:, npairs * 16 - 16 + q * 8:npairs * 16 - 8 + q * 8, 0:wd],
                                     G[:, q, :, 0:wd]).then_inc(S[f"{x}st{q}"], 16)

            def load_stash(x, npairs, wd, freed):
                def body(i, q, first):
                    if not first:
                        sp.wait_ge(*freed(i, q))
                    sp.dma_start(G[:, q, :, 0:wd], stash[:, bass.ds(i * 16 + q * 8, GT), 0:wd]).then_inc(S[f"{x}ld{q}"], 16)
                pairs(sp, npairs, body)

            table(0, 1, GR)
            sp.wait_ge(S["jdone"], 1)
            stage_gathers("a", PAIRS0, 0, D, True)
            for q in range(2):
                sp.wait_ge(S[f"ast{q}"], PAIRS0 * 16)
            sp.wait_ge(S["au"], 4 * 2 * PAIRS0)
            load_stash("b", PAIRS0, D, lambda i, q: (S["bv"], i * 2 + q - 1))
            for r in range(3):
                table(1 + r, 2 + r, Hn[:])
                stage_gathers("c", PAIRS, r * PAIRS, D, False)
            table(4, 5, TB3)
            stage_gathers("d", PAIRS, 0, D + H3, True)
            for q in range(2):
                sp.wait_ge(S[f"dst{q}"], PAIRS * 16)
            sp.wait_ge(S["db"], 16 * PAIRS)
            load_stash("e", PAIRS, D + H3, lambda i, q: (S["ev3"], (i * 2 + q - 1) * GT))
            sp.wait_ge(S["xp"], 1)
            sp.dma_start(out[0:NF * P, :].rearrange("(c p) d -> p c d", p=P), OUTN[:, 0:NF, :]).then_inc(S["out"], 16)
            sp.dma_start(out[NF * P:N, :], OUTN[0:NR, NF, :]).then_inc(S["out"], 16)
            sp.wait_ge(S["out"], 32)

        @block.gpsimd
        def _(gp):
            gp.iota(iota_i[:], [[1, NT]], base=0, channel_multiplier=0).then_inc(S["iota"], 1)
            gp.memset(ones[:], 1.0).then_inc(S["const"], 1)
            gp.memset(zrow[:], 0.0).then_inc(S["const"], 1)
            gp.memset(pdum[:], 0.0).then_inc(S["pd"], 1)
            gp.memset(X[:], 0.0).then_inc(S["x"], 1)
            gp.memset(blank[:], 0.0).then_inc(S["blank"], 1)
            gp.memset(slraw[:], 0.0).then_inc(S["blank"], 1)
            gp.wait_ge(S["blank"], 2)
            gp.memset(blank[:, :, D + 1:REC], -1.0).then_inc(S["blank"], 1)
            gp.memset(slraw[:, :, 1:2], -1.0).then_inc(S["blank"], 1)
            gp.wait_ge(S["const"], 2)
            gp.affine_select(out=tri[:], in_=ones[:], compare_op=ALU.is_gt, fill=0.0, base=0,
                             pattern=[[1, P]], channel_multiplier=-1).then_inc(S["const"], 1)
            gp.affine_select(out=triinc[:], in_=ones[:], compare_op=ALU.is_ge, fill=0.0, base=0,
                             pattern=[[1, P]], channel_multiplier=-1).then_inc(S["const"], 1)
            gp.affine_select(out=ident[:], in_=ones[:], compare_op=ALU.is_equal, fill=0.0, base=0,
                             pattern=[[1, P]], channel_multiplier=-1).then_inc(S["const"], 1)
            gp.wait_ge(S["fill"], 16 * 18)

            def hold(sem_, val, count):
                gp.wait_ge(S["pd"], count)
                gp.wait_ge(sem_, val)
                nc.gpsimd.tensor_tensor(pdum[:, 1:2], pdum[:, 0:1], pdum[:, 0:1], ALU.add).then_inc(S["pd"], 1)

            def scatter_recs(i, q, first):
                hold(S[f"attr{q}"], (i + 1) * 16, i * 4 + 2 * q + 1)
                hold(S["recst"], (2 * i + q + 1) * 3, i * 4 + 2 * q + 2)
                for k in range(GT):
                    gp.indirect_dma_start(rec[:, :], bass.IndirectOffsetOnAxis(ap=rowst[:, q, k:k + 1], axis=0),
                                          recst[:, q, k, :], None).then_inc(S[f"scat{q}"], 16)
            pairs(gp, SG, scatter_recs)

            def scatter_s(i, q, first):
                hold(S["sst"], (2 * i + q + 1) * 3, SG * 4 + 2 * i + q + 1)
                for k in range(GT):
                    gp.indirect_dma_start(slist[:, :], bass.IndirectOffsetOnAxis(ap=rowst[:, q, k:k + 1], axis=0),
                                          sst[:, q, k, :], None).then_inc(S[f"sscat{q}"], 16)
            pairs(gp, SG, scatter_s)
            held = [SG * 6 + 1]

            def gather(x, npairs, R0, k, wd, freed):
                gp.wait_ge(S["tb"], 16 * (k + 1))
                nh = 1 + len(freed(1, 0))

                def body(i, q, first):
                    at = held[0] + (2 * i + q) * nh
                    waits = [] if first and not R0 else freed(i, q)
                    waits = waits + [(S[f"{x}j{q}"], (R0 + i + 1) * 16)] * (nh - len(waits))
                    for n, (which, val) in enumerate(waits):
                        hold(which, val, at + n)
                    for j in range(GT):
                        gp.indirect_dma_start(G[:, q, j, 0:wd], None, tab[k][:, :],
                                              bass.IndirectOffsetOnAxis(ap=jst[:, q, j:j + 1], axis=0)).then_inc(S[f"{x}g{q}"], 16)
                pairs(gp, npairs, body)
                held[0] += 2 * npairs * nh

            gather("a", PAIRS0, 0, 0, D, lambda i, q: [(S["au"], (i * 2 + q - 1) * 4), (S[f"ast{q}"], i * 16)])
            for r in range(3):
                gather("c", PAIRS, r * PAIRS, 1 + r, D, lambda i, q: [(S["cmm"], (r * PAIRS + i) * 2 + q - 1)])
            gather("d", PAIRS, 0, 4, D + H3, lambda i, q: [(S["db"], (i * 2 + q - 1) * GT), (S[f"dst{q}"], i * 16)])

        @block.scalar
        def _(act):
            A = nc.scalar
            act.wait_ge(S["wtp"], 1)
            A.copy(WT[0:D, :, :], pt[0:D, 0:5 * D].rearrange("p (k d) -> p k d", d=D)).then_inc(S["wtc"], 1)
            for k in (2, 4):
                A.copy(WT[D:2 * D, k, :], pt[D:2 * D, k * D:(k + 1) * D]).then_inc(S["wtc"], 1)
            ntc, nln = [0], [0]

            def transposed(K, dst=None):
                for b in range(-(-NC // 4)):
                    m = min(4, NC - 4 * b) * P
                    act.wait_ge(S["tp"], ntc[0] + 1)
                    bank = (ntc[0] % 2) * 512
                    A.copy((T if dst is None else dst)[0:K, b * 512:b * 512 + m], pt[0:K, bank:bank + m]).then_inc(S["tc"], 1)
                    ntc[0] += 1

            def sqrt_():
                nln[0] += 1
                act.wait_ge(S["lnv"], nln[0])
                A.activation(st[:, 2, :], st[:, 1, :], ACT.Sqrt).then_inc(S["lns"], 1)

            def ff_up(n0, func, K, b1):
                for g in range(8):
                    act.wait_ge(S["up"], n0 + g + 1)
                    A.activation(T2[0:K, g * 400:(g + 1) * 400], (pu, accw)[g % 2][0:K, 0:400], func, bias=b1[:]).then_inc(S["upc"], 1)
            sqrt_()
            transposed(D)
            act.wait_ge(S["rows"], 2)

            def stage(i, q, first):
                c = bass.ds(i * 16 + q * 8, GT)
                if not first:
                    act.wait_ge(S[f"scat{q}"], i * 16 * GT)
                nc.scalar.copy(recst[:, q, :, D:D + 1], idf[1][:, c].unsqueeze(2)).then_inc(S["recst"], 1)
                nc.scalar.copy(recst[:, q, :, D + 1:D + 2], lof[0][:, c].unsqueeze(2)).then_inc(S["recst"], 1)
                nc.scalar.copy(rowst[:, q, :], rowidx[0][:, c]).then_inc(S["recst"], 1)
            pairs(act, SG, stage)
            for q in range(2):
                act.wait_ge(S[f"scat{q}"], SG * 16 * GT)

            def stage_s(i, q, first):
                c = bass.ds(i * 16 + q * 8, GT)
                if not first:
                    act.wait_ge(S[f"sscat{q}"], i * 16 * GT)
                nc.scalar.copy(sst[:, q, :, 0:1], idf[0][:, c].unsqueeze(2)).then_inc(S["sst"], 1)
                nc.scalar.copy(sst[:, q, :, 1:2], lof[1][:, c].unsqueeze(2)).then_inc(S["sst"], 1)
                nc.scalar.copy(rowst[:, q, :], rowidx[1][:, c]).then_inc(S["sst"], 1)
            pairs(act, SG, stage_s)
            A = nc.scalar

            def ohts(x, a, keep, penal):
                i, q, first = a
                g = 2 * i + q
                act.wait_ge(S[f"{x}tr"], g + 1)
                if not first:
                    for which, val in (keep(g) if keep else []) + (penal(g) if penal else []):
                        act.wait_ge(which, val)
                for h in range(2):
                    src = pt[:, h * 512:(h + 1) * 512].rearrange("p (t n) -> p t n", n=P)
                    if keep:
                        A.copy(ohT[:, q, 4 * h:4 * h + 4, :], src).then_inc(S[f"{x}oht"], 1)
                    if penal:
                        A.activation(pen[:, q, 4 * h:4 * h + 4, :], src, ACT.Copy, bias=-BIG, scale=BIG).then_inc(S[f"{x}pen"], 1)

            def step_a(a, b):
                if a:
                    ohts("a", a, lambda g: [(S["apu"], g - 1)], lambda g: [(S["amx"], g * 41 - 41)])
                if b:
                    i, q, first = b
                    act.wait_ge(S["au"], (2 * i + q) * 4 + 4)
                    A.copy(score[:, bass.ds((i * 16 + q * 8) * H0, GT * H0)],
                           scst[:, q].rearrange("p t h -> p (t h)")).then_inc(S["ascc"], 1)
            pipe(act, PAIRS0, step_a)

            def step_b(a, b):
                if a:
                    ohts("b", a, lambda g: [(S["bpm"], g - 1)], None)
                if b:
                    i, q, first = b
                    g = 2 * i + q
                    act.wait_ge(S["bd"], 2 * g + 2)
                    if not first:
                        act.wait_ge(S["bagg"], g - 1)
                    A.activation(w[:, q, :, 0:H0], scst[:, q], ACT.Exp).then_inc(S["bw"], 1)
            pipe(act, PAIRS0, step_b)
            transposed(2 * D)
            ff_up(0, ACT.Gelu, D, b1c0)
            sqrt_()
            transposed(2 * D)
            transposed(D, NRT)
            transposed(2 * D)
            sqrt_()
            transposed(2 * D)
            sqrt_()
            transposed(D)

            def step_d(a, b):
                if a:
                    ohts("d", a, None, lambda g: [(S["dmx"], g * 73 - 73)])
            pipe(act, PAIRS, step_d)
            act.wait_ge(S["bm"], 1)
            A.activation(es[:], es[:], ACT.Exp).then_inc(S["es"], 1)

            def step_e(a, b):
                if a:
                    ohts("e", a, lambda g: [(S["epm"], g - 1)], None)
                if b:
                    i, q, first = b
                    g = 2 * i + q
                    act.wait_ge(S["ed"], 4 * g + 4)
                    if not first:
                        act.wait_ge(S["emm"], 8 * g - 8)
                    A.activation(w[:, q], w8[:, q], ACT.Exp).then_inc(S["ew"], 1)
            pipe(act, PAIRS, step_e)
            for c in range(NC):
                act.wait_ge(S["ftp"], c + 1)
                if c >= 2:
                    act.wait_ge(S["fmm"], c - 1)
                A.copy(TT[c % 2], pt[:, (c % 2) * 512:(c % 2) * 512 + 512]).then_inc(S["ftc"], 1)
            sqrt_()
            transposed(D)
            ff_up(8, ACT.Relu, 2 * D, b1c3)
            sqrt_()

        @block.vector
        def _(v):
            V = nc.vector
            n = [0]

            def link(ins):
                n[0] += 1
                ins.then_inc(S["v"], 1)
                v.wait_ge(S["v"], n[0])

            v.wait_ge(S["iota"], 1)
            link(V.tensor_copy(iota[:], iota_i[:]))
            v.wait_ge(S["const"], 5)
            link(V.memset(sone, 1.0))
            v.wait_ge(S["keys"], 32)
            for l in range(2):
                link(V.tensor_copy(idf[l], key_i[l]))
                link(V.tensor_scalar(low_i, key_i[l], 127, None, ALU.bitwise_and))
                link(V.tensor_copy(lof[l], low_i))
                link(V.tensor_scalar(key_i[l], key_i[l], 7, None, ALU.logical_shift_right))
                link(V.tensor_copy(bkf[l], key_i[l]))
                link(V.memset(slot[l], 0.0))
            base = n[0]
            with v.Fori(0, NC) as b:
                bs = iota[0:EP, bass.ds(b, 1)]
                for l in range(2):
                    V.tensor_scalar(mask[l], bkf[l], bs, 0.0, ALU.is_equal, ALU.add,
                                    accum_out=cnt[l][:, bass.ds(b, 1)]).then_inc(S["cnt"], 1)
                v.wait_ge(S["cnt"], b * 2 + 2)
            v.wait_ge(S["tot"], 1)
            link(V.tensor_scalar(tcol[:], pu[0:NC, 0:2], float(P - 1), None, ALU.add))
            link(V.tensor_copy(tcol_i[:], tcol[:]))
            link(V.tensor_scalar(tcol_i[:], tcol_i[:], 7, None, ALU.logical_shift_right))
            link(V.tensor_copy(tcol[:], tcol_i[:]))
            for l in range(2):
                last = V.tensor_scalar(t128[:, l, :], ones[0:NC, 0:EP], tcol[:, l:l + 1], float(P), ALU.mult, ALU.mult)
                last.then_inc(S["tcol"], 1)
            v.wait_ge(S["end"], 1)
            link(V.tensor_copy(endc[:], pu[0:NC, 8:10]))
            for l in range(2):
                link(V.tensor_copy(off[l][:], pu[0:EP, 64 + 32 * l:64 + 32 * l + NC]))
            for l in range(2):
                V.tensor_scalar(gmat[:, l, :], iota[0:NC, :], endc[:, l:l + 1], None, ALU.is_ge).then_inc(S["gm"], 1)
            v.wait_ge(S["ct"], 1)
            V.tensor_scalar(ctab[:, :].rearrange("o (a b) -> o a b", a=4),
                                 acc[0:1, :].rearrange("o (a b) -> o a b", a=4)[:, :, 0:NT // 2],
                                 float(NC - 1), None, ALU.min).then_inc(S["ctab"], 1)
            with v.Fori(0, NC) as b:
                bs = iota[0:EP, bass.ds(b, 1)]
                for l in range(2):
                    V.tensor_scalar(mask[l], bkf[l], bs, None, ALU.is_equal).then_inc(S["vl"], 1)
                v.wait_ge(S["vl"], b * 7 + 2)
                for l in range(2):
                    V.tensor_tensor_scan(pos[l], sone, mask[l], off[l][:, bass.ds(b, 1)], ALU.mult, ALU.add).then_inc(S["vl"], 1)
                v.wait_ge(S["vl"], b * 7 + 4)
                V.memset(vdum[:], 0.0).then_inc(S["vl"], 1)
                for l in range(2):
                    V.copy_predicated(slot[l], mask[l].bitcast(U), pos[l]).then_inc(S["vl"], 1)
                v.wait_ge(S["vl"], b * 7 + 7)
            for l in range(2):
                link(V.tensor_scalar(key_i[0], slot[l], -1.0, None, ALU.add))
                link(V.tensor_scalar(key_i[1], key_i[0], 7, None, ALU.logical_shift_right))
                link(V.tensor_scalar(key_i[0], key_i[0], 127, None, ALU.bitwise_and))
                link(V.tensor_copy(pos[0], key_i[0]))
                link(V.tensor_copy(pos[1], key_i[1]))
                link(V.scalar_tensor_tensor(slot[l], pos[0], float(NT), pos[1], ALU.mult, ALU.add))
                V.tensor_copy(rowidx[l][:], slot[l]).then_inc(S["rows"], 1)

            nln = [0]

            def norm(dst, src, g=None, b=None):
                link(V.tensor_reduce(st[:, 0, :], src, AX, ALU.add))
                link(V.tensor_scalar(st[:, 0, :], st[:, 0, :], 1.0 / D, None, ALU.mult))
                link(V.tensor_tensor(XC, src, st[:, 0, :].unsqueeze(2).to_broadcast([P, NC, D]), ALU.subtract))
                link(V.tensor_tensor(SQ, XC, XC, ALU.mult))
                link(V.tensor_reduce(st[:, 1, :], SQ, AX, ALU.add))
                V.tensor_scalar(st[:, 1, :], st[:, 1, :], 1.0 / D, EPS, ALU.mult, ALU.add).then_inc(S["lnv"], 1)
                nln[0] += 1
                v.wait_ge(S["lns"], nln[0])
                link(V.reciprocal(st[:, 3, :], st[:, 2, :]))
                link(V.tensor_tensor(XC, XC, st[:, 3, :].unsqueeze(2).to_broadcast([P, NC, D]), ALU.mult))
                if g is None:
                    link(V.tensor_scalar(dst, XC, 0.0, None, ALU.max))
                else:
                    link(V.tensor_tensor(XC, XC, lnb[:, g, :].unsqueeze(1).to_broadcast([P, NC, D]), ALU.mult))
                    link(V.tensor_tensor(dst, XC, lnb[:, b, :].unsqueeze(1).to_broadcast([P, NC, D]), ALU.add))

            acc_n = acc[:, 0:NC * D].rearrange("p (c d) -> p c d", d=D)
            v.wait_ge(S["wts"], 16 * 31)
            for k in range(2):
                link(V.tensor_tensor(attsd[:, k, :], attsd[:, k, :], watt, ALU.mult))
                link(V.tensor_reduce(Asd[:, k, :], attsd[:, k, :].rearrange("p (h c) -> p h c", c=D), AX, ALU.add))
            link(V.memset(M[:], -BIG))
            norm(Hn[:], X[:])
            V.memset(vdum[:], 0.0).then_inc(S["ev"], 1)
            v.wait_ge(S["lin"], 1)
            V.tensor_copy(GL, acc_n).then_inc(S["ev"], 1)
            v.wait_ge(S["lin"], 2)
            V.tensor_copy(GR, acc_n).then_inc(S["tsrc"], 1)

            def rec_tiles(i, q, first):
                v.wait_ge(S[f"rld{q}"], (i + 1) * 16)
                c = bass.ds(i * 16 + q * 8, GT)
                V.tensor_copy(jidx[:, c].unsqueeze(2), G[:, q, :, D:D + 1]).then_inc(S["rcp"], 1)
                V.tensor_copy(iloc[:, c].unsqueeze(2), G[:, q, :, D + 1:REC]).then_inc(S["rcp"], 1)
                if not first:
                    v.wait_ge(S["rmm"], i * 2 + q - 1)
                V.tensor_tensor(oh[:, q], iota1.unsqueeze(1).to_broadcast([P, GT, P]),
                                G[:, q, :, D + 1:REC].to_broadcast([P, GT, P]), ALU.is_equal).then_inc(S["roh"], 1)
            pairs(v, PAIRS, rec_tiles)
            v.wait_ge(S["rmm"], 2 * PAIRS)
            link(V.tensor_copy(nbr_r[:], acc_n))
            link(V.tensor_copy(deg[:], accw[:, 0:NC]))
            link(V.tensor_scalar(invdeg[:], deg[:], 1.0, None, ALU.max))
            link(V.reciprocal(invdeg[:], invdeg[:]))
            link(V.tensor_scalar(hasin[:], deg[:], 0.0, None, ALU.is_gt))
            deg_b = invdeg[:].unsqueeze(2).to_broadcast([P, NC, D])
            V.tensor_tensor(nbr_r[:], nbr_r[:], deg_b, ALU.mult).then_inc(S["ev"], 1)
            v.wait_ge(S["slist"], 16)
            link(V.tensor_copy(iloc[:, NT:2 * NT], slraw[:, :, 1]))
            link(V.tensor_copy(jidx[:, NT:2 * NT], slraw[:, :, 0]))
            V.memset(vdum[:], 0.0).then_inc(S["jdone"], 1)

            def chunks(c0):
                return nc.values_load_multi_w_load_instructions(ctab[0:1, bass.ds(c0, GT)], engines=[mybir.EngineType.DVE],
                                                                min_val=0, max_val=NC - 1)[1]

            def onehots(x, a, freed):
                i, q, first = a
                if freed(i, q) and not first:
                    v.wait_ge(*freed(i, q))
                V.tensor_tensor(oh[:, q], iota1.unsqueeze(1).to_broadcast([P, GT, P]),
                                iloc[:, bass.ds(i * 16 + q * 8, GT)].unsqueeze(2).to_broadcast([P, GT, P]),
                                ALU.is_equal).then_inc(S[f"{x}oh"], 1)

            def maxima(x, b, H, banks):
                i, q, first = b
                g = 2 * i + q
                per = GT * (H + 1) + 1
                chunk = chunks(i * 16 + q * 8)
                if not (first and q == 0):
                    v.wait_ge(S[f"{x}mx"], g * per)
                v.wait_ge(S[f"{x}pen"], 2 * g + 2)
                v.wait_ge(S[f"{x}b"], g * GT + 1)
                V.memset(vdum[:], 0.0).then_inc(S[f"{x}mx"], 1)
                for k in range(GT):
                    for h in range(H):
                        at = (k % banks) * H * P + h * P
                        V.tensor_tensor_reduce(out=junk[:, h, :], in0=pen[:, q, k, :], in1=acc[:, at:at + P], scale=1.0, scalar=-BIG,
                                               op0=ALU.add, op1=ALU.max, accum_out=mx[:, k, h:h + 1]).then_inc(S[f"{x}mx"], 1)
                    if k < GT - 1:
                        v.wait_ge(S[f"{x}b"], g * GT + k + 2)
                    v.wait_ge(S[f"{x}mx"], g * per + 1 + k * (H + 1) + H)
                    m = M[:, bass.ds(chunk[k] * H, H)]
                    V.tensor_tensor(m, m, mx[:, k, 0:H], ALU.max).then_inc(S[f"{x}mx"], 1)

            def step_a(a, b):
                if a:
                    onehots("a", a, lambda i, q: (S["atr"], 2 * i + q - 1))
                if b:
                    maxima("a", b, H0, 4)
                if a:
                    i, q, first = a
                    g = 2 * i + q
                    v.wait_ge(S[f"ag{q}"], (i + 1) * 16 * GT)
                    v.wait_ge(S["apu"], g + 1)
                    if not (first and q == 0):
                        v.wait_ge(S["au"], 4 * g)
                    V.tensor_tensor(work[:], pu[:, :].rearrange("p (t d) -> p t d", d=D), G[:, q, :, 0:D], ALU.add).then_inc(S["au"], 1)
                    v.wait_ge(S["au"], 4 * g + 1)
                    V.scalar_tensor_tensor(work[:], work[:], 0.2, work[:], ALU.mult, ALU.max).then_inc(S["au"], 1)
                    v.wait_ge(S["au"], 4 * g + 2)
                    V.tensor_tensor(work[:], work[:], attb[:].unsqueeze(1).to_broadcast([P, GT, D]), ALU.mult).then_inc(S["au"], 1)
                    v.wait_ge(S["au"], 4 * g + 3)
                    if not first:
                        v.wait_ge(S["ab"], 8 * g - 8)
                        v.wait_ge(S["ascc"], g - 1)
                    V.tensor_reduce(scst[:, q].rearrange("p t h -> p (t h)"), work[:].rearrange("p t (h d) -> p (t h) d", h=H0),
                                    AX, ALU.add).then_inc(S["au"], 1)
            pipe(v, PAIRS0, step_a)
            v.wait_ge(S["amx"], 2 * PAIRS0 * 41)
            v.wait_ge(S["ascc"], 2 * PAIRS0)
            V.memset(vdum[:], 0.0).then_inc(S["m0"], 1)

            def step_b(a, b):
                if a:
                    onehots("b", a, lambda i, q: (S["bagg"], 2 * i + q - 1))
                if b:
                    i, q, first = b
                    g = 2 * i + q
                    v.wait_ge(S["bw"], g + 1)
                    v.wait_ge(S[f"bld{q}"], (i + 1) * 16)
                    if not first:
                        v.wait_ge(S["bagg"], g - 1)
                    V.tensor_tensor(V0[:, q].rearrange("p t (h d) -> p t h d", h=H0),
                                    G[:, q, :, 0:D].rearrange("p t (h d) -> p t h d", h=H0),
                                    w[:, q, :, 0:H0].unsqueeze(3).to_broadcast([P, GT, H0, D // H0]), ALU.mult).then_inc(S["bv"], 1)
                if a:
                    i, q, first = a
                    g = 2 * i + q
                    v.wait_ge(S["bpm"], g + 1)
                    if not first:
                        v.wait_ge(S["bw"], g - 1)
                    sc = scst[:, q].rearrange("p t h -> p (t h)")
                    V.tensor_tensor(sc, score[:, bass.ds((i * 16 + q * 8) * H0, GT * H0)], pu[:, 0:GT * H0], ALU.subtract).then_inc(S["bd"], 1)
                    v.wait_ge(S["bd"], 2 * g + 1)
                    V.tensor_scalar(sc, sc, 0.0, None, ALU.min).then_inc(S["bd"], 1)
            pipe(v, PAIRS0, step_b)
            v.wait_ge(S["bagg"], 2 * PAIRS0)
            den = es[:, :, 0:H0]
            link(V.tensor_scalar(den, accw[:, 0:NC * H0].rearrange("p (c h) -> p c h", h=H0), 1e-16, None, ALU.add))
            link(V.reciprocal(den, den))
            for c in range(NC):
                last = V.tensor_tensor(CAT[:, c, 0:D].rearrange("p (h d) -> p h d", h=H0),
                                       acc[:, c * D:(c + 1) * D].rearrange("p (h d) -> p h d", h=H0),
                                       es[:, c, 0:H0].unsqueeze(2).to_broadcast([P, H0, D // H0]), ALU.mult)
            last.then_inc(S["v"], 1)
            n[0] += 1
            V.tensor_copy(CAT[:, :, D:2 * D], Hn[:]).then_inc(S["ev"], 1)
            v.wait_ge(S["lin"], 3)
            link(V.tensor_tensor(X[:], X[:], acc_n, ALU.add))
            norm(Hn[:], X[:])
            V.memset(vdum[:], 0.0).then_inc(S["tsrc"], 1)

            for r in range(3):
                def gathered(i, q, first):
                    R = r * PAIRS + i
                    if not first or r:
                        v.wait_ge(S["cmm"], 2 * R + q - 1)
                    onehots("c", (i, q, first), lambda i, q: None)
                pairs(v, PAIRS, gathered)
                v.wait_ge(S["cmm"], (r + 1) * 2 * PAIRS)
                link(V.tensor_copy(CAT[:, :, 0:D], Hn[:]))
                link(V.tensor_tensor(CAT[:, :, D:2 * D], acc_n, deg_b, ALU.mult))
                if r == 2:
                    link(V.tensor_tensor(CAT[:, :, D:2 * D], CAT[:, :, D:2 * D], Hn[:], ALU.subtract))
                V.memset(vdum[:], 0.0).then_inc(S["ev"], 1)
                v.wait_ge(S["lin"], 4 + r)
                if r == 0:
                    V.tensor_scalar(Hn[:], acc_n, 0.0, None, ALU.max).then_inc(S["tsrc"], 1)
                    continue
                if r == 1:
                    link(V.tensor_scalar(XC, acc_n, 0.0, None, ALU.max))
                else:
                    link(V.tensor_tensor(XC, acc_n, hasin[:].unsqueeze(2).to_broadcast([P, NC, D]), ALU.mult))
                link(V.tensor_tensor(X[:], X[:], XC, ALU.add))
                norm(Hn[:], X[:])
                if r == 1:
                    V.memset(vdum[:], 0.0).then_inc(S["tsrc"], 1)
            V.memset(vdum[:], 0.0).then_inc(S["ev"], 1)

            v.wait_ge(S["lin"], 7)
            link(V.tensor_copy(AS[:], acc[:, 0:NC * 2 * H3].rearrange("p (c h) -> p c h", h=2 * H3)))
            link(V.tensor_copy(TB3[:, :, 0:D], Hn[:]))
            link(V.memset(M[:], -BIG))
            V.tensor_copy(TB3[:, :, D:D + H3], AS[:, :, 0:H3]).then_inc(S["tsrc"], 1)

            def step_d(a, b):
                if a:
                    onehots("d", a, lambda i, q: (S["dtr"], 2 * i + q - 1))
                if b:
                    maxima("d", b, H3, 2)
            pipe(v, PAIRS, step_d)
            v.wait_ge(S["dmx"], 2 * PAIRS * 73)
            Mv = M[:].rearrange("p (c h) -> p c h", h=H3)
            bm = BM[:, :, H3:2 * H3]
            link(V.tensor_copy(BM[:, :, 0:H3], AS[:, :, H3:2 * H3]))
            link(V.tensor_tensor(bm, Mv, AS[:, :, 0:H3], ALU.max))
            link(V.tensor_tensor(bm, bm, BM[:, :, 0:H3], ALU.add))
            link(V.scalar_tensor_tensor(bm, bm, 0.2, bm, ALU.mult, ALU.max))
            link(V.tensor_tensor(es[:], AS[:, :, 0:H3], AS[:, :, H3:2 * H3], ALU.add))
            link(V.scalar_tensor_tensor(es[:], es[:], 0.2, es[:], ALU.mult, ALU.max))
            link(V.tensor_tensor(es[:], es[:], bm, ALU.subtract))
            v.wait_ge(S["tb"], 16 * 5)
            link(V.memset(acc3, 0.0))
            V.memset(vdum[:], 0.0).then_inc(S["bm"], 1)

            def step_e(a, b):
                if a:
                    onehots("e", a, lambda i, q: (S["emm"], (2 * i + q - 1) * GT))
                if b:
                    i, q, first = b
                    g = 2 * i + q
                    chunk = chunks(i * 16 + q * 8)
                    v.wait_ge(S["ew"], g + 1)
                    v.wait_ge(S[f"eld{q}"], (i + 1) * 16)

                    def add(k):
                        v.wait_ge(S["emm"], g * GT + k + 1)
                        if not (first and q == 0 and k == 0):
                            v.wait_ge(S["ead"], g * GT + k)
                        o = acc3[:, bass.ds(chunk[k] * (H3 * D), H3 * D)]
                        V.tensor_tensor(o, o, acc[:, (k % 4) * 512:(k % 4) * 512 + 512], ALU.add).then_inc(S["ead"], 1)
                    for k in range(GT):
                        if not (first and q == 0 and k < 2):
                            v.wait_ge(S["emm"], g * GT + k - 1)
                        V.tensor_tensor(V0[:, k % 2], G[:, q, k, 0:D].unsqueeze(1).to_broadcast([P, H3, D]),
                                        w[:, q, k, :].unsqueeze(2).to_broadcast([P, H3, D]), ALU.mult).then_inc(S["ev3"], 1)
                        if k:
                            add(k - 1)
                    add(GT - 1)
                if a:
                    i, q, first = a
                    g = 2 * i + q
                    v.wait_ge(S["epm"], g + 1)
                    v.wait_ge(S[f"eld{q}"], (i + 1) * 16)
                    if not first:
                        v.wait_ge(S["ew"], g - 1)
                    pm = pu[:, 0:GT * 2 * H3].rearrange("p (t h) -> p t h", h=2 * H3)
                    V.tensor_tensor(w8[:, q], G[:, q, :, D:D + H3], pm[:, :, 0:H3], ALU.add).then_inc(S["ed"], 1)
                    v.wait_ge(S["ed"], 4 * g + 1)
                    V.scalar_tensor_tensor(w8[:, q], w8[:, q], 0.2, w8[:, q], ALU.mult, ALU.max).then_inc(S["ed"], 1)
                    v.wait_ge(S["ed"], 4 * g + 2)
                    V.tensor_tensor(w8[:, q], w8[:, q], pm[:, :, H3:2 * H3], ALU.subtract).then_inc(S["ed"], 1)
                    v.wait_ge(S["ed"], 4 * g + 3)
                    V.tensor_scalar(w8[:, q], w8[:, q], 0.0, None, ALU.min).then_inc(S["ed"], 1)
            pipe(v, PAIRS, step_e)
            v.wait_ge(S["ead"], NT)
            v.wait_ge(S["es"], 1)
            link(V.tensor_tensor(rden[:], accw[:, 0:NC * H3].rearrange("p (c h) -> p c h", h=H3), es[:], ALU.add))
            link(V.tensor_scalar(rden[:], rden[:], 1e-16, None, ALU.add))
            link(V.reciprocal(rden[:], rden[:]))
            link(V.tensor_scalar(rden[:], rden[:], 1.0 / H3, None, ALU.mult))
            for c in range(NC):
                o = acc3[:, c * H3 * D:(c + 1) * H3 * D].rearrange("p (h d) -> p h d", d=D)
                link(V.tensor_tensor(work[:], Hn[:, c, :].unsqueeze(1).to_broadcast([P, H3, D]),
                                     es[:, c, :].unsqueeze(2).to_broadcast([P, H3, D]), ALU.mult))
                link(V.tensor_tensor(o, o, work[:], ALU.add))
                V.tensor_tensor(o, o, rden[:, c, :].unsqueeze(2).to_broadcast([P, H3, D]), ALU.mult).then_inc(S["fac"], 1)
            v.wait_ge(S["fmm"], NC)
            link(V.tensor_tensor(Hn[:], Hn[:], acc_n, ALU.add))
            link(V.tensor_tensor(Hn[:], Hn[:], lnb[:, 0, :].unsqueeze(1).to_broadcast([P, NC, D]), ALU.add))
            norm(Hn[:], Hn[:], 1, 2)
            V.memset(vdum[:], 0.0).then_inc(S["ev"], 1)
            v.wait_ge(S["lin"], 8)
            link(V.tensor_tensor(Hn[:], Hn[:], acc_n, ALU.add))
            norm(Hn[:], Hn[:], 3, 4)
            V.tensor_tensor(OUTN, X[:], Hn[:], ALU.add).then_inc(S["xp"], 1)

        @block.tensor
        def _(pe):
            pe.wait_ge(S["cnt"], 2 * NC)
            pe.wait_ge(S["const"], 5)
            for l in range(2):
                last = nc.tensor.matmul(pu[0:NC, l:l + 1], cnt[l][:], ones[0:EP, 0:1], start=True, stop=True)
            last.then_inc(S["tot"], 1)
            pe.wait_ge(S["tcol"], 2)
            nc.tensor.matmul(pu[0:NC, 8:10], triinc[0:NC, 0:NC], tcol[:], start=True, stop=True)
            for l in range(2):
                o = pu[0:EP, 64 + 32 * l:64 + 32 * l + NC]
                nc.tensor.matmul(o, tri[0:EP, 0:EP], cnt[l][:], start=True, stop=False)
                last = nc.tensor.matmul(o, t128[:, l, :], tri[0:NC, 0:NC], start=False, stop=True)
            last.then_inc(S["end"], 1)
            pe.wait_ge(S["gm"], 2)
            for l in range(2):
                for h in range(2):
                    last = nc.tensor.matmul(acc[0:1, (2 * l + h) * 512:(2 * l + h) * 512 + NT // 2], ones[0:NC, 0:1],
                                            gmat[:, l, h * (NT // 2):(h + 1) * (NT // 2)], start=True, stop=True)
            last.then_inc(S["ct"], 1)

            pe.wait_ge(S["wts"], 16 * 31)
            at = 0
            for k, wd in enumerate((D, D, 2 * D, D, 2 * D)):
                last = nc.tensor.transpose(pt[0:wd, k * D:(k + 1) * D], wraw[:, at:at + wd], ident[0:D, 0:D])
                at += wd
            last.then_inc(S["wtp"], 1)
            pe.wait_ge(S["wtc"], 3)
            ntp, nln, nup = [0], [0], [0]

            def transposes(src, K):
                for b in range(-(-NC // 4)):
                    if ntp[0] >= 2:
                        pe.wait_ge(S["tc"], ntp[0] - 1)
                    bank = (ntp[0] % 2) * 512
                    for j in range(min(4, NC - 4 * b)):
                        last = nc.tensor.transpose(pt[0:K, bank + j * P:bank + (j + 1) * P], src[:, 4 * b + j, :], ident[:])
                    last.then_inc(S["tp"], 1)
                    ntp[0] += 1

            def product(parts, width, bk=None):
                pe.wait_ge(S["tc"], ntp[0])
                for c in range(NC):
                    o = acc[:, c * width:(c + 1) * width]
                    for n, (TL, K, R) in enumerate(parts):
                        last = nc.tensor.matmul(o, TL[0:K, c * P:(c + 1) * P], R, start=n == 0, stop=n == len(parts) - 1 and bk is None)
                    if bk is not None:
                        last = nc.tensor.matmul(o, ones[0:1, :], bias[:, bk, :], start=False, stop=True)
                last.then_inc(S["lin"], 1)

            def hidden(W, K, n0):
                pe.wait_ge(S["tc"], ntp[0])
                for g in range(8):
                    if g >= 2:
                        pe.wait_ge(S["upc"], n0 + g - 1)
                    nc.tensor.matmul((pu, accw)[g % 2][0:W.shape[1], 0:400], W, T[0:K, g * 400:(g + 1) * 400],
                                     start=True, stop=True).then_inc(S["up"], 1)
                pe.wait_ge(S["upc"], n0 + 8)

            def zero_acc():
                for k in range(4):
                    nc.tensor.matmul(acc[:, k * 512:(k + 1) * 512], zrow[0:1, 0:P], zrow[0:1, :], start=True, stop=True,
                                     skip_group_check=True)
                zero_accw()

            def zero_accw():
                nc.tensor.matmul(accw[:, :], zrow[0:1, 0:P], zrow[0:1, :], start=True, stop=True, skip_group_check=True)

            pe.wait_ge(S["ctab"], 1)
            pe.wait_ge(S["ev"], 1)
            transposes(Hn[:], D)
            product([(T, D, WT[0:D, 0, :])], D)
            pe.wait_ge(S["ev"], 2)
            product([(T, D, WT[0:D, 1, :])], D)
            pe.wait_ge(S["tsrc"], 1)

            def load_chunks(c0):
                _, vals = nc.values_load_multi_w_load_instructions(ctab[0:1, bass.ds(c0, GT)], engines=[mybir.EngineType.PE],
                                                                   min_val=0, max_val=NC - 1)
                return vals

            zero_acc()

            def rec_mm(i, q, first):
                chunk = load_chunks(i * 16 + q * 8)
                pe.wait_ge(S["roh"], 2 * i + q + 1)
                for k in range(GT):
                    nc.tensor.matmul(acc[:, bass.ds(chunk[k] * D, D)], oh[:, q, k, :], G[:, q, k, 0:D],
                                     start=False, stop=True, skip_group_check=True)
                    last = nc.tensor.matmul(accw[:, bass.ds(chunk[k], 1)], oh[:, q, k, :], ones[:, 0:1],
                                            start=False, stop=True, skip_group_check=True)
                last.then_inc(S["rmm"], 1)
            pairs(pe, PAIRS, rec_mm)

            def T_onehots(x, a, freed):
                i, q, first = a
                g = 2 * i + q
                pe.wait_ge(S[f"{x}oh"], g + 1)
                if not (first and q == 0):
                    for which in freed:
                        pe.wait_ge(which, 2 * g)
                for k in range(GT):
                    last = nc.tensor.transpose(pt[:, k * P:(k + 1) * P], oh[:, q, k, :], ident[:])
                last.then_inc(S[f"{x}tr"], 1)

            def own_rows(a, x, table, width, done, freed):
                i, q, first = a
                g = 2 * i + q
                chunk = load_chunks(i * 16 + q * 8)
                pe.wait_ge(S[f"{x}oht"], 2 * g + 2)
                if not (first and q == 0):
                    pe.wait_ge(*freed(g))
                for k in range(GT):
                    last = nc.tensor.matmul(pu[:, k * width:(k + 1) * width], ohT[:, q, k, :],
                                            table[:, bass.ds(chunk[k] * width, width)], start=True, stop=True)
                last.then_inc(S[done], 1)

            pe.wait_ge(S["ev"], 3)
            pe.wait_ge(S["jdone"], 1)
            GLf = area(0)

            def step_a(a, b):
                if a:
                    T_onehots("a", a, (S["aoht"], S["apen"]))

                def spread(ks):
                    i, q, first = b
                    g = 2 * i + q
                    pe.wait_ge(S["au"], 4 * g + 4)
                    for k in ks:
                        if not (first and q == 0 and k < 4):
                            pe.wait_ge(S["amx"], g * 41 + 5 * k - (15 if k >= 4 else 16))
                        for h in range(H0):
                            last = nc.tensor.matmul(acc[:, (k % 4) * 512 + h * P:(k % 4) * 512 + (h + 1) * P],
                                                    scst[:, q, k, h:h + 1].to_broadcast([P, P]), ident[:], start=True, stop=True)
                        last.then_inc(S["ab"], 1)
                if b:
                    spread(range(0, 4))
                if a:
                    own_rows(a, "a", GLf, D, "apu", lambda g: (S["au"], 4 * g - 3))
                if b:
                    spread(range(4, 8))
            pipe(pe, PAIRS0, step_a)

            pe.wait_ge(S["m0"], 1)
            zero_acc()

            def step_b(a, b):
                if a:
                    T_onehots("b", a, (S["boht"],))
                if b:
                    i, q, first = b
                    g = 2 * i + q
                    chunk = load_chunks(i * 16 + q * 8)
                    pe.wait_ge(S["bv"], g + 1)
                    for k in range(GT):
                        nc.tensor.matmul(acc[:, bass.ds(chunk[k] * D, D)], oh[:, q, k, :], V0[:, q, k, :],
                                         start=False, stop=True, skip_group_check=True)
                        last = nc.tensor.matmul(accw[:, bass.ds(chunk[k] * H0, H0)], oh[:, q, k, :], w[:, q, k, 0:H0],
                                                start=False, stop=True, skip_group_check=True)
                    last.then_inc(S["bagg"], 1)
                if a:
                    own_rows(a, "b", M[:], H0, "bpm", lambda g: (S["bd"], 2 * g - 1))
            pipe(pe, PAIRS0, step_b)
            pe.wait_ge(S["ev"], 4)
            transposes(CAT, 2 * D)
            hidden(WT[:, 2, :], 2 * D, 0)
            product([(T2, D, WT[0:D, 3, :])], D, 0)

            for r in range(3):
                pe.wait_ge(S["tsrc"], 2 + r)
                zero_acc()

                def mean_mm(i, q, first):
                    chunk = load_chunks(i * 16 + q * 8)
                    R = r * PAIRS + i
                    pe.wait_ge(S["coh"], 2 * R + q + 1)
                    pe.wait_ge(S[f"cg{q}"], (R + 1) * 16 * GT)
                    for k in range(GT):
                        last = nc.tensor.matmul(acc[:, bass.ds(chunk[k] * D, D)], oh[:, q, k, :], G[:, q, k, 0:D],
                                                start=False, stop=True, skip_group_check=True)
                    last.then_inc(S["cmm"], 1)
                pairs(pe, PAIRS, mean_mm)
                pe.wait_ge(S["ev"], 5 + r)
                transposes(CAT, 2 * D)
                if r == 0:
                    transposes(nbr_r[:], D)
                if r < 2:
                    product([(T, 2 * D, W1a[:, r, :]), (NRT, D, W1b[:, r, :])], D, 1 + r)
                else:
                    product([(T, 2 * D, WT[:, 4, :])], D, 3)

            pe.wait_ge(S["ev"], 8)
            transposes(Hn[:], D)
            product([(T, D, Asd[:].rearrange("p s h -> p (s h)"))], 2 * H3)
            pe.wait_ge(S["tsrc"], 5)

            def step_d(a, b):
                if a:
                    T_onehots("d", a, (S["dpen"],))
                if b:
                    i, q, first = b
                    g = 2 * i + q
                    pe.wait_ge(S[f"dg{q}"], (i + 1) * 16 * GT)
                    for k in range(GT):
                        if not (first and q == 0 and k < 2):
                            pe.wait_ge(S["dmx"], g * 73 + 9 * k - (9 if k >= 2 else 10))
                        for h in range(H3):
                            at = (k % 2) * 1024 + h * P
                            last = nc.tensor.matmul(acc[:, at:at + P], G[:, q, k, D + h:D + h + 1].to_broadcast([P, P]), ident[:],
                                                    start=True, stop=True)
                        last.then_inc(S["db"], 1)
            pipe(pe, PAIRS, step_d)

            pe.wait_ge(S["bm"], 1)
            zero_accw()

            def step_e(a, b):
                if a:
                    T_onehots("e", a, (S["eoht"],))
                if b:
                    i, q, first = b
                    g = 2 * i + q
                    chunk = load_chunks(i * 16 + q * 8)
                    for k in range(GT):
                        pe.wait_ge(S["ev3"], g * GT + k + 1)
                        if not (first and q == 0 and k < 4):
                            pe.wait_ge(S["ead"], g * GT + k - 3)
                        nc.tensor.matmul(acc[:, (k % 4) * 512:(k % 4) * 512 + 512], oh[:, q, k, :],
                                         V0[:, k % 2].rearrange("p h d -> p (h d)"), start=True, stop=True)
                        nc.tensor.matmul(accw[:, bass.ds(chunk[k] * H3, H3)], oh[:, q, k, :], w[:, q, k, :],
                                         start=False, stop=True, skip_group_check=True).then_inc(S["emm"], 1)
                if a:
                    own_rows(a, "e", BM[:].rearrange("p c h -> p (c h)"), 2 * H3, "epm", lambda g: (S["ed"], 4 * g - 1))
            pipe(pe, PAIRS, step_e)
            pe.wait_ge(S["ead"], NT)
            for c in range(NC + 1):
                if c < NC:
                    pe.wait_ge(S["fac"], c + 1)
                    if c >= 2:
                        pe.wait_ge(S["ftc"], c - 1)
                    for j in range(4):
                        last = nc.tensor.transpose(pt[:, (c % 2) * 512 + j * P:(c % 2) * 512 + (j + 1) * P],
                                                   acc3[:, c * 512 + j * P:c * 512 + (j + 1) * P], ident[:])
                    last.then_inc(S["ftp"], 1)
                if c:
                    pe.wait_ge(S["ftc"], c)
                    for j in range(4):
                        last = nc.tensor.matmul(acc[:, (c - 1) * D:c * D], TT[(c - 1) % 2][:, j * P:(j + 1) * P], Wp[:, j, :],
                                                start=j == 0, stop=j == 3)
                    last.then_inc(S["fmm"], 1)
            pe.wait_ge(S["ev"], 9)
            transposes(Hn[:], D)
            hidden(F1[:], D, 8)
            product([(T2, 2 * D, F2[:])], D, 4)


_INS = ['x', 'src', 'dst', 'edge_attr_64', 'L0_gnn_Wl', 'L0_gnn_Wr', 'L0_gnn_att', 'L0_gnn_W1', 'L0_gnn_b1', 'L0_gnn_W2', 'L0_gnn_b2',
        'L1_gnn_W1', 'L1_gnn_b1', 'L1_gnn_W2', 'L1_gnn_b2', 'L2_gnn_W', 'L2_gnn_b', 'L3_gnn_W_att', 'L3_gnn_att_src',
        'L3_gnn_att_dst', 'L3_gnn_bias_att', 'L3_gnn_W1', 'L3_gnn_b1', 'L3_gnn_W2', 'L3_gnn_b2', 'L3_gnn_ln1_g', 'L3_gnn_ln1_b',
        'L3_gnn_ln2_g', 'L3_gnn_ln2_b']


def kernel(**inputs):
    import numpy as _np
    import concourse.bacc as _bacc
    from concourse import mybir as _mybir
    from concourse.bass_utils import run_bass_kernel_spmd as _run

    nc = _bacc.Bacc("TRN2", target_bir_lowering=False, num_devices=1)
    arrays, args = {}, {}
    for name in _INS:
        a = _np.ascontiguousarray(inputs[name])
        arrays[f"in_{name}_dram"] = a
        args[name] = nc.dram_tensor(f"in_{name}_dram", a.shape, _mybir.dt.from_np(a.dtype), kind="ExternalInput").ap()
    out = nc.dram_tensor("out_0_dram", (N, D), _mybir.dt.float32, kind="ExternalOutput").ap()
    build(nc, args, out)
    r = _run(nc, [arrays], core_ids=[0])
    return r.results[0]["out_0_dram"]
```

```python
import concourse.bass as bass
from concourse import mybir
from contextlib import ExitStack

import numpy as np

N, D, E = 3125, 64, 100000
P = 128
NC = -(-N // P)
NF = N // P
NR = N - NF * P
NP = NC * P
EP = 125
EC = E // EP
GT = 8
NG = E // (GT * P) + NC
NT = NG * GT
assert NG % 2 == 0 and NG <= P
PAIRS = NG // 2
NG0 = 2 * NG
SG = EC // (2 * GT)
REC = D + 2
EPS, SLOPE = 1e-5, 0.2
PM, DENC = 256, 448
VA = 4
BIG = 1e30
H0, H3 = 4, 8
NA = {H0: 2, H3: 4}


def build(nc, t, out):
    F, I, U, BF = mybir.dt.float32, mybir.dt.int32, mybir.dt.uint32, mybir.dt.bfloat16
    ALU, ACT, AX = mybir.AluOpType, mybir.ActivationFunctionType, mybir.AxisListType.X
    ctx = ExitStack()
    with ctx:
        def sb(name, shape, dt=F):
            return ctx.enter_context(nc.sbuf_tensor(name, shape, dt))

        def ps(name, shape):
            return ctx.enter_context(nc.psum_tensor(name, shape, F))

        def sem(name):
            return ctx.enter_context(nc.semaphore(name))

        rec = nc.dram_tensor("rec_dram", (P * NT, REC), F).ap()
        recv = rec.rearrange("(p t) f -> p t f", p=P)
        slist = nc.dram_tensor("slist_dram", (P * NT, 2), F).ap()
        slv = slist.rearrange("(p t) f -> p t f", p=P)
        tab = [nc.dram_tensor(f"tab{k}_dram", (NP, w), F).ap() for k, w in enumerate((D, D, D, D, D + H3))]

        iota = sb("iota", [P, P])
        iota1 = iota[:, :]
        ones = sb("ones", [P, P])
        zrow = sb("zrow", [1, 512])
        tri = sb("tri", [P, P])
        triinc = sb("triinc", [P, P])
        ident = sb("ident", [P, P])
        identb = sb("identb", [P, P], BF)

        jidx = sb("jidx", [P, 2 * NT], U)
        iloc = sb("iloc", [P, 2 * NT])
        ctab = sb("ctab", [1, 2 * NG], I)

        arena = sb("arena", [P, 13312])
        arena2 = sb("arena2", [P, 6628])

        def cols(k, dt=F):
            v = arena[0:EP, k * EC:(k + 1) * EC]
            return v if dt == F else v.bitcast(dt)
        key_i = [cols(0, I), cols(1, I)]
        idf = [cols(2), cols(3)]
        lof = [cols(4), cols(5)]
        bkf = [cols(6), cols(7)]
        slot = [cols(8), cols(9)]
        mask = [cols(10), cols(11)]
        pos = [cols(12), cols(13)]
        sone = cols(14)
        low_i = cols(15, I)
        iota_i = arena2[:, 2 * NG:2 * NG + P].bitcast(I)
        gmat = arena2[0:NC, 0:2 * NG].rearrange("p (l t) -> p l t", l=2)
        rowidx = [arena2[0:EP, 512 + l * EC:512 + (l + 1) * EC].bitcast(U) for l in range(2)]
        V3 = sb("V3", [P, GT, H3, D])
        V3f = V3[:].rearrange("p t h d -> p (t h d)")
        at = [H3 * D]

        def under_V3(parts, *shape):
            size = int(np.prod(shape))
            at[0] += size
            names = "abc"[:len(shape)]
            return V3f[0:parts, at[0] - size:at[0]].rearrange(f"p ({' '.join(names)}) -> p {' '.join(names)}", **dict(zip(names, shape)))
        slraw = under_V3(P, NT, 2)
        blank = under_V3(P, GT, REC)
        recst = V3f[0:EP, at[0]:at[0] + 2 * GT * REC].rearrange("p (q t f) -> p q t f", q=2, t=GT)
        cnt = [sb("cnt0", [EP, NC]), sb("cnt1", [EP, NC])]
        off = [sb("off0", [EP, NC]), sb("off1", [EP, NC])]
        tcol_i = sb("tcol_i", [NC, 2], I)
        tcol = sb("tcol", [NC, 2])
        t128 = sb("t128", [NC, 2, EP])
        endc = sb("endc", [NC, 2])

        sst = sb("sst", [EP, 2, GT, 2])
        rowst = sb("rowst", [EP, 2, GT], U)
        pdum = sb("pdum", [P, 2])
        vdum = sb("vdum", [1, 1])

        G = sb("G", [P, 4, GT, D + H3])
        oh = sb("oh", [P, 4, GT, P])
        ohb = sb("ohb", [P, GT, P], BF)
        ohT = sb("ohT", [P, 2, GT, P])
        pen = sb("pen", [P, 2, GT, P], BF)
        jst = sb("jst", [P, 4, GT], U)
        work = sb("work", [P, GT, D])
        sc = sb("sc", [P, 2, GT * H3])
        rem = sb("rem", [P, GT * H3])
        part = sb("part", [P, 2, GT, 3, H3], BF)
        sT = sb("sT", [3 * H3, 2, GT * P], BF)
        sel0 = sb("sel0", [3 * H0, H0, P], BF)
        sel3 = sb("sel3", [3 * H3, H3, P], BF)
        mx = sb("mx", [P, 2, H3])
        mn = sb("mn", [P, 2, H3])
        cr = sb("cr", [P, 2, H3])
        w = sb("w", [P, 2, GT * H3])
        V0 = sb("V0", [P, 2, GT, H0, D // H0 + 1])
        junk = sb("junk", [P, GT * P], BF)

        X = sb("X", [P, NC, D])
        Hn = sb("Hn", [P, NC, D])
        M = sb("M", [P, NC * H3])
        AS = sb("AS", [P, NC, 2 * H3])
        Dn, AD = (arena2[:, k * NC * H3:(k + 1) * NC * H3] for k in range(2))
        rden, es = (arena2[:, k * NC * H3:(k + 1) * NC * H3].rearrange("p (c h) -> p c h", h=H3) for k in (2, 3))
        b1c0 = sb("b1c0", [D, 1]); b1c3 = sb("b1c3", [2 * D, 1])
        st = sb("st", [P, 4, NC])
        invdeg = sb("invdeg", [P, NC])
        hasin = sb("hasin", [P, NC])
        nbr_r = sb("nbr_r", [P, NC, D])
        deg = sb("deg", [P, NC])

        def area(k, n=1):
            return arena[:, k * NC * D:(k + n) * NC * D]
        GL = area(0).rearrange("p (c d) -> p c d", d=D)
        GR = area(3).rearrange("p (c d) -> p c d", d=D)
        NRT = area(1, 2)[0:D, :]
        CAT = area(4, 2).rearrange("p (c d) -> p c d", d=2 * D)
        T = area(6, 2)
        XC = arena2[:, 3328:3328 + NC * D].rearrange("p (c d) -> p c d", d=D)
        SQ = arena2[:, 3328 + NC * D:3328 + 2 * NC * D].rearrange("p (c d) -> p c d", d=D)
        A0 = arena2[:, 3328 + NC * D:3328 + NC * D + NC * H0 * (D // H0 + 1)]
        T2 = area(4, 2)
        TT = [ohT[:, q, 0:4, :].rearrange("p t n -> p (t n)") for q in range(2)]
        TB3 = arena[:, 0:NC * (D + H3)].rearrange("p (c d) -> p c d", d=D + H3)
        OUTN = XC
        acc3 = arena[:, 0:NC * H3 * D]

        wraw = sb("wraw", [D, 7 * D])
        WT = sb("WT", [P, 5, D])
        W1a = sb("W1a", [P, 2, D]); W1b = sb("W1b", [D, 2, D])
        Wp = sb("Wp", [P, 4, D])
        watt = V3[0:D, 0].rearrange("p h d -> p (h d)")
        attsd = ohT[0:D].rearrange("p q t d -> p (q t d)")[:, 0:2 * H3 * D].rearrange("p (s f) -> p s f", s=2)
        Asd = sb("Asd", [D, 2, H3])
        F1 = sb("F1", [D, 2 * D]); F2 = sb("F2", [2 * D, D])
        attb = sb("attb", [P, D])
        bias = sb("bias", [1, 5, D])
        lnb = sb("lnb", [P, 5, D])

        acc = ps("acc", [P, 4 * 512])
        accw = ps("accw", [P, 512])
        pu = ps("pu", [P, 512])
        pt = ps("pt", [P, 1024])
        ptb = pt[:, 0:512].bitcast(BF)
        psT = pt[:, 512:1024].bitcast(BF)

        names = """iota sel rcp jdone const keys v cnt tot tcol end gm ct ctab rows blank fill attr0 attr1 recst pd scat0 scat1 sst
            sscat0 sscat1 rld0 rld1 roh rmm vl slist nbr x wts wtp wtc lnv lns tsrc tp tc lin ev tb up upc xp
            aoh aohb atr aoht apen aown au asp ast asc abc amx amn acr apm ad aw av aag aA
            doh dohb dtr doht dpen down du dsp dst dsc dbc dmx dmn dcr dpm dd dw dv dva dag dA
            coh cmm init3
            es fac ftp ftc fmm out""".split()
        names += [f"{x}{k}{r}" for x in "acd" for k in "jg" for r in range(4)]
        S = {x: sem("s_" + x) for x in names}

        attr_v = t["edge_attr_64"].rearrange("(p j) d -> p j d", p=EP)

        block = ctx.enter_context(nc.Block())

        def turns_before(r):
            return [r * len(range(k, NG, 4)) for k in range(4)]

        def pairs(eng, n, body):
            for q in range(2):
                body(0, q, True)
            with eng.Fori(1, n) as i:
                for q in range(2):
                    body(i, q, False)

        class Group:
            def __init__(self, i, t):
                self.g, self.r, self.q, self.turn = i * 4 + t, t % 4, t % 2, i + t // 4

        def after(eng, which, val):
            if not (isinstance(val, int) and val <= 0):
                eng.wait_ge(which, val)

        def quads(eng, n, body):
            for t in range(4):
                body(Group(0, t))
            with eng.Fori(1, n // 4) as i:
                for t in range(4):
                    body(Group(i, t))
            for t in range(n % 4):
                body(Group(n // 4, t))

        def pipe(eng, n, step):
            def at(i, t, all_in=False):
                step(*[Group(i, t + d) if all_in or 0 <= 4 * i + t + d < n else None for d in (1, 0, -1)])
            turns = (n - 1) // 4
            for t in range(-1, 4):
                at(0, t)
            with eng.Fori(1, turns) as i:
                for t in range(4):
                    at(i, t, True)
            for t in range(4 * turns, n + 1):
                at(0, t)

        @block.sync
        def _(sp):
            sp.dma_start(key_i[0], t["dst"].rearrange("(p j) -> p j", p=EP)).then_inc(S["keys"], 16)
            sp.dma_start(key_i[1], t["src"].rearrange("(p j) -> p j", p=EP)).then_inc(S["keys"], 16)
            sp.wait_ge(S["x"], 1)
            sp.dma_start(X[:, 0:NF, :], t["x"][0:NF * P, :].rearrange("(c p) d -> p c d", p=P)).then_inc(S["wts"], 16)
            sp.dma_start(X[0:NR, NF, :], t["x"][NF * P:N, :]).then_inc(S["wts"], 16)
            at = 0
            for name, wd in (("L0_gnn_Wl", D), ("L0_gnn_Wr", D), ("L0_gnn_W1", 2 * D), ("L0_gnn_W2", D), ("L2_gnn_W", 2 * D)):
                sp.dma_start(wraw[:, at:at + wd], t[name]).then_inc(S["wts"], 16)
                at += wd
            for k in range(2):
                sp.dma_start(W1a[:, k, :], t[f"L1_gnn_W{k + 1}"][0:2 * D, :]).then_inc(S["wts"], 16)
                sp.dma_start(W1b[:, k, :], t[f"L1_gnn_W{k + 1}"][2 * D:3 * D, :]).then_inc(S["wts"], 16)
                sp.dma_start(Wp[k * D:(k + 1) * D, :, :],
                             t["L3_gnn_W_att"].rearrange("d (q h c) -> h d q c", h=2, c=D)[k]).then_inc(S["wts"], 16)
                sp.dma_start(attsd[:, k, :], t["L3_gnn_att_" + ("src", "dst")[k]].rearrange("h c -> (h c)").unsqueeze(0)
                             .to_broadcast([D, H3 * D])).then_inc(S["wts"], 16)
            sp.dma_start(watt, t["L3_gnn_W_att"]).then_inc(S["wts"], 16)
            sp.dma_start(F1[:], t["L3_gnn_W1"]).then_inc(S["wts"], 16)
            sp.dma_start(F2[:], t["L3_gnn_W2"]).then_inc(S["wts"], 16)
            sp.dma_start(attb[:], t["L0_gnn_att"].rearrange("o h d -> o (h d)").to_broadcast([P, D])).then_inc(S["wts"], 16)
            for k, name in enumerate(("L0_gnn_b2", "L1_gnn_b1", "L1_gnn_b2", "L2_gnn_b", "L3_gnn_b2")):
                sp.dma_start(bias[:, k, :], t[name].unsqueeze(0)).then_inc(S["wts"], 16)
            for k, name in enumerate(("L3_gnn_bias_att", "L3_gnn_ln1_g", "L3_gnn_ln1_b", "L3_gnn_ln2_g", "L3_gnn_ln2_b")):
                sp.dma_start(lnb[:, k, :], t[name].unsqueeze(0).to_broadcast([P, D])).then_inc(S["wts"], 16)
            sp.dma_start(b1c0[:], t["L0_gnn_b1"].unsqueeze(1)).then_inc(S["wts"], 16)
            sp.dma_start(b1c3[:], t["L3_gnn_b1"].unsqueeze(1)).then_inc(S["wts"], 16)
            sp.wait_ge(S["blank"], 4)
            for k in range(2):
                sp.dma_start(recv[:, k * NT // 2:(k + 1) * NT // 2, :].rearrange("p (a b) f -> p a (b f)", b=GT),
                             blank[:].rearrange("p b f -> p (b f)").unsqueeze(1).to_broadcast([P, NG // 2, GT * REC])).then_inc(S["fill"], 16)
            sp.dma_start(slv, slraw[:]).then_inc(S["fill"], 16)

            def attrs(i, q, first):
                if not first:
                    sp.wait_ge(S[f"scat{q}"], i * 16 * GT)
                sp.dma_start(recst[:, q, :, 0:D], attr_v[:, bass.ds(i * 16 + q * 8, GT), :]).then_inc(S[f"attr{q}"], 16)
            pairs(sp, SG, attrs)

            for q in range(2):
                sp.wait_ge(S[f"scat{q}"], SG * 16 * GT)

            def recs(i, q, first):
                if not first:
                    sp.wait_ge(S["rmm"], i * 2 + q - 1)
                sp.dma_start(G[:, q, :, 0:REC], recv[:, bass.ds(i * 16 + q * 8, GT), :]).then_inc(S[f"rld{q}"], 16)
            pairs(sp, PAIRS, recs)
            for q in range(2):
                sp.wait_ge(S[f"sscat{q}"], SG * 16 * GT)
            sp.dma_start(slraw[:], slv).then_inc(S["slist"], 16)

            def table(k, n, src):
                sp.wait_ge(S["tsrc"], n)
                sp.dma_start(tab[k].rearrange("(c p) d -> p c d", p=P), src).then_inc(S["tb"], 16)

            def stage_gathers(x, n, R0):
                def body(a):
                    after(sp, S[f"{x}g{a.r}"], (R0[a.r] + a.turn) * 16 * GT)
                    sp.dma_start(jst[:, a.r, :], jidx[:, bass.ds(a.g * GT, GT)]).then_inc(S[f"{x}j{a.r}"], 16)
                quads(sp, n, body)

            table(0, 1, GR)
            sp.wait_ge(S["jdone"], 1)
            stage_gathers("a", NG0, (0,) * 4)
            for r in range(3):
                table(1 + r, 2 + r, Hn[:])
                stage_gathers("c", NG, turns_before(r))
            table(4, 5, TB3)
            stage_gathers("d", NG, (0,) * 4)
            sp.wait_ge(S["xp"], 1)
            sp.dma_start(out[0:NF * P, :].rearrange("(c p) d -> p c d", p=P), OUTN[:, 0:NF, :]).then_inc(S["out"], 16)
            sp.dma_start(out[NF * P:N, :], OUTN[0:NR, NF, :]).then_inc(S["out"], 16)
            sp.wait_ge(S["out"], 32)

        @block.gpsimd
        def _(gp):
            gp.iota(iota_i[:], [[1, P]], base=0, channel_multiplier=0).then_inc(S["iota"], 1)
            gp.memset(ones[:], 1.0).then_inc(S["const"], 1)
            gp.memset(zrow[:], 0.0).then_inc(S["const"], 1)
            gp.memset(pdum[:], 0.0).then_inc(S["pd"], 1)
            gp.memset(X[:], 0.0).then_inc(S["x"], 1)
            gp.memset(blank[:], 0.0).then_inc(S["blank"], 1)
            gp.memset(slraw[:], 0.0).then_inc(S["blank"], 1)
            gp.wait_ge(S["blank"], 2)
            gp.memset(blank[:, :, D + 1:REC], -1.0).then_inc(S["blank"], 1)
            gp.memset(slraw[:, :, 1:2], -1.0).then_inc(S["blank"], 1)
            gp.wait_ge(S["const"], 2)
            gp.affine_select(out=tri[:], in_=ones[:], compare_op=ALU.is_gt, fill=0.0, base=0,
                             pattern=[[1, P]], channel_multiplier=-1).then_inc(S["const"], 1)
            gp.affine_select(out=triinc[:], in_=ones[:], compare_op=ALU.is_ge, fill=0.0, base=0,
                             pattern=[[1, P]], channel_multiplier=-1).then_inc(S["const"], 1)
            gp.affine_select(out=ident[:], in_=ones[:], compare_op=ALU.is_equal, fill=0.0, base=0,
                             pattern=[[1, P]], channel_multiplier=-1).then_inc(S["const"], 1)
            for n, (sel, H) in enumerate(((sel0, H0), (sel3, H3))):
                gp.memset(sel[:], 0.0).then_inc(S["sel"], 1)
                for k in range(3):
                    gp.wait_ge(S["sel"], 4 * n + k + 1)
                    gp.affine_select(out=sel[:], in_=sel[:], compare_op=ALU.not_equal, fill=1.0, base=-k * H,
                                     pattern=[[-1, H], [0, P]], channel_multiplier=1).then_inc(S["sel"], 1)
            gp.wait_ge(S["fill"], 16 * 3)

            def hold(sem_, val, count):
                gp.wait_ge(S["pd"], count)
                gp.wait_ge(sem_, val)
                nc.gpsimd.tensor_tensor(pdum[:, 1:2], pdum[:, 0:1], pdum[:, 0:1], ALU.add).then_inc(S["pd"], 1)

            def scatter_recs(i, q, first):
                hold(S[f"attr{q}"], (i + 1) * 16, i * 4 + 2 * q + 1)
                hold(S["recst"], (2 * i + q + 1) * 3, i * 4 + 2 * q + 2)
                for k in range(GT):
                    gp.indirect_dma_start(rec[:, :], bass.IndirectOffsetOnAxis(ap=rowst[:, q, k:k + 1], axis=0),
                                          recst[:, q, k, :], None).then_inc(S[f"scat{q}"], 16)
            pairs(gp, SG, scatter_recs)

            def scatter_s(i, q, first):
                hold(S["sst"], (2 * i + q + 1) * 3, SG * 4 + 2 * i + q + 1)
                for k in range(GT):
                    gp.indirect_dma_start(slist[:, :], bass.IndirectOffsetOnAxis(ap=rowst[:, q, k:k + 1], axis=0),
                                          sst[:, q, k, :], None).then_inc(S[f"sscat{q}"], 16)
            pairs(gp, SG, scatter_s)
            held = [SG * 6 + 1]

            def gather(x, n, R0, k, wd, freed):
                gp.wait_ge(S["tb"], 16 * (k + 1))

                def body(a):
                    hold(S[f"{x}j{a.r}"], (R0[a.r] + a.turn + 1) * 16, held[0] + a.g * 2)
                    which, val = freed(a)
                    if isinstance(val, int) and val <= 0:
                        which, val = S[f"{x}j{a.r}"], 16
                    hold(which, val, held[0] + a.g * 2 + 1)
                    for j in range(GT):
                        gp.indirect_dma_start(G[:, a.r, j, 0:wd], None, tab[k][:, :],
                                              bass.IndirectOffsetOnAxis(ap=jst[:, a.r, j:j + 1], axis=0)).then_inc(S[f"{x}g{a.r}"], 16)
                quads(gp, n, body)
                held[0] += 2 * n

            gather("a", NG0, (0,) * 4, 0, D, lambda a: (S["av"], a.g - 3))
            for r in range(3):
                gather("c", NG, turns_before(r), 1 + r, D, lambda a: (S["cmm"], r * NG + a.g - 3))
            gather("d", NG, (0,) * 4, 4, D + H3, lambda a: (S["dag"], a.g - 3))

        @block.scalar
        def _(act):
            A = nc.scalar
            act.wait_ge(S["wtp"], 1)
            A.copy(WT[0:D, :, :], pt[0:D, 0:5 * D].rearrange("p (k d) -> p k d", d=D)).then_inc(S["wtc"], 1)
            for k in (2, 4):
                A.copy(WT[D:2 * D, k, :], pt[D:2 * D, k * D:(k + 1) * D]).then_inc(S["wtc"], 1)
            ntc, nln = [0], [0]

            def transposed(K, dst=None):
                for b in range(-(-NC // 4)):
                    m = min(4, NC - 4 * b) * P
                    act.wait_ge(S["tp"], ntc[0] + 1)
                    bank = (ntc[0] % 2) * 512
                    A.copy((T if dst is None else dst)[0:K, b * 512:b * 512 + m], pt[0:K, bank:bank + m]).then_inc(S["tc"], 1)
                    ntc[0] += 1

            def sqrt_():
                nln[0] += 1
                act.wait_ge(S["lnv"], nln[0])
                A.activation(st[:, 2, :], st[:, 1, :], ACT.Sqrt).then_inc(S["lns"], 1)

            def ff_up(n0, func, K, b1):
                for g in range(8):
                    act.wait_ge(S["up"], n0 + g + 1)
                    A.activation(T2[0:K, g * 400:(g + 1) * 400], (pu, accw)[g % 2][0:K, 0:400], func, bias=b1[:]).then_inc(S["upc"], 1)
            sqrt_()
            transposed(D)
            act.wait_ge(S["rows"], 2)

            def stage(i, q, first):
                c = bass.ds(i * 16 + q * 8, GT)
                if not first:
                    act.wait_ge(S[f"scat{q}"], i * 16 * GT)
                nc.scalar.copy(recst[:, q, :, D:D + 1], idf[1][:, c].unsqueeze(2)).then_inc(S["recst"], 1)
                nc.scalar.copy(recst[:, q, :, D + 1:D + 2], lof[0][:, c].unsqueeze(2)).then_inc(S["recst"], 1)
                nc.scalar.copy(rowst[:, q, :], rowidx[0][:, c]).then_inc(S["recst"], 1)
            pairs(act, SG, stage)
            for q in range(2):
                act.wait_ge(S[f"scat{q}"], SG * 16 * GT)

            def stage_s(i, q, first):
                c = bass.ds(i * 16 + q * 8, GT)
                if not first:
                    act.wait_ge(S[f"sscat{q}"], i * 16 * GT)
                nc.scalar.copy(sst[:, q, :, 0:1], idf[0][:, c].unsqueeze(2)).then_inc(S["sst"], 1)
                nc.scalar.copy(sst[:, q, :, 1:2], lof[1][:, c].unsqueeze(2)).then_inc(S["sst"], 1)
                nc.scalar.copy(rowst[:, q, :], rowidx[1][:, c]).then_inc(S["sst"], 1)
            pairs(act, SG, stage_s)
            A = nc.scalar

            def attention(x, n, H):
                def step(a, b, c):
                    if a:
                        act.wait_ge(S[x + "oh"], a.g + 1)
                        after(act, S[x + "tr"], a.g)
                        A.copy(ohb[:], oh[:, a.r]).then_inc(S[x + "ohb"], 1)
                    if c and H == H3:
                        act.wait_ge(S[x + "w"], c.g + 1)
                        after(act, S[x + "ag"], c.g)
                        for k in range(GT - VA, GT):
                            for h in range(H):
                                last = A.activation(V3[:, k, h, :], G[:, c.r, k, 0:D], ACT.Copy,
                                                    scale=w[:, c.q, k * H + h:k * H + h + 1])
                            last.then_inc(S[x + "va"], 1)
                    if a:
                        act.wait_ge(S[x + "tr"], a.g + 1)
                        after(act, S[x + "pm"], a.g - 1)
                        src = ptb.rearrange("p (t n) -> p t n", n=P)
                        A.copy(ohT[:, a.q], src).then_inc(S[x + "oht"], 1)
                        after(act, S[x + "mx"], (a.g - 1) * H)
                        A.activation(pen[:, a.q], src, ACT.Copy, bias=-BIG, scale=BIG).then_inc(S[x + "pen"], 1)
                    if b:
                        act.wait_ge(S[x + "mn"], 3 * b.g + 2)
                        after(act, S[x + "A"], NA[H] * (b.g - 1))
                        A.activation(cr[:, b.q, 0:H], cr[:, b.q, 0:H], ACT.Exp).then_inc(S[x + "cr"], 1)
                        act.wait_ge(S[x + "d"], 2 * b.g + 2)
                        after(act, S[x + "ag"], b.g - 1)
                        A.activation(w[:, b.q, 0:GT * H], w[:, b.q, 0:GT * H], ACT.Exp).then_inc(S[x + "w"], 1)
                        if H == H0:
                            act.wait_ge(S[x + "w"], 2 * b.g + 1)
                            A.copy(V0[:, b.q, :, :, D // H0:], w[:, b.q, 0:GT * H].rearrange("p (t h o) -> p t h o", h=H, o=1)
                                   ).then_inc(S[x + "w"], 1)
                    if a:
                        act.wait_ge(S[x + "st"], a.g + 1)
                        after(act, S[x + "bc"], H * (a.g - 1))
                        A.copy(sT[0:3 * H, a.q], psT[0:3 * H]).then_inc(S[x + "sc"], 1)
                pipe(act, n, step)

            attention("a", NG0, H0)
            transposed(2 * D)
            ff_up(0, ACT.Gelu, D, b1c0)
            sqrt_()
            transposed(2 * D)
            transposed(D, NRT)
            transposed(2 * D)
            sqrt_()
            transposed(2 * D)
            sqrt_()
            transposed(D)

            attention("d", NG, H3)
            for c in range(NC):
                act.wait_ge(S["ftp"], c + 1)
                if c >= 2:
                    act.wait_ge(S["fmm"], c - 1)
                A.copy(TT[c % 2], pt[:, (c % 2) * 512:(c % 2) * 512 + 512]).then_inc(S["ftc"], 1)
            sqrt_()
            transposed(D)
            ff_up(8, ACT.Relu, 2 * D, b1c3)
            sqrt_()

        @block.vector
        def _(v):
            V = nc.vector
            n = [0]

            def link(ins):
                n[0] += 1
                ins.then_inc(S["v"], 1)
                v.wait_ge(S["v"], n[0])

            v.wait_ge(S["iota"], 1)
            link(V.tensor_copy(iota[:], iota_i[:]))
            v.wait_ge(S["const"], 5)
            link(V.tensor_copy(identb[:], ident[:]))
            link(V.memset(sone, 1.0))
            v.wait_ge(S["keys"], 32)
            for l in range(2):
                link(V.tensor_copy(idf[l], key_i[l]))
                link(V.tensor_scalar(low_i, key_i[l], 127, None, ALU.bitwise_and))
                link(V.tensor_copy(lof[l], low_i))
                link(V.tensor_scalar(key_i[l], key_i[l], 7, None, ALU.logical_shift_right))
                link(V.tensor_copy(bkf[l], key_i[l]))
                link(V.memset(slot[l], 0.0))
            base = n[0]
            with v.Fori(0, NC) as b:
                bs = iota[0:EP, bass.ds(b, 1)]
                for l in range(2):
                    V.tensor_scalar(mask[l], bkf[l], bs, 0.0, ALU.is_equal, ALU.add,
                                    accum_out=cnt[l][:, bass.ds(b, 1)]).then_inc(S["cnt"], 1)
                v.wait_ge(S["cnt"], b * 2 + 2)
            v.wait_ge(S["tot"], 1)
            link(V.tensor_scalar(tcol[:], pu[0:NC, 0:2], float(GT * P - 1), None, ALU.add))
            link(V.tensor_copy(tcol_i[:], tcol[:]))
            link(V.tensor_scalar(tcol_i[:], tcol_i[:], (GT * P).bit_length() - 1, None, ALU.logical_shift_right))
            link(V.tensor_copy(tcol[:], tcol_i[:]))
            for l in range(2):
                last = V.tensor_scalar(t128[:, l, :], ones[0:NC, 0:EP], tcol[:, l:l + 1], float(GT * P), ALU.mult, ALU.mult)
                last.then_inc(S["tcol"], 1)
            v.wait_ge(S["end"], 1)
            link(V.tensor_copy(endc[:], pu[0:NC, 8:10]))
            for l in range(2):
                link(V.tensor_copy(off[l][:], pu[0:EP, 64 + 32 * l:64 + 32 * l + NC]))
            for l in range(2):
                V.tensor_scalar(gmat[:, l, :], iota[0:NC, 0:NG], endc[:, l:l + 1], None, ALU.is_ge).then_inc(S["gm"], 1)
            v.wait_ge(S["ct"], 1)
            V.tensor_scalar(ctab[:, :], acc[0:1, 0:2 * NG], float(NC - 1), None, ALU.min).then_inc(S["ctab"], 1)
            with v.Fori(0, NC) as b:
                bs = iota[0:EP, bass.ds(b, 1)]
                for l in range(2):
                    V.tensor_scalar(mask[l], bkf[l], bs, None, ALU.is_equal).then_inc(S["vl"], 1)
                v.wait_ge(S["vl"], b * 7 + 2)
                for l in range(2):
                    V.tensor_tensor_scan(pos[l], sone, mask[l], off[l][:, bass.ds(b, 1)], ALU.mult, ALU.add).then_inc(S["vl"], 1)
                v.wait_ge(S["vl"], b * 7 + 4)
                V.memset(vdum[:], 0.0).then_inc(S["vl"], 1)
                for l in range(2):
                    V.copy_predicated(slot[l], mask[l].bitcast(U), pos[l]).then_inc(S["vl"], 1)
                v.wait_ge(S["vl"], b * 7 + 7)
            for l in range(2):
                link(V.tensor_scalar(key_i[0], slot[l], -1.0, None, ALU.add))
                link(V.tensor_scalar(key_i[1], key_i[0], 7, None, ALU.logical_shift_right))
                link(V.tensor_scalar(key_i[0], key_i[0], 127, None, ALU.bitwise_and))
                link(V.tensor_copy(pos[0], key_i[0]))
                link(V.tensor_copy(pos[1], key_i[1]))
                link(V.scalar_tensor_tensor(slot[l], pos[0], float(NT), pos[1], ALU.mult, ALU.add))
                V.tensor_copy(rowidx[l][:], slot[l]).then_inc(S["rows"], 1)

            nln = [0]

            def norm(dst, src, g=None, b=None):
                link(V.tensor_reduce(st[:, 0, :], src, AX, ALU.add))
                link(V.tensor_scalar(st[:, 0, :], st[:, 0, :], 1.0 / D, None, ALU.mult))
                link(V.tensor_tensor(XC, src, st[:, 0, :].unsqueeze(2).to_broadcast([P, NC, D]), ALU.subtract))
                link(V.tensor_tensor(SQ, XC, XC, ALU.mult))
                link(V.tensor_reduce(st[:, 1, :], SQ, AX, ALU.add))
                V.tensor_scalar(st[:, 1, :], st[:, 1, :], 1.0 / D, EPS, ALU.mult, ALU.add).then_inc(S["lnv"], 1)
                nln[0] += 1
                v.wait_ge(S["lns"], nln[0])
                link(V.reciprocal(st[:, 3, :], st[:, 2, :]))
                link(V.tensor_tensor(XC, XC, st[:, 3, :].unsqueeze(2).to_broadcast([P, NC, D]), ALU.mult))
                if g is None:
                    link(V.tensor_scalar(dst, XC, 0.0, None, ALU.max))
                else:
                    link(V.tensor_tensor(XC, XC, lnb[:, g, :].unsqueeze(1).to_broadcast([P, NC, D]), ALU.mult))
                    link(V.tensor_tensor(dst, XC, lnb[:, b, :].unsqueeze(1).to_broadcast([P, NC, D]), ALU.add))

            acc_n = acc[:, 0:NC * D].rearrange("p (c d) -> p c d", d=D)
            v.wait_ge(S["wts"], 16 * 31)
            for k in range(2):
                link(V.tensor_tensor(attsd[:, k, :], attsd[:, k, :], watt, ALU.mult))
                link(V.tensor_reduce(Asd[:, k, :], attsd[:, k, :].rearrange("p (h c) -> p h c", c=D), AX, ALU.add))
            link(V.memset(M[:], -BIG))
            norm(Hn[:], X[:])
            link(V.memset(A0[:], 0.0))
            V.memset(vdum[:], 0.0).then_inc(S["ev"], 1)
            v.wait_ge(S["lin"], 1)
            V.tensor_copy(GL, acc_n).then_inc(S["ev"], 1)
            v.wait_ge(S["lin"], 2)
            V.tensor_copy(GR, acc_n).then_inc(S["tsrc"], 1)

            def rec_tiles(i, q, first):
                v.wait_ge(S[f"rld{q}"], (i + 1) * 16)
                c = bass.ds(i * 16 + q * 8, GT)
                V.tensor_copy(jidx[:, c].unsqueeze(2), G[:, q, :, D:D + 1]).then_inc(S["rcp"], 1)
                V.tensor_copy(iloc[:, c].unsqueeze(2), G[:, q, :, D + 1:REC]).then_inc(S["rcp"], 1)
                if not first:
                    v.wait_ge(S["rmm"], i * 2 + q - 1)
                V.tensor_tensor(oh[:, q], iota1.unsqueeze(1).to_broadcast([P, GT, P]),
                                G[:, q, :, D + 1:REC].to_broadcast([P, GT, P]), ALU.is_equal).then_inc(S["roh"], 1)
            pairs(v, PAIRS, rec_tiles)
            v.wait_ge(S["rmm"], 2 * PAIRS)
            link(V.tensor_copy(nbr_r[:], acc_n))
            link(V.tensor_copy(deg[:], accw[:, 0:NC]))
            link(V.tensor_scalar(invdeg[:], deg[:], 1.0, None, ALU.max))
            link(V.reciprocal(invdeg[:], invdeg[:]))
            link(V.tensor_scalar(hasin[:], deg[:], 0.0, None, ALU.is_gt))
            deg_b = invdeg[:].unsqueeze(2).to_broadcast([P, NC, D])
            V.tensor_tensor(nbr_r[:], nbr_r[:], deg_b, ALU.mult).then_inc(S["ev"], 1)
            v.wait_ge(S["slist"], 16)
            link(V.tensor_copy(iloc[:, NT:2 * NT], slraw[:, :, 1]))
            link(V.tensor_copy(jidx[:, NT:2 * NT], slraw[:, :, 0]))
            V.memset(vdum[:], 0.0).then_inc(S["jdone"], 1)

            def chunk_of(g):
                return nc.values_load(ctab[0:1, bass.ds(g, 1)], engines=[mybir.EngineType.DVE], min_val=0, max_val=NC - 1)

            def onehots(which, a):
                V.tensor_tensor(oh[:, a.r], iota1.unsqueeze(1).to_broadcast([P, GT, P]),
                                iloc[:, bass.ds(a.g * GT, GT)].unsqueeze(2).to_broadcast([P, GT, P]),
                                ALU.is_equal).then_inc(which, 1)

            def attention(x, n, H):
                HD = D // H0 + 1 if H == H0 else D
                wd = GT * H
                nu = 4 if H == H0 else 2
                Asum = A0 if H == H0 else acc3

                def step(a, b, c):
                    if a:
                        after(v, S[x + "ag"], a.g - 3)
                        onehots(S[x + "oh"], a)
                    if c:
                        v.wait_ge(S[x + "w"], (2 if H == H0 else 1) * (c.g + 1))
                        if H == H0:
                            after(v, S[x + "ag"], c.g - 1)
                            V.tensor_tensor(V0[:, c.q, :, :, 0:D // H0], G[:, c.r, :, 0:D].rearrange("p t (h d) -> p t h d", h=H0),
                                            w[:, c.q, 0:wd].rearrange("p (t h) -> p t h", h=H).unsqueeze(3).to_broadcast([P, GT, H0, D // H0]),
                                            ALU.mult).then_inc(S[x + "v"], 1)
                        else:
                            after(v, S[x + "ag"], c.g)
                            for k in range(GT - VA):
                                V.tensor_tensor(V3[:, k], G[:, c.r, k, 0:D].unsqueeze(1).to_broadcast([P, H, D]),
                                                w[:, c.q, k * H:(k + 1) * H].unsqueeze(2).to_broadcast([P, H, D]),
                                                ALU.mult).then_inc(S[x + "v"], 1)
                    if b:
                        v.wait_ge(S[x + "pen"], b.g + 1)
                        after(v, S[x + "mn"], 3 * (b.g - 1))
                        for h in range(H):
                            v.wait_ge(S[x + "bc"], H * b.g + h + 1)
                            after(v, S[x + "mx"], H * b.g + h)
                            V.memset(vdum[:], 0.0)
                            V.tensor_tensor_reduce(out=junk[:], in0=pen[:, b.q].rearrange("p t n -> p (t n)"),
                                                   in1=acc[:, (h % 2) * 1024:(h % 2) * 1024 + 1024], scale=1.0, scalar=-BIG,
                                                   op0=ALU.add, op1=ALU.max, accum_out=mx[:, b.q, h:h + 1]).then_inc(S[x + "mx"], 1)
                        cb = chunk_of(b.g)
                        m = M[:, bass.ds(cb * H, H)]
                        v.wait_ge(S[x + "mx"], H * (b.g + 1))
                        after(v, S[x + "pm"], b.g - 1)
                        V.tensor_tensor(mn[:, b.q, 0:H], m, mx[:, b.q, 0:H], ALU.max).then_inc(S[x + "mn"], 1)
                        v.wait_ge(S[x + "mn"], 3 * b.g + 1)
                        after(v, S[x + "A"], NA[H] * (b.g - 1))
                        V.tensor_tensor(cr[:, b.q, 0:H], m, mn[:, b.q, 0:H], ALU.subtract).then_inc(S[x + "mn"], 1)
                        v.wait_ge(S[x + "mn"], 3 * b.g + 2)
                        V.tensor_tensor(m, mn[:, b.q, 0:H], mn[:, b.q, 0:H], ALU.max).then_inc(S[x + "mn"], 1)
                    if a:
                        v.wait_ge(S[f"{x}g{a.r}"], (a.turn + 1) * 16 * GT)
                        v.wait_ge(S[x + "own"], a.g + 1)
                        s_a = sc[:, a.q, 0:wd]
                        after(v, S[x + "u"], nu * a.g)
                        if H == H0:
                            V.tensor_tensor(work[:], pu[:, :].rearrange("p (t d) -> p t d", d=D), G[:, a.r, :, 0:D], ALU.add).then_inc(S[x + "u"], 1)
                            v.wait_ge(S[x + "u"], nu * a.g + 1)
                            V.scalar_tensor_tensor(work[:], work[:], SLOPE, work[:], ALU.mult, ALU.max).then_inc(S[x + "u"], 1)
                            v.wait_ge(S[x + "u"], nu * a.g + 2)
                            V.tensor_tensor(work[:], work[:], attb[:].unsqueeze(1).to_broadcast([P, GT, D]), ALU.mult).then_inc(S[x + "u"], 1)
                            v.wait_ge(S[x + "u"], nu * a.g + 3)
                            after(v, S[x + "d"], 2 * (a.g - 1))
                            V.tensor_reduce(s_a, work[:].rearrange("p t (h d) -> p (t h) d", h=H0), AX, ALU.add).then_inc(S[x + "u"], 1)
                        else:
                            after(v, S[x + "d"], 2 * (a.g - 1))
                            V.tensor_tensor(s_a.rearrange("p (t h) -> p t h", h=H), pu[:, 0:wd].rearrange("p (t h) -> p t h", h=H),
                                            G[:, a.r, :, D:D + H], ALU.add).then_inc(S[x + "u"], 1)
                            v.wait_ge(S[x + "u"], nu * a.g + 1)
                            V.scalar_tensor_tensor(s_a, s_a, SLOPE, s_a, ALU.mult, ALU.max).then_inc(S[x + "u"], 1)
                        v.wait_ge(S[x + "u"], nu * (a.g + 1))
                        after(v, S[x + "st"], a.g - 1)
                        s3 = s_a.rearrange("p (t h) -> p t h", h=H)
                        r3 = rem[:, 0:wd].rearrange("p (t h) -> p t h", h=H)
                        p3 = [part[:, a.q].rearrange("p t k h -> p (t k h)")[:, 0:3 * wd].rearrange("p (t k h) -> p t k h", k=3, h=H)[:, :, k, :]
                              for k in range(3)]
                        V.tensor_copy(p3[0], s3).then_inc(S[x + "sp"], 1)
                        v.wait_ge(S[x + "sp"], 5 * a.g + 1)
                        V.tensor_tensor(r3, s3, p3[0], ALU.subtract).then_inc(S[x + "sp"], 1)
                        v.wait_ge(S[x + "sp"], 5 * a.g + 2)
                        V.tensor_copy(p3[1], r3).then_inc(S[x + "sp"], 1)
                        v.wait_ge(S[x + "sp"], 5 * a.g + 3)
                        V.tensor_tensor(r3, r3, p3[1], ALU.subtract).then_inc(S[x + "sp"], 1)
                        v.wait_ge(S[x + "sp"], 5 * a.g + 4)
                        V.tensor_copy(p3[2], r3).then_inc(S[x + "sp"], 1)
                    if b:
                        v.wait_ge(S[x + "pm"], b.g + 1)
                        after(v, S[x + "ag"], b.g - 1)
                        w_b = w[:, b.q, 0:wd]
                        pm = (accw if H == H0 else pu)[:, PM:PM + wd]
                        V.tensor_tensor(w_b, sc[:, b.q, 0:wd], pm, ALU.subtract).then_inc(S[x + "d"], 1)
                        v.wait_ge(S[x + "d"], 2 * b.g + 1)
                        V.tensor_scalar(w_b, w_b, 0.0, None, ALU.min).then_inc(S[x + "d"], 1)
                    if c:
                        cc = chunk_of(c.g)
                        v.wait_ge(S[x + "ag"], c.g + 1)
                        v.wait_ge(S[x + "cr"], c.g + 1)
                        at = NA[H] * c.g
                        after(v, S[x + "A"], at)
                        so = Asum[:, bass.ds(cc * (H * HD), H * HD)]
                        V.tensor_tensor(so.rearrange("p (h d) -> p h d", h=H), so.rearrange("p (h d) -> p h d", h=H),
                                        cr[:, c.q, 0:H].unsqueeze(2).to_broadcast([P, H, HD]), ALU.mult).then_inc(S[x + "A"], 1)
                        if H == H3:
                            dn = Dn[:, bass.ds(cc * H, H)]
                            V.tensor_tensor(dn, dn, cr[:, c.q, 0:H], ALU.mult).then_inc(S[x + "A"], 1)
                        v.wait_ge(S[x + "A"], at + 1)
                        V.tensor_tensor(so, so, accw[:, 0:H * HD], ALU.add).then_inc(S[x + "A"], 1)
                        if H == H3:
                            v.wait_ge(S[x + "A"], at + 2)
                            V.tensor_tensor(dn, dn, pu[:, DENC:DENC + H], ALU.add).then_inc(S[x + "A"], 1)
                pipe(v, n, step)
                v.wait_ge(S[x + "A"], NA[H] * n)

            attention("a", NG0, H0)
            A0v = A0[:].rearrange("p (c h e) -> p c h e", c=NC, h=H0)
            den = es[:, :, 0:H0]
            link(V.tensor_scalar(den, A0v[:, :, :, D // H0], 1e-16, None, ALU.add))
            link(V.reciprocal(den, den))
            for c in range(NC):
                last = V.tensor_tensor(CAT[:, c, 0:D].rearrange("p (h d) -> p h d", h=H0), A0v[:, c, :, 0:D // H0],
                                       es[:, c, 0:H0].unsqueeze(2).to_broadcast([P, H0, D // H0]), ALU.mult)
            last.then_inc(S["v"], 1)
            n[0] += 1
            V.tensor_copy(CAT[:, :, D:2 * D], Hn[:]).then_inc(S["ev"], 1)
            v.wait_ge(S["lin"], 3)
            link(V.tensor_tensor(X[:], X[:], acc_n, ALU.add))
            norm(Hn[:], X[:])
            V.memset(vdum[:], 0.0).then_inc(S["tsrc"], 1)

            for r in range(3):
                def gathered(a):
                    after(v, S["cmm"], r * NG + a.g - 3)
                    onehots(S["coh"], a)
                quads(v, NG, gathered)
                v.wait_ge(S["cmm"], (r + 1) * NG)
                link(V.tensor_copy(CAT[:, :, 0:D], Hn[:]))
                link(V.tensor_tensor(CAT[:, :, D:2 * D], acc_n, deg_b, ALU.mult))
                if r == 2:
                    link(V.tensor_tensor(CAT[:, :, D:2 * D], CAT[:, :, D:2 * D], Hn[:], ALU.subtract))
                V.memset(vdum[:], 0.0).then_inc(S["ev"], 1)
                v.wait_ge(S["lin"], 4 + r)
                if r == 0:
                    V.tensor_scalar(Hn[:], acc_n, 0.0, None, ALU.max).then_inc(S["tsrc"], 1)
                    continue
                if r == 1:
                    link(V.tensor_scalar(XC, acc_n, 0.0, None, ALU.max))
                else:
                    link(V.tensor_tensor(XC, acc_n, hasin[:].unsqueeze(2).to_broadcast([P, NC, D]), ALU.mult))
                link(V.tensor_tensor(X[:], X[:], XC, ALU.add))
                norm(Hn[:], X[:])
                if r == 1:
                    V.memset(vdum[:], 0.0).then_inc(S["tsrc"], 1)
            V.memset(vdum[:], 0.0).then_inc(S["ev"], 1)

            v.wait_ge(S["lin"], 7)
            link(V.tensor_copy(AS[:], acc[:, 0:NC * 2 * H3].rearrange("p (c h) -> p c h", h=2 * H3)))
            link(V.tensor_copy(TB3[:, :, 0:D], Hn[:]))
            V.tensor_copy(TB3[:, :, D:D + H3], AS[:, :, 0:H3]).then_inc(S["tsrc"], 1)
            Mv = M[:].rearrange("p (c h) -> p c h", h=H3)
            link(V.tensor_copy(AD[:].rearrange("p (c h) -> p c h", h=H3), AS[:, :, H3:2 * H3]))
            link(V.tensor_tensor(Mv, AS[:, :, 0:H3], AS[:, :, H3:2 * H3], ALU.add))
            link(V.scalar_tensor_tensor(Mv, Mv, SLOPE, Mv, ALU.mult, ALU.max))
            link(V.memset(Dn[:], 1.0))
            v.wait_ge(S["tb"], 16 * 5)
            for h in range(H3):
                last = V.tensor_copy(acc3.rearrange("p (c h d) -> p c h d", h=H3, d=D)[:, :, h, :], Hn[:])
            last.then_inc(S["init3"], 1)
            v.wait_ge(S["init3"], 1)
            attention("d", NG, H3)
            Dv = Dn[:].rearrange("p (c h) -> p c h", h=H3)
            link(V.tensor_scalar(rden[:], Dv, 1e-16, None, ALU.add))
            link(V.reciprocal(rden[:], rden[:]))
            link(V.tensor_scalar(rden[:], rden[:], 1.0 / H3, None, ALU.mult))
            for c in range(NC):
                o = acc3[:, c * H3 * D:(c + 1) * H3 * D].rearrange("p (h d) -> p h d", d=D)
                V.tensor_tensor(o, o, rden[:, c, :].unsqueeze(2).to_broadcast([P, H3, D]), ALU.mult).then_inc(S["fac"], 1)
            v.wait_ge(S["fmm"], NC)
            link(V.tensor_tensor(Hn[:], Hn[:], acc_n, ALU.add))
            link(V.tensor_tensor(Hn[:], Hn[:], lnb[:, 0, :].unsqueeze(1).to_broadcast([P, NC, D]), ALU.add))
            norm(Hn[:], Hn[:], 1, 2)
            V.memset(vdum[:], 0.0).then_inc(S["ev"], 1)
            v.wait_ge(S["lin"], 8)
            link(V.tensor_tensor(Hn[:], Hn[:], acc_n, ALU.add))
            norm(Hn[:], Hn[:], 3, 4)
            V.tensor_tensor(OUTN, X[:], Hn[:], ALU.add).then_inc(S["xp"], 1)

        @block.tensor
        def _(pe):
            pe.wait_ge(S["cnt"], 2 * NC)
            pe.wait_ge(S["const"], 5)
            for l in range(2):
                last = nc.tensor.matmul(pu[0:NC, l:l + 1], cnt[l][:], ones[0:EP, 0:1], start=True, stop=True)
            last.then_inc(S["tot"], 1)
            pe.wait_ge(S["tcol"], 2)
            nc.tensor.matmul(pu[0:NC, 8:10], triinc[0:NC, 0:NC], tcol[:], start=True, stop=True)
            for l in range(2):
                o = pu[0:EP, 64 + 32 * l:64 + 32 * l + NC]
                nc.tensor.matmul(o, tri[0:EP, 0:EP], cnt[l][:], start=True, stop=False)
                last = nc.tensor.matmul(o, t128[:, l, :], tri[0:NC, 0:NC], start=False, stop=True)
            last.then_inc(S["end"], 1)
            pe.wait_ge(S["gm"], 2)
            last = nc.tensor.matmul(acc[0:1, 0:2 * NG], ones[0:NC, 0:1], gmat[:, :, :].rearrange("p l t -> p (l t)"), start=True, stop=True)
            last.then_inc(S["ct"], 1)

            pe.wait_ge(S["wts"], 16 * 31)
            at = 0
            for k, wd in enumerate((D, D, 2 * D, D, 2 * D)):
                last = nc.tensor.transpose(pt[0:wd, k * D:(k + 1) * D], wraw[:, at:at + wd], ident[0:D, 0:D])
                at += wd
            last.then_inc(S["wtp"], 1)
            pe.wait_ge(S["wtc"], 3)
            ntp, nln, nup = [0], [0], [0]

            def transposes(src, K):
                for b in range(-(-NC // 4)):
                    if ntp[0] >= 2:
                        pe.wait_ge(S["tc"], ntp[0] - 1)
                    bank = (ntp[0] % 2) * 512
                    for j in range(min(4, NC - 4 * b)):
                        last = nc.tensor.transpose(pt[0:K, bank + j * P:bank + (j + 1) * P], src[:, 4 * b + j, :], ident[:])
                    last.then_inc(S["tp"], 1)
                    ntp[0] += 1

            def product(parts, width, bk=None):
                pe.wait_ge(S["tc"], ntp[0])
                for c in range(NC):
                    o = acc[:, c * width:(c + 1) * width]
                    for n, (TL, K, R) in enumerate(parts):
                        last = nc.tensor.matmul(o, TL[0:K, c * P:(c + 1) * P], R, start=n == 0, stop=n == len(parts) - 1 and bk is None)
                    if bk is not None:
                        last = nc.tensor.matmul(o, ones[0:1, :], bias[:, bk, :], start=False, stop=True)
                last.then_inc(S["lin"], 1)

            def hidden(W, K, n0):
                pe.wait_ge(S["tc"], ntp[0])
                for g in range(8):
                    if g >= 2:
                        pe.wait_ge(S["upc"], n0 + g - 1)
                    nc.tensor.matmul((pu, accw)[g % 2][0:W.shape[1], 0:400], W, T[0:K, g * 400:(g + 1) * 400],
                                     start=True, stop=True).then_inc(S["up"], 1)
                pe.wait_ge(S["upc"], n0 + 8)

            def zero_acc():
                for k in range(4):
                    nc.tensor.matmul(acc[:, k * 512:(k + 1) * 512], zrow[0:1, 0:P], zrow[0:1, :], start=True, stop=True,
                                     skip_group_check=True)
                zero_accw()

            def zero_accw():
                nc.tensor.matmul(accw[:, :], zrow[0:1, 0:P], zrow[0:1, :], start=True, stop=True, skip_group_check=True)

            pe.wait_ge(S["ctab"], 1)
            pe.wait_ge(S["ev"], 1)
            transposes(Hn[:], D)
            product([(T, D, WT[0:D, 0, :])], D)
            pe.wait_ge(S["ev"], 2)
            product([(T, D, WT[0:D, 1, :])], D)
            pe.wait_ge(S["tsrc"], 1)

            def chunk_of(g):
                return nc.values_load(ctab[0:1, bass.ds(g, 1)], engines=[mybir.EngineType.PE], min_val=0, max_val=NC - 1)

            zero_acc()

            def rec_mm(i, q, first):
                chunk = chunk_of(i * 2 + q)
                pe.wait_ge(S["roh"], 2 * i + q + 1)
                o, od = acc[:, bass.ds(chunk * D, D)], accw[:, bass.ds(chunk, 1)]
                for k in range(GT):
                    nc.tensor.matmul(o, oh[:, q, k, :], G[:, q, k, 0:D], start=False, stop=True, skip_group_check=True)
                    last = nc.tensor.matmul(od, oh[:, q, k, :], ones[:, 0:1], start=False, stop=True, skip_group_check=True)
                last.then_inc(S["rmm"], 1)
            pairs(pe, PAIRS, rec_mm)

            def attention(x, n, H, table, width):
                sel = sel0 if H == H0 else sel3
                HD = D // H0 + 1 if H == H0 else D
                pmb = accw if H == H0 else pu

                def step(a, b, c):
                    def spread(h):
                        after(pe, S[x + "mx"], H * b.g + h - 1)
                        for j in range(2):
                            last = nc.tensor.matmul(acc[:, (h % 2) * 1024 + j * 512:(h % 2) * 1024 + j * 512 + 512], sel[:, h, :],
                                                    sT[0:3 * H, b.q, j * 512:(j + 1) * 512], start=True, stop=True)
                        last.then_inc(S[x + "bc"], 1)
                    if b:
                        pe.wait_ge(S[x + "sc"], b.g + 1)
                        spread(0)
                        spread(1)
                    if a:
                        pe.wait_ge(S[x + "ohb"], a.g + 1)
                        after(pe, S[x + "pen"], a.g)
                        after(pe, S[x + "oht"], a.g)
                        for k in range(GT):
                            last = nc.tensor.transpose(ptb[:, k * P:(k + 1) * P], ohb[:, k, :], identb[:])
                        last.then_inc(S[x + "tr"], 1)
                    if b:
                        spread(2)
                    if c:
                        after(pe, S[x + "A"], NA[H] * c.g)
                        if H == H0:
                            pe.wait_ge(S[x + "v"], c.g + 1)
                            for k in range(GT):
                                last = nc.tensor.matmul(accw[:, 0:H * HD], oh[:, c.r, k, :], V0[:, c.q, k].rearrange("p h e -> p (h e)"),
                                                        start=k == 0, stop=k == GT - 1)
                        else:
                            pe.wait_ge(S[x + "w"], c.g + 1)
                            for k in range(GT):
                                nc.tensor.matmul(pu[:, DENC:DENC + H], oh[:, c.r, k, :], w[:, c.q, k * H:(k + 1) * H],
                                                 start=k == 0, stop=k == GT - 1)
                            for k in range(GT):
                                if k < GT - VA:
                                    pe.wait_ge(S[x + "v"], (GT - VA) * c.g + k + 1)
                                else:
                                    pe.wait_ge(S[x + "va"], VA * c.g + k - (GT - VA) + 1)
                                last = nc.tensor.matmul(accw[:, 0:H * HD], oh[:, c.r, k, :], V3[:, k].rearrange("p h d -> p (h d)"),
                                                        start=k == 0, stop=k == GT - 1)
                        last.then_inc(S[x + "ag"], 1)
                    if b:
                        for h in range(3, H):
                            spread(h)
                    if a:
                        rows = table[:, bass.ds(chunk_of(a.g) * width, width)]
                        pe.wait_ge(S[x + "oht"], a.g + 1)
                        after(pe, S[x + "u"], (4 if H == H0 else 2) * (a.g - 1) + 1)
                        for k in range(GT):
                            last = nc.tensor.matmul(pu[:, k * width:(k + 1) * width], ohT[:, a.q, k, :], rows, start=True, stop=True)
                        last.then_inc(S[x + "own"], 1)
                    if b:
                        pe.wait_ge(S[x + "mn"], 3 * b.g + 1)
                        after(pe, S[x + "d"], 2 * b.g - 1)
                        if a and H == H3:
                            pe.wait_ge(S[x + "u"], 2 * a.g + 1)
                        for k in range(GT):
                            last = nc.tensor.matmul(pmb[:, PM + k * H:PM + (k + 1) * H], ohT[:, b.q, k, :], mn[:, b.q, 0:H],
                                                    start=True, stop=True)
                        last.then_inc(S[x + "pm"], 1)
                    if a:
                        pe.wait_ge(S[x + "sp"], 5 * (a.g + 1))
                        after(pe, S[x + "sc"], a.g)
                        pa = part[:, a.q].rearrange("p t k h -> p (t k h)")
                        for k in range(GT):
                            last = nc.tensor.transpose(psT[0:3 * H, k * P:(k + 1) * P], pa[:, k * 3 * H:(k + 1) * 3 * H], identb[:])
                        last.then_inc(S[x + "st"], 1)
                pipe(pe, n, step)

            pe.wait_ge(S["ev"], 3)
            pe.wait_ge(S["jdone"], 1)
            pe.wait_ge(S["sel"], 8)
            GLf = area(0)

            attention("a", NG0, H0, GLf, D)
            pe.wait_ge(S["ev"], 4)
            transposes(CAT, 2 * D)
            hidden(WT[:, 2, :], 2 * D, 0)
            product([(T2, D, WT[0:D, 3, :])], D, 0)

            for r in range(3):
                pe.wait_ge(S["tsrc"], 2 + r)
                zero_acc()

                def mean_mm(a):
                    chunk = chunk_of(a.g)
                    pe.wait_ge(S["coh"], r * NG + a.g + 1)
                    pe.wait_ge(S[f"cg{a.r}"], (turns_before(r)[a.r] + a.turn + 1) * 16 * GT)
                    o = acc[:, bass.ds(chunk * D, D)]
                    for k in range(GT):
                        last = nc.tensor.matmul(o, oh[:, a.r, k, :], G[:, a.r, k, 0:D], start=False, stop=True, skip_group_check=True)
                    last.then_inc(S["cmm"], 1)
                quads(pe, NG, mean_mm)
                pe.wait_ge(S["ev"], 5 + r)
                transposes(CAT, 2 * D)
                if r == 0:
                    transposes(nbr_r[:], D)
                if r < 2:
                    product([(T, 2 * D, W1a[:, r, :]), (NRT, D, W1b[:, r, :])], D, 1 + r)
                else:
                    product([(T, 2 * D, WT[:, 4, :])], D, 3)

            pe.wait_ge(S["ev"], 8)
            transposes(Hn[:], D)
            product([(T, D, Asd[:].rearrange("p s h -> p (s h)"))], 2 * H3)
            pe.wait_ge(S["tsrc"], 5)

            pe.wait_ge(S["init3"], 1)
            attention("d", NG, H3, AD[:], H3)
            for c in range(NC + 1):
                if c < NC:
                    pe.wait_ge(S["fac"], c + 1)
                    if c >= 2:
                        pe.wait_ge(S["ftc"], c - 1)
                    for j in range(4):
                        last = nc.tensor.transpose(pt[:, (c % 2) * 512 + j * P:(c % 2) * 512 + (j + 1) * P],
                                                   acc3[:, c * 512 + j * P:c * 512 + (j + 1) * P], ident[:])
                    last.then_inc(S["ftp"], 1)
                if c:
                    pe.wait_ge(S["ftc"], c)
                    for j in range(4):
                        last = nc.tensor.matmul(acc[:, (c - 1) * D:c * D], TT[(c - 1) % 2][:, j * P:(j + 1) * P], Wp[:, j, :],
                                                start=j == 0, stop=j == 3)
                    last.then_inc(S["fmm"], 1)
            pe.wait_ge(S["ev"], 9)
            transposes(Hn[:], D)
            hidden(F1[:], D, 8)
            product([(T2, 2 * D, F2[:])], D, 4)


_INS = ['x', 'src', 'dst', 'edge_attr_64', 'L0_gnn_Wl', 'L0_gnn_Wr', 'L0_gnn_att', 'L0_gnn_W1', 'L0_gnn_b1', 'L0_gnn_W2', 'L0_gnn_b2',
        'L1_gnn_W1', 'L1_gnn_b1', 'L1_gnn_W2', 'L1_gnn_b2', 'L2_gnn_W', 'L2_gnn_b', 'L3_gnn_W_att', 'L3_gnn_att_src',
        'L3_gnn_att_dst', 'L3_gnn_bias_att', 'L3_gnn_W1', 'L3_gnn_b1', 'L3_gnn_W2', 'L3_gnn_b2', 'L3_gnn_ln1_g', 'L3_gnn_ln1_b',
        'L3_gnn_ln2_g', 'L3_gnn_ln2_b']


def kernel(**inputs):
    import numpy as _np
    import concourse.bacc as _bacc
    from concourse import mybir as _mybir
    from concourse.bass_utils import run_bass_kernel_spmd as _run

    nc = _bacc.Bacc("TRN2", target_bir_lowering=False, num_devices=1)
    arrays, args = {}, {}
    for name in _INS:
        a = _np.ascontiguousarray(inputs[name])
        arrays[f"in_{name}_dram"] = a
        args[name] = nc.dram_tensor(f"in_{name}_dram", a.shape, _mybir.dt.from_np(a.dtype), kind="ExternalInput").ap()
    out = nc.dram_tensor("out_0_dram", (N, D), _mybir.dt.float32, kind="ExternalOutput").ap()
    build(nc, args, out)
    r = _run(nc, [arrays], core_ids=[0])
    return r.results[0]["out_0_dram"]
```

```python
import concourse.bass as bass
from concourse import mybir
from contextlib import ExitStack

import numpy as np

N, D, E = 3125, 64, 100000
P = 128
NC = -(-N // P)
NF = N // P
NR = N - NF * P
NP = NC * P
EP = 125
EC = E // EP
GT = 8
NG = E // (GT * P) + NC
NT = NG * GT
assert NG % 4 == 2 and NG <= P
NG0 = 2 * NG
SG = EC // (2 * GT)
HT = GT // 2
SR = NG // 4
ST = EC // (4 * HT) - SR
MID = (NG - 10) // 4
assert MID >= ST + 2 and (SR + ST) * 4 * HT == EC
REC = D + 2
EPS, SLOPE = 1e-5, 0.2
PM, DENC = 256, 448
VA = 5
BIG = 1e30
H0, H3 = 4, 8


def build(nc, t, out):
    F, I, U, BF = mybir.dt.float32, mybir.dt.int32, mybir.dt.uint32, mybir.dt.bfloat16
    ALU, ACT, AX = mybir.AluOpType, mybir.ActivationFunctionType, mybir.AxisListType.X
    ctx = ExitStack()
    with ctx:
        def sb(name, shape, dt=F):
            return ctx.enter_context(nc.sbuf_tensor(name, shape, dt))

        def ps(name, shape):
            return ctx.enter_context(nc.psum_tensor(name, shape, F))

        def sem(name):
            return ctx.enter_context(nc.semaphore(name))

        rec = nc.dram_tensor("rec_dram", (P * NT, REC), F).ap()
        recv = rec.rearrange("(p t) f -> p t f", p=P)
        slist = nc.dram_tensor("slist_dram", (P * NT, 2), F).ap()
        slv = slist.rearrange("(p t) f -> p t f", p=P)
        tab = [nc.dram_tensor(f"tab{k}_dram", (NP, w), F).ap() for k, w in enumerate((D, D, D, D, D + H3))]

        iota = sb("iota", [P, P])
        iota1 = iota[:, :]
        iotab = sb("iotab", [P, P], BF)
        ones = sb("ones", [P, P])
        zrow = sb("zrow", [1, 512])
        onesb = sb("onesb", [P, 1], BF)
        tri = sb("tri", [P, P])
        triinc = sb("triinc", [P, P])
        ident = sb("ident", [P, P])
        identb = sb("identb", [P, P], BF)

        jidx = sb("jidx", [P, 2 * NT], U)
        iloc = sb("iloc", [P, 2 * NT], BF)
        ctab = sb("ctab", [1, 2 * NG], I)

        arena = sb("arena", [P, 13312])
        arena2 = sb("arena2", [P, 6628])

        def cols(k, dt=F):
            v = arena[0:EP, k * EC:(k + 1) * EC]
            return v if dt == F else v.bitcast(dt)
        key_i = [cols(0, I), cols(1, I)]
        idf = [cols(2), cols(3)]
        lof = [cols(4), cols(5)]
        bkf = [cols(6), cols(7)]
        slot = [cols(8), cols(9)]
        mask = [cols(10), cols(11)]
        pos = [cols(12), cols(13)]
        sone = cols(14)
        low_i = cols(15, I)
        iota_i = arena2[:, 2 * NG:2 * NG + P].bitcast(I)
        gmat = arena2[0:NC, 0:2 * NG].rearrange("p (l t) -> p l t", l=2)
        rowidx = [arena2[0:EP, 512 + l * EC:512 + (l + 1) * EC].bitcast(U) for l in range(2)]
        V3 = sb("V3", [P, GT, H3, D])
        V3f = V3[:].rearrange("p t h d -> p (t h d)")
        at = [H3 * D]

        def under_V3(parts, *shape):
            size = int(np.prod(shape))
            at[0] += size
            names = "abc"[:len(shape)]
            return V3f[0:parts, at[0] - size:at[0]].rearrange(f"p ({' '.join(names)}) -> p {' '.join(names)}", **dict(zip(names, shape)))
        slraw = under_V3(P, NT, 2)
        blank = under_V3(P, GT, REC)
        recst = V3f[0:EP, at[0]:at[0] + 2 * GT * REC].rearrange("p (q t f) -> p q t f", q=2, t=GT)
        cnt = [sb("cnt0", [EP, NC]), sb("cnt1", [EP, NC])]
        off = [sb("off0", [EP, NC]), sb("off1", [EP, NC])]
        tcol_i = sb("tcol_i", [NC, 2], I)
        tcol = sb("tcol", [NC, 2])
        t128 = sb("t128", [NC, 2, EP])
        endc = sb("endc", [NC, 2])

        sst = sb("sst", [EP, 4, HT, 2])
        rowst = sb("rowst", [EP, 4, GT], U)
        pdum = sb("pdum", [P, 2])
        vdum = sb("vdum", [1, 4])

        G = sb("G", [P, 4, GT, D + H3])
        oh = sb("oh", [P, 4, GT, P])
        ohb = sb("ohb", [P, 2, GT, P], BF)
        ohT = sb("ohT", [P, 2, GT, P], BF)
        pen = sb("pen", [P, 2, GT, P], BF)
        jst = sb("jst", [P, 4, GT], U)
        work = sb("work", [P, GT, D])
        mne = sb("mne", [P, GT * H3])
        sc = sb("sc", [P, 2, GT * H3])
        rem = sb("rem", [P, GT * H3])
        part = sb("part", [P, 2, GT, 3, H3], BF)
        sT = sb("sT", [3 * H3, 2, GT * P], BF)
        sel0 = sb("sel0", [3 * H0, H0, P], BF)
        sel3 = sb("sel3", [3 * H3, H3, P], BF)
        mx = sb("mx", [P, 2, H3])
        mn = sb("mn", [P, 2, H3])
        mnr = sb("mnr", [P, H3])
        mnp = sb("mnp", [P, 2, 3 * H3], BF)
        cr = sb("cr", [P, 2, H3])
        w = sb("w", [P, 2, GT * H3])
        V0 = sb("V0", [P, 2, GT, H0, D // H0 + 1])
        junk = sb("junk", [P, 2, GT * P], BF)

        X = sb("X", [P, NC, D])
        Hn = sb("Hn", [P, NC, D])
        M = sb("M", [P, NC * H3])
        AS = sb("AS", [P, NC, 2 * H3])
        Dn = arena2[:, 0:NC * H3]
        rden, rden0 = (arena2[:, k * NC * H3:(k + 1) * NC * H3].rearrange("p (c h) -> p c h", h=H3) for k in (2, 3))
        b1c0 = sb("b1c0", [D, 1]); b1c3 = sb("b1c3", [2 * D, 1])
        st = sb("st", [P, 4, NC])
        invdeg = sb("invdeg", [P, NC])
        hasin = sb("hasin", [P, NC])
        nbr_r = sb("nbr_r", [P, NC, D])
        deg = sb("deg", [P, NC])

        def area(k, n=1):
            return arena[:, k * NC * D:(k + n) * NC * D]
        GL = area(0).rearrange("p (c d) -> p c d", d=D)
        GR = area(3).rearrange("p (c d) -> p c d", d=D)
        NRT = area(1, 2)[0:D, :]
        CAT = area(4, 2).rearrange("p (c d) -> p c d", d=2 * D)
        T = area(6, 2)
        XC = arena2[:, 3328:3328 + NC * D].rearrange("p (c d) -> p c d", d=D)
        SQ = arena2[:, 3328 + NC * D:3328 + 2 * NC * D].rearrange("p (c d) -> p c d", d=D)
        A0 = arena2[:, 3328 + NC * D:3328 + NC * D + NC * H0 * (D // H0 + 1)]
        T2 = area(4, 2)
        own = {H0: area(4, 2).bitcast(BF)[:, 0:NC * 3 * D], H3: arena2[:, 4 * NC * H3:4 * NC * H3 + NC * 3 * H3 // 2].bitcast(BF)}
        TT = [ohT[:, q].rearrange("p t n -> p (t n)").bitcast(F) for q in range(2)]
        TB3 = arena[:, 0:NC * (D + H3)].rearrange("p (c d) -> p c d", d=D + H3)
        OUTN = XC
        acc3 = arena[:, 0:NC * H3 * D]

        wraw = sb("wraw", [D, 7 * D])
        WT = sb("WT", [P, 5, D])
        W1a = sb("W1a", [P, 2, D]); W1b = sb("W1b", [D, 2, D])
        Wp = sb("Wp", [P, 4, D])
        watt = V3[0:D, 0].rearrange("p h d -> p (h d)")
        attsd = ohT[0:D].rearrange("p q t d -> p (q t d)").bitcast(F).rearrange("p (s f) -> p s f", s=2)
        Asd = sb("Asd", [D, 2, H3])
        F1 = sb("F1", [D, 2 * D]); F2 = sb("F2", [2 * D, D])
        attb = sb("attb", [P, D])
        bias = sb("bias", [1, 5, D])
        lnb = sb("lnb", [P, 5, D])

        acc = ps("acc", [P, 4 * 512])
        accw = ps("accw", [P, 512])
        pu = ps("pu", [P, 512])
        pt = ps("pt", [P, 1024])
        ptb = pt[:, 0:512].bitcast(BF)
        psT = pt[:, 512:1024].bitcast(BF)

        names = """iota sel rcp jdone const keys v cnt tot tcol end gm ct ctab rows blank fill attr0 attr1 recst pd scat0 scat1 sst
            sscat0 sscat1 sscat2 sscat3 rob rld0 rld1 rld2 rld3 roh rmm vl slist x wts wtp wtc lnv lns tsrc tp tc lin ev tb up upc xp
            aoh aohf atr aoht apen aown au asp ast asc abc amx amn amp acr apm ad aw av aag aA
            doh dohf dtr doht dpen down du dsp dst dsc dbc dmx dmn dmp dcr dpm dd dw dv dva dag dA
            dden ddn coh cmm init3
            fac ftp ftc fmm out""".split()
        names += [f"{x}{k}{r}" for x in "acd" for k in "jg" for r in range(4)]
        S = {x: sem("s_" + x) for x in names}

        attr_v = t["edge_attr_64"].rearrange("(p j) d -> p j d", p=EP)

        block = ctx.enter_context(nc.Block())

        def turns_before(r):
            return [r * len(range(k, NG, 4)) for k in range(4)]

        def pairs(eng, n, body):
            for q in range(2):
                body(0, q, True)
            with eng.Fori(1, n) as i:
                for q in range(2):
                    body(i, q, False)

        class Group:
            def __init__(self, i, t):
                self.g, self.r, self.q, self.turn = i * 4 + t, t % 4, t % 2, i + t // 4

        def after(eng, which, val):
            if not (isinstance(val, int) and val <= 0):
                eng.wait_ge(which, val)

        def quads(eng, n, body, begin=0, end=None):
            if begin == 0:
                for t in range(4):
                    body(Group(0, t))
            turns = n // 4 if end is None else end
            if turns > max(begin, 1):
                with eng.Fori(max(begin, 1), turns) as i:
                    for t in range(4):
                        body(Group(i, t))
            if end is None:
                for t in range(n % 4):
                    body(Group(n // 4, t))

        def pipe(eng, n, step, part=1, between=None, extra=None):
            def at(i, t, all_in=False):
                step(*[Group(i, t + d) if all_in or 0 <= 4 * i + t + d < n else None for d in (2, 1, 0, -1)])
            turns = (n - 2) // 4
            for t in range(-2, 4):
                at(0, t)
                if extra and t >= 0:
                    extra(0, t)
            if part > 1:
                with eng.Fori(1, part) as i:
                    for t in range(4):
                        at(i, t, True)
                        if extra:
                            extra(i, t)
            if between:
                between()
            with eng.Fori(part, turns) as i:
                for t in range(4):
                    at(i, t, True)
            for t in range(4 * turns, n + 1):
                at(0, t)

        @block.sync
        def _(sp):
            sp.dma_start(key_i[0], t["dst"].rearrange("(p j) -> p j", p=EP)).then_inc(S["keys"], 16)
            sp.dma_start(key_i[1], t["src"].rearrange("(p j) -> p j", p=EP)).then_inc(S["keys"], 16)
            sp.wait_ge(S["x"], 1)
            sp.dma_start(X[:, 0:NF, :], t["x"][0:NF * P, :].rearrange("(c p) d -> p c d", p=P)).then_inc(S["wts"], 16)
            sp.dma_start(X[0:NR, NF, :], t["x"][NF * P:N, :]).then_inc(S["wts"], 16)
            at = 0
            for name, wd in (("L0_gnn_Wl", D), ("L0_gnn_Wr", D), ("L0_gnn_W1", 2 * D), ("L0_gnn_W2", D), ("L2_gnn_W", 2 * D)):
                sp.dma_start(wraw[:, at:at + wd], t[name]).then_inc(S["wts"], 16)
                at += wd
            for k in range(2):
                sp.dma_start(W1a[:, k, :], t[f"L1_gnn_W{k + 1}"][0:2 * D, :]).then_inc(S["wts"], 16)
                sp.dma_start(W1b[:, k, :], t[f"L1_gnn_W{k + 1}"][2 * D:3 * D, :]).then_inc(S["wts"], 16)
                sp.dma_start(Wp[k * D:(k + 1) * D, :, :],
                             t["L3_gnn_W_att"].rearrange("d (q h c) -> h d q c", h=2, c=D)[k]).then_inc(S["wts"], 16)
                sp.dma_start(attsd[:, k, :], t["L3_gnn_att_" + ("src", "dst")[k]].rearrange("h c -> (h c)").unsqueeze(0)
                             .to_broadcast([D, H3 * D])).then_inc(S["wts"], 16)
            sp.dma_start(watt, t["L3_gnn_W_att"]).then_inc(S["wts"], 16)
            sp.dma_start(F1[:], t["L3_gnn_W1"]).then_inc(S["wts"], 16)
            sp.dma_start(F2[:], t["L3_gnn_W2"]).then_inc(S["wts"], 16)
            sp.dma_start(attb[:], t["L0_gnn_att"].rearrange("o h d -> o (h d)").to_broadcast([P, D])).then_inc(S["wts"], 16)
            for k, name in enumerate(("L0_gnn_b2", "L1_gnn_b1", "L1_gnn_b2", "L2_gnn_b", "L3_gnn_b2")):
                sp.dma_start(bias[:, k, :], t[name].unsqueeze(0)).then_inc(S["wts"], 16)
            for k, name in enumerate(("L3_gnn_bias_att", "L3_gnn_ln1_g", "L3_gnn_ln1_b", "L3_gnn_ln2_g", "L3_gnn_ln2_b")):
                sp.dma_start(lnb[:, k, :], t[name].unsqueeze(0).to_broadcast([P, D])).then_inc(S["wts"], 16)
            sp.dma_start(b1c0[:], t["L0_gnn_b1"].unsqueeze(1)).then_inc(S["wts"], 16)
            sp.dma_start(b1c3[:], t["L3_gnn_b1"].unsqueeze(1)).then_inc(S["wts"], 16)
            sp.wait_ge(S["blank"], 4)
            for k in range(2):
                sp.dma_start(recv[:, k * NT // 2:(k + 1) * NT // 2, :].rearrange("p (a b) f -> p a (b f)", b=GT),
                             blank[:].rearrange("p b f -> p (b f)").unsqueeze(1).to_broadcast([P, NG // 2, GT * REC])).then_inc(S["fill"], 16)
            sp.dma_start(slv, slraw[:]).then_inc(S["fill"], 16)

            def attrs(i, q, first):
                if not first:
                    sp.wait_ge(S[f"scat{q}"], i * 16 * GT)
                sp.dma_start(recst[:, q, :, 0:D], attr_v[:, bass.ds((i * 2 + q) * GT, GT), :]).then_inc(S[f"attr{q}"], 16)
            pairs(sp, SG, attrs)

            for q in range(2):
                sp.wait_ge(S[f"scat{q}"], SG * 16 * GT)

            def recs(a):
                after(sp, S["rmm"], a.g - 3)
                sp.dma_start(G[:, a.r, :, 0:REC], recv[:, bass.ds(a.g * GT, GT), :]).then_inc(S[f"rld{a.r}"], 16)
            quads(sp, NG, recs)

            def table(k, n, src):
                sp.wait_ge(S["tsrc"], n)
                sp.dma_start(tab[k].rearrange("(c p) d -> p c d", p=P), src).then_inc(S["tb"], 16)

            def stage_gathers(x, n, R0, mid=None):
                def body(a):
                    after(sp, S[f"{x}g{a.r}"], (R0[a.r] + a.turn) * 16 * GT)
                    sp.dma_start(jst[:, a.r, :], jidx[:, bass.ds(a.g * GT, GT)]).then_inc(S[f"{x}j{a.r}"], 16)
                if mid is None:
                    quads(sp, n, body)
                    return
                quads(sp, n, body, 0, mid)
                for r in range(4):
                    sp.wait_ge(S[f"sscat{r}"], (SR + ST) * 16 * HT)
                sp.dma_start(slraw[:], slv).then_inc(S["slist"], 16)
                quads(sp, n, body, mid, mid + 2)
                sp.wait_ge(S["jdone"], 2)
                quads(sp, n, body, mid + 2)

            table(0, 1, GR)
            sp.wait_ge(S["jdone"], 1)
            stage_gathers("a", NG0, (0,) * 4, MID)
            for r in range(3):
                table(1 + r, 2 + r, Hn[:])
                stage_gathers("c", NG, turns_before(r))
            table(4, 5, TB3)
            stage_gathers("d", NG, (0,) * 4)
            sp.wait_ge(S["xp"], 1)
            sp.dma_start(out[0:NF * P, :].rearrange("(c p) d -> p c d", p=P), OUTN[:, 0:NF, :]).then_inc(S["out"], 16)
            sp.dma_start(out[NF * P:N, :], OUTN[0:NR, NF, :]).then_inc(S["out"], 16)
            sp.wait_ge(S["out"], 32)

        @block.gpsimd
        def _(gp):
            gp.iota(iota_i[:], [[1, P]], base=0, channel_multiplier=0).then_inc(S["iota"], 1)
            gp.memset(ones[:], 1.0).then_inc(S["const"], 1)
            gp.memset(zrow[:], 0.0).then_inc(S["const"], 1)
            gp.memset(pdum[:], 0.0).then_inc(S["pd"], 1)
            gp.memset(X[:], 0.0).then_inc(S["x"], 1)
            gp.memset(blank[:], 0.0).then_inc(S["blank"], 1)
            gp.memset(slraw[:], 0.0).then_inc(S["blank"], 1)
            gp.wait_ge(S["blank"], 2)
            gp.memset(blank[:, :, D + 1:REC], -1.0).then_inc(S["blank"], 1)
            gp.memset(slraw[:, :, 1:2], -1.0).then_inc(S["blank"], 1)
            gp.wait_ge(S["const"], 2)
            gp.affine_select(out=tri[:], in_=ones[:], compare_op=ALU.is_gt, fill=0.0, base=0,
                             pattern=[[1, P]], channel_multiplier=-1).then_inc(S["const"], 1)
            gp.affine_select(out=triinc[:], in_=ones[:], compare_op=ALU.is_ge, fill=0.0, base=0,
                             pattern=[[1, P]], channel_multiplier=-1).then_inc(S["const"], 1)
            gp.affine_select(out=ident[:], in_=ones[:], compare_op=ALU.is_equal, fill=0.0, base=0,
                             pattern=[[1, P]], channel_multiplier=-1).then_inc(S["const"], 1)
            for n, (sel, H) in enumerate(((sel0, H0), (sel3, H3))):
                gp.memset(sel[:], 0.0).then_inc(S["sel"], 1)
                for k in range(3):
                    gp.wait_ge(S["sel"], 4 * n + k + 1)
                    gp.affine_select(out=sel[:], in_=sel[:], compare_op=ALU.not_equal, fill=1.0, base=-k * H,
                                     pattern=[[-1, H], [0, P]], channel_multiplier=1).then_inc(S["sel"], 1)
            gp.wait_ge(S["fill"], 16 * 3)

            def hold(sem_, val, count):
                gp.wait_ge(S["pd"], count)
                gp.wait_ge(sem_, val)
                nc.gpsimd.tensor_tensor(pdum[:, 1:2], pdum[:, 0:1], pdum[:, 0:1], ALU.add).then_inc(S["pd"], 1)

            def scatter_recs(i, q, first):
                hold(S[f"attr{q}"], (i + 1) * 16, i * 4 + 2 * q + 1)
                hold(S["recst"], (2 * i + q + 1) * 3, i * 4 + 2 * q + 2)
                for k in range(GT):
                    gp.indirect_dma_start(rec[:, :], bass.IndirectOffsetOnAxis(ap=rowst[:, q, k:k + 1], axis=0),
                                          recst[:, q, k, :], None).then_inc(S[f"scat{q}"], 16)
            pairs(gp, SG, scatter_recs)

            def scatter_s(g, r, count):
                hold(S["sst"], (g + 1) * 3, count)
                for k in range(HT):
                    gp.indirect_dma_start(slist[:, :], bass.IndirectOffsetOnAxis(ap=rowst[:, r, k:k + 1], axis=0),
                                          sst[:, r, k, :], None).then_inc(S[f"sscat{r}"], 16)
            quads(gp, 4 * SR, lambda a: scatter_s(a.g, a.r, SG * 4 + 1 + a.g))
            held = [SG * 4 + 4 * SR + 1]

            def gather(x, n, R0, k, wd, freed, scatters=0):
                gp.wait_ge(S["tb"], 16 * (k + 1))

                def rows(a, base, per):
                    at = base + a.g * per
                    hold(S[f"{x}j{a.r}"], (R0[a.r] + a.turn + 1) * 16, at)
                    which, val = freed(a)
                    if isinstance(val, int) and val <= 0:
                        which, val = S[f"{x}j{a.r}"], 16
                    hold(which, val, at + 1)
                    for j in range(GT):
                        gp.indirect_dma_start(G[:, a.r, j, 0:wd], None, tab[k][:, :],
                                              bass.IndirectOffsetOnAxis(ap=jst[:, a.r, j:j + 1], axis=0)).then_inc(S[f"{x}g{a.r}"], 16)

                def rows_and_scatter(a):
                    rows(a, held[0], 3)
                    scatter_s(a.g + 4 * SR, a.r, held[0] + a.g * 3 + 2)
                if scatters:
                    quads(gp, n, rows_and_scatter, 0, scatters)
                    held[0] += 4 * scatters
                quads(gp, n, lambda a: rows(a, held[0], 2), scatters)
                held[0] += 2 * n

            gather("a", NG0, (0,) * 4, 0, D, lambda a: (S["av"], a.g - 3), ST)
            for r in range(3):
                gather("c", NG, turns_before(r), 1 + r, D, lambda a: (S["cmm"], r * NG + a.g - 3))
            gather("d", NG, (0,) * 4, 4, D + H3, lambda a: (S["dag"], a.g - 3))

        @block.scalar
        def _(act):
            A = nc.scalar
            act.wait_ge(S["wtp"], 1)
            A.copy(WT[0:D, :, :], pt[0:D, 0:5 * D].rearrange("p (k d) -> p k d", d=D)).then_inc(S["wtc"], 1)
            for k in (2, 4):
                A.copy(WT[D:2 * D, k, :], pt[D:2 * D, k * D:(k + 1) * D]).then_inc(S["wtc"], 1)
            ntc, nln = [0], [0]

            def transposed(K, dst=None):
                for b in range(-(-NC // 4)):
                    m = min(4, NC - 4 * b) * P
                    act.wait_ge(S["tp"], ntc[0] + 1)
                    bank = (ntc[0] % 2) * 512
                    A.copy((T if dst is None else dst)[0:K, b * 512:b * 512 + m], pt[0:K, bank:bank + m]).then_inc(S["tc"], 1)
                    ntc[0] += 1

            def sqrt_():
                nln[0] += 1
                act.wait_ge(S["lnv"], nln[0])
                A.activation(st[:, 2, :], st[:, 1, :], ACT.Sqrt).then_inc(S["lns"], 1)

            def ff_up(n0, func, K, b1):
                for g in range(8):
                    act.wait_ge(S["up"], n0 + g + 1)
                    A.activation(T2[0:K, g * 400:(g + 1) * 400], (pu, accw)[g % 2][0:K, 0:400], func, bias=b1[:]).then_inc(S["upc"], 1)
            sqrt_()
            transposed(D)
            act.wait_ge(S["rows"], 2)

            def stage(i, q, first):
                c = bass.ds((i * 2 + q) * GT, GT)
                if not first:
                    act.wait_ge(S[f"scat{q}"], i * 16 * GT)
                nc.scalar.copy(recst[:, q, :, D:D + 1], idf[1][:, c].unsqueeze(2)).then_inc(S["recst"], 1)
                nc.scalar.copy(recst[:, q, :, D + 1:D + 2], lof[0][:, c].unsqueeze(2)).then_inc(S["recst"], 1)
                nc.scalar.copy(rowst[:, q, :], rowidx[0][:, c]).then_inc(S["recst"], 1)
            pairs(act, SG, stage)
            for q in range(2):
                act.wait_ge(S[f"scat{q}"], SG * 16 * GT)

            def stage_s(s, r, turn):
                c = bass.ds(s * HT, HT)
                after(act, S[f"sscat{r}"], turn * 16 * HT)
                nc.scalar.copy(sst[:, r, :, 0:1], idf[0][:, c].unsqueeze(2)).then_inc(S["sst"], 1)
                nc.scalar.copy(sst[:, r, :, 1:2], lof[1][:, c].unsqueeze(2)).then_inc(S["sst"], 1)
                nc.scalar.copy(rowst[:, r, 0:HT], rowidx[1][:, c]).then_inc(S["sst"], 1)

            def rec_oh(a):
                act.wait_ge(S["roh"], a.g + 1)
                after(act, S["rmm"], a.g - 1)
                nc.scalar.copy(ohb[:, a.q], oh[:, a.r]).then_inc(S["rob"], 1)

            def rec_oh_and_stage(a):
                rec_oh(a)
                stage_s(a.g, a.r, a.turn)
            quads(act, NG, rec_oh_and_stage, 0, SR)
            quads(act, NG, rec_oh, SR)
            for r in range(4):
                stage_s(4 * SR + r, r, SR)

            def attention(x, n, H):
                def rescale(b):
                    act.wait_ge(S[x + "mn"], 3 * b.g + 2)
                    after(act, S[x + "A"], 2 * (b.g - 1))
                    A.activation(cr[:, b.q, 0:H], cr[:, b.q, 0:H], ACT.Exp).then_inc(S[x + "cr"], 1)

                def step(z, a, b, c):
                    def weighted(k):
                        for h in range(H):
                            last = A.activation(V3[:, k, h, :], G[:, c.r, k, 0:D], ACT.Copy,
                                                scale=w[:, c.q, k * H + h:k * H + h + 1])
                        last.then_inc(S[x + "va"], 1)
                    if a:
                        act.wait_ge(S[x + "tr"], a.g + 1)
                        after(act, S[x + "pm"], a.g - 1)
                        src = ptb.rearrange("p (t n) -> p t n", n=P)
                        A.copy(ohT[:, a.q], src).then_inc(S[x + "oht"], 1)
                        after(act, S[x + "mx"], (a.g - 1) * H)
                        A.activation(pen[:, a.q], src, ACT.Copy, bias=-BIG, scale=BIG).then_inc(S[x + "pen"], 1)
                    if c and H == H3:
                        act.wait_ge(S[x + "w"], c.g + 1)
                        after(act, S[x + "ag"], c.g)
                        for k in range(GT - VA, GT):
                            weighted(k)
                    if a:
                        after(act, S[x + "ag"], a.g - 3)
                        A.copy(oh[:, a.r], ohb[:, a.q]).then_inc(S[x + "ohf"], 1)
                    if b and H == H0:
                        rescale(b)
                    if a:
                        act.wait_ge(S[x + "st"], a.g + 1)
                        after(act, S[x + "bc"], H * (a.g - 1))
                        A.copy(sT[0:3 * H, a.q], psT[0:3 * H]).then_inc(S[x + "sc"], 1)
                    if b:
                        if H == H3:
                            rescale(b)
                        act.wait_ge(S[x + "d"], 3 * b.g + 3)
                        after(act, S[x + "ag"], b.g - 1)
                        A.activation(w[:, b.q, 0:GT * H], w[:, b.q, 0:GT * H], ACT.Exp).then_inc(S[x + "w"], 1)
                        if H == H0:
                            act.wait_ge(S[x + "w"], 2 * b.g + 1)
                            A.copy(V0[:, b.q, :, :, D // H0:], w[:, b.q, 0:GT * H].rearrange("p (t h o) -> p t h o", h=H, o=1)
                                   ).then_inc(S[x + "w"], 1)
                if H == H0:
                    pipe(act, n, step, ST - 1, None, lambda i, t: stage_s(i * 4 + t + 4 + 4 * SR, t, i + 1 + SR))
                else:
                    pipe(act, n, step)

            attention("a", NG0, H0)
            transposed(2 * D)
            ff_up(0, ACT.Gelu, D, b1c0)
            sqrt_()
            transposed(2 * D)
            transposed(D, NRT)
            transposed(2 * D)
            sqrt_()
            transposed(2 * D)
            sqrt_()
            transposed(D)

            attention("d", NG, H3)
            for c in range(NC):
                act.wait_ge(S["ftp"], c + 1)
                if c >= 2:
                    act.wait_ge(S["fmm"], c - 1)
                A.copy(TT[c % 2], pt[:, (c % 2) * 512:(c % 2) * 512 + 512]).then_inc(S["ftc"], 1)
            sqrt_()
            transposed(D)
            ff_up(8, ACT.Relu, 2 * D, b1c3)
            sqrt_()

        @block.vector
        def _(v):
            V = nc.vector
            n = [0]

            def link(ins):
                n[0] += 1
                ins.then_inc(S["v"], 1)
                v.wait_ge(S["v"], n[0])

            v.wait_ge(S["iota"], 1)
            link(V.tensor_copy(iota[:], iota_i[:]))
            v.wait_ge(S["const"], 5)
            link(V.tensor_copy(identb[:], ident[:]))
            link(V.tensor_copy(iotab[:], iota[:]))
            link(V.memset(onesb[:], 1.0))
            link(V.memset(sone, 1.0))
            v.wait_ge(S["keys"], 32)
            for l in range(2):
                link(V.tensor_copy(idf[l], key_i[l]))
                link(V.tensor_scalar(low_i, key_i[l], 127, None, ALU.bitwise_and))
                link(V.tensor_copy(lof[l], low_i))
                link(V.tensor_scalar(key_i[l], key_i[l], 7, None, ALU.logical_shift_right))
                link(V.tensor_copy(bkf[l], key_i[l]))
                link(V.memset(slot[l], 0.0))
            base = n[0]
            with v.Fori(0, NC) as b:
                bs = iota[0:EP, bass.ds(b, 1)]
                for l in range(2):
                    V.tensor_scalar(mask[l], bkf[l], bs, 0.0, ALU.is_equal, ALU.add,
                                    accum_out=cnt[l][:, bass.ds(b, 1)]).then_inc(S["cnt"], 1)
                v.wait_ge(S["cnt"], b * 2 + 2)
            v.wait_ge(S["tot"], 1)
            link(V.tensor_scalar(tcol[:], pu[0:NC, 0:2], float(GT * P - 1), None, ALU.add))
            link(V.tensor_copy(tcol_i[:], tcol[:]))
            link(V.tensor_scalar(tcol_i[:], tcol_i[:], (GT * P).bit_length() - 1, None, ALU.logical_shift_right))
            link(V.tensor_copy(tcol[:], tcol_i[:]))
            for l in range(2):
                last = V.tensor_scalar(t128[:, l, :], ones[0:NC, 0:EP], tcol[:, l:l + 1], float(GT * P), ALU.mult, ALU.mult)
                last.then_inc(S["tcol"], 1)
            v.wait_ge(S["end"], 1)
            link(V.tensor_copy(endc[:], pu[0:NC, 8:10]))
            for l in range(2):
                link(V.tensor_copy(off[l][:], pu[0:EP, 64 + 32 * l:64 + 32 * l + NC]))
            for l in range(2):
                V.tensor_scalar(gmat[:, l, :], iota[0:NC, 0:NG], endc[:, l:l + 1], None, ALU.is_ge).then_inc(S["gm"], 1)
            v.wait_ge(S["ct"], 1)
            V.tensor_scalar(ctab[:, :], acc[0:1, 0:2 * NG], float(NC - 1), None, ALU.min).then_inc(S["ctab"], 1)
            with v.Fori(0, NC) as b:
                bs = iota[0:EP, bass.ds(b, 1)]
                for l in range(2):
                    V.tensor_scalar(mask[l], bkf[l], bs, None, ALU.is_equal).then_inc(S["vl"], 1)
                v.wait_ge(S["vl"], b * 7 + 2)
                for l in range(2):
                    V.tensor_tensor_scan(pos[l], sone, mask[l], off[l][:, bass.ds(b, 1)], ALU.mult, ALU.add).then_inc(S["vl"], 1)
                v.wait_ge(S["vl"], b * 7 + 4)
                V.memset(vdum[:, 0:1], 0.0).then_inc(S["vl"], 1)
                for l in range(2):
                    V.copy_predicated(slot[l], mask[l].bitcast(U), pos[l]).then_inc(S["vl"], 1)
                v.wait_ge(S["vl"], b * 7 + 7)
            for l in range(2):
                link(V.tensor_scalar(key_i[0], slot[l], -1.0, None, ALU.add))
                link(V.tensor_scalar(key_i[1], key_i[0], 7, None, ALU.logical_shift_right))
                link(V.tensor_scalar(key_i[0], key_i[0], 127, None, ALU.bitwise_and))
                link(V.tensor_copy(pos[0], key_i[0]))
                link(V.tensor_copy(pos[1], key_i[1]))
                link(V.scalar_tensor_tensor(slot[l], pos[0], float(NT), pos[1], ALU.mult, ALU.add))
                V.tensor_copy(rowidx[l][:], slot[l]).then_inc(S["rows"], 1)

            nln = [0]

            def norm(dst, src, g=None, b=None):
                link(V.tensor_reduce(st[:, 0, :], src, AX, ALU.add))
                link(V.tensor_scalar(st[:, 0, :], st[:, 0, :], 1.0 / D, None, ALU.mult))
                link(V.tensor_tensor(XC, src, st[:, 0, :].unsqueeze(2).to_broadcast([P, NC, D]), ALU.subtract))
                link(V.tensor_tensor(SQ, XC, XC, ALU.mult))
                link(V.tensor_reduce(st[:, 1, :], SQ, AX, ALU.add))
                V.tensor_scalar(st[:, 1, :], st[:, 1, :], 1.0 / D, EPS, ALU.mult, ALU.add).then_inc(S["lnv"], 1)
                nln[0] += 1
                v.wait_ge(S["lns"], nln[0])
                link(V.reciprocal(st[:, 3, :], st[:, 2, :]))
                link(V.tensor_tensor(XC, XC, st[:, 3, :].unsqueeze(2).to_broadcast([P, NC, D]), ALU.mult))
                if g is None:
                    link(V.tensor_scalar(dst, XC, 0.0, None, ALU.max))
                else:
                    link(V.tensor_tensor(XC, XC, lnb[:, g, :].unsqueeze(1).to_broadcast([P, NC, D]), ALU.mult))
                    link(V.tensor_tensor(dst, XC, lnb[:, b, :].unsqueeze(1).to_broadcast([P, NC, D]), ALU.add))

            acc_n = acc[:, 0:NC * D].rearrange("p (c d) -> p c d", d=D)
            v.wait_ge(S["wts"], 16 * 31)
            for k in range(2):
                link(V.tensor_tensor(attsd[:, k, :], attsd[:, k, :], watt, ALU.mult))
                link(V.tensor_reduce(Asd[:, k, :], attsd[:, k, :].rearrange("p (h c) -> p h c", c=D), AX, ALU.add))
            link(V.memset(M[:], -BIG))

            def parts_of(rows, H, width):
                p = [own[H].rearrange("p (c k d) -> p c k d", k=3, d=width)[:, :, k, :] for k in range(3)]
                left = SQ[:, :, 0:width]
                link(V.tensor_copy(p[0], rows))
                link(V.tensor_tensor(left, rows, p[0], ALU.subtract))
                link(V.tensor_copy(p[1], left))
                link(V.tensor_tensor(p[2], left, p[1], ALU.subtract))
            norm(Hn[:], X[:])
            V.memset(vdum[:, 0:1], 0.0).then_inc(S["ev"], 1)
            v.wait_ge(S["lin"], 1)
            link(V.tensor_copy(GL, acc_n))
            parts_of(GL, H0, D)
            link(V.memset(A0[:], 0.0))
            V.memset(vdum[:, 0:1], 0.0).then_inc(S["ev"], 1)
            v.wait_ge(S["lin"], 2)
            V.tensor_copy(GR, acc_n).then_inc(S["tsrc"], 1)

            def rec_tiles(a):
                v.wait_ge(S[f"rld{a.r}"], (a.turn + 1) * 16)
                c = bass.ds(a.g * GT, GT)
                V.tensor_copy(jidx[:, c].unsqueeze(2), G[:, a.r, :, D:D + 1]).then_inc(S["rcp"], 1)
                V.tensor_copy(iloc[:, c].unsqueeze(2), G[:, a.r, :, D + 1:REC]).then_inc(S["rcp"], 1)
                after(v, S["rmm"], a.g - 3)
                V.tensor_tensor(oh[:, a.r], iota1.unsqueeze(1).to_broadcast([P, GT, P]),
                                G[:, a.r, :, D + 1:REC].to_broadcast([P, GT, P]), ALU.is_equal).then_inc(S["roh"], 1)
            quads(v, NG, rec_tiles)
            v.wait_ge(S["rmm"], NG)
            link(V.tensor_copy(nbr_r[:], acc_n))
            link(V.tensor_copy(deg[:], accw[:, 0:NC]))
            link(V.tensor_scalar(invdeg[:], deg[:], 1.0, None, ALU.max))
            link(V.reciprocal(invdeg[:], invdeg[:]))
            link(V.tensor_scalar(hasin[:], deg[:], 0.0, None, ALU.is_gt))
            deg_b = invdeg[:].unsqueeze(2).to_broadcast([P, NC, D])
            V.tensor_tensor(nbr_r[:], nbr_r[:], deg_b, ALU.mult).then_inc(S["ev"], 1)
            V.memset(vdum[:, 0:1], 0.0).then_inc(S["jdone"], 1)

            def second_list():
                v.wait_ge(S["slist"], 16)
                link(V.tensor_copy(iloc[:, NT:2 * NT], slraw[:, :, 1]))
                link(V.tensor_copy(jidx[:, NT:2 * NT], slraw[:, :, 0]))
                V.memset(vdum[:, 3:4], 0.0).then_inc(S["jdone"], 1)

            def chunk_of(g):
                return nc.values_load(ctab[0:1, bass.ds(g, 1)], engines=[mybir.EngineType.DVE], min_val=0, max_val=NC - 1,
                                      skip_runtime_bounds_check_because="the table is capped at the last chunk")

            def onehots(o, which, a):
                V.tensor_tensor(o, iotab[:].unsqueeze(1).to_broadcast([P, GT, P]),
                                iloc[:, bass.ds(a.g * GT, GT)].unsqueeze(2).to_broadcast([P, GT, P]),
                                ALU.is_equal).then_inc(which, 1)

            def attention(x, n, H):
                HD = D // H0 + 1 if H == H0 else D
                wd = GT * H
                nu = 4 if H == H0 else 2
                Asum = A0 if H == H0 else acc3

                def new_maximum(b):
                    m = M[:, bass.ds(chunk_of(b.g) * H, H)]
                    v.wait_ge(S[x + "mx"], H * (b.g + 1))
                    after(v, S[x + "pm"], b.g - 1)
                    V.tensor_tensor(mn[:, b.q, 0:H], m, mx[:, b.q, 0:H], ALU.max).then_inc(S[x + "mn"], 1)
                    v.wait_ge(S[x + "mn"], 3 * b.g + 1)
                    after(v, S[x + "A"], 2 * (b.g - 1))
                    V.tensor_tensor(cr[:, b.q, 0:H], m, mn[:, b.q, 0:H], ALU.subtract).then_inc(S[x + "mn"], 1)
                    v.wait_ge(S[x + "mn"], 3 * b.g + 2)
                    V.tensor_tensor(m, mn[:, b.q, 0:H], mn[:, b.q, 0:H], ALU.max).then_inc(S[x + "mn"], 1)
                    mp = [mnp[:, b.q, k * H:(k + 1) * H] for k in range(3)]
                    after(v, S[x + "mp"], 4 * b.g)
                    V.tensor_copy(mp[0], mn[:, b.q, 0:H]).then_inc(S[x + "mp"], 1)
                    v.wait_ge(S[x + "mp"], 4 * b.g + 1)
                    V.tensor_tensor(mnr[:, 0:H], mn[:, b.q, 0:H], mp[0], ALU.subtract).then_inc(S[x + "mp"], 1)
                    V.tensor_tensor(mp[1], mn[:, b.q, 0:H], mp[0], ALU.subtract).then_inc(S[x + "mp"], 1)
                    v.wait_ge(S[x + "mp"], 4 * b.g + 3)
                    V.tensor_tensor(mp[2], mnr[:, 0:H], mp[1], ALU.subtract).then_inc(S[x + "mp"], 1)

                def step(z, a, b, c):
                    def maxima(heads):
                        for h in heads:
                            v.wait_ge(S[x + "bc"], H * b.g + h + 1)
                            after(v, S[x + "mx"], H * b.g + h - 1)
                            V.memset(vdum[:, 1 + h % 2:2 + h % 2], 0.0)
                            V.tensor_tensor_reduce(out=junk[:, h % 2], in0=pen[:, b.q].rearrange("p t n -> p (t n)"),
                                                   in1=acc[:, (h % 2) * 1024:(h % 2) * 1024 + 1024], scale=1.0, scalar=-BIG,
                                                   op0=ALU.add, op1=ALU.max, accum_out=mx[:, b.q, h:h + 1]).then_inc(S[x + "mx"], 1)

                    def add_up():
                        cc = chunk_of(c.g)
                        v.wait_ge(S[x + "ag"], c.g + 1)
                        v.wait_ge(S[x + "cr"], c.g + 1)
                        at = 2 * c.g
                        after(v, S[x + "A"], at)
                        so = Asum[:, bass.ds(cc * (H * HD), H * HD)]
                        V.tensor_tensor(so.rearrange("p (h d) -> p h d", h=H), so.rearrange("p (h d) -> p h d", h=H),
                                        cr[:, c.q, 0:H].unsqueeze(2).to_broadcast([P, H, HD]), ALU.mult).then_inc(S[x + "A"], 1)
                        v.wait_ge(S[x + "A"], at + 1)
                        V.tensor_tensor(so, so, accw[:, 0:H * HD], ALU.add).then_inc(S[x + "A"], 1)

                    def add_weights():
                        dn = Dn[:, bass.ds(chunk_of(c.g) * H, H)]
                        v.wait_ge(S["dden"], c.g + 1)
                        v.wait_ge(S[x + "cr"], c.g + 1)
                        after(v, S["ddn"], 2 * c.g)
                        V.tensor_tensor(dn, dn, cr[:, c.q, 0:H], ALU.mult).then_inc(S["ddn"], 1)
                        v.wait_ge(S["ddn"], 2 * c.g + 1)
                        V.tensor_tensor(dn, dn, pu[:, DENC:DENC + H], ALU.add).then_inc(S["ddn"], 1)

                    if b:
                        v.wait_ge(S[x + "pen"], b.g + 1)
                        after(v, S[x + "mn"], 3 * (b.g - 1))
                    if c:
                        v.wait_ge(S[x + "w"], (2 if H == H0 else 1) * (c.g + 1))
                        if H == H0:
                            after(v, S[x + "ag"], c.g - 1)
                            V.tensor_tensor(V0[:, c.q, :, :, 0:D // H0], G[:, c.r, :, 0:D].rearrange("p t (h d) -> p t h d", h=H0),
                                            w[:, c.q, 0:wd].rearrange("p (t h) -> p t h", h=H).unsqueeze(3).to_broadcast([P, GT, H0, D // H0]),
                                            ALU.mult).then_inc(S[x + "v"], 1)
                        else:
                            after(v, S[x + "ag"], c.g)
                            for k in range(GT - VA):
                                V.tensor_tensor(V3[:, k], G[:, c.r, k, 0:D].unsqueeze(1).to_broadcast([P, H, D]),
                                                w[:, c.q, k * H:(k + 1) * H].unsqueeze(2).to_broadcast([P, H, D]),
                                                ALU.mult).then_inc(S[x + "v"], 1)
                    if b:
                        maxima(range(4) if H == H0 else range(2))
                    if z and H == H3:
                        after(v, S[x + "tr"], z.g - 1)
                        after(v, S[x + "ohf"], z.g - 1)
                        onehots(ohb[:, z.q], S[x + "oh"], z)
                    if b and H == H3:
                        maxima(range(2, 3))
                    if b and H == H0:
                        new_maximum(b)
                    if a:
                        v.wait_ge(S[f"{x}g{a.r}"], (a.turn + 1) * 16 * GT)
                        v.wait_ge(S[x + "own"], a.g + 1)
                        s_a = sc[:, a.q, 0:wd]
                        after(v, S[x + "u"], nu * a.g)
                        if H == H0:
                            V.tensor_tensor(work[:], pu[:, :].rearrange("p (t d) -> p t d", d=D), G[:, a.r, :, 0:D], ALU.add).then_inc(S[x + "u"], 1)
                            v.wait_ge(S[x + "u"], nu * a.g + 1)
                            V.scalar_tensor_tensor(work[:], work[:], SLOPE, work[:], ALU.mult, ALU.max).then_inc(S[x + "u"], 1)
                            v.wait_ge(S[x + "u"], nu * a.g + 2)
                            V.tensor_tensor(work[:], work[:], attb[:].unsqueeze(1).to_broadcast([P, GT, D]), ALU.mult).then_inc(S[x + "u"], 1)
                            v.wait_ge(S[x + "u"], nu * a.g + 3)
                            after(v, S[x + "d"], 3 * (a.g - 1))
                            V.tensor_reduce(s_a, work[:].rearrange("p t (h d) -> p (t h) d", h=H0), AX, ALU.add).then_inc(S[x + "u"], 1)
                        else:
                            after(v, S[x + "d"], 3 * (a.g - 1))
                            V.tensor_tensor(s_a.rearrange("p (t h) -> p t h", h=H), pu[:, 0:wd].rearrange("p (t h) -> p t h", h=H),
                                            G[:, a.r, :, D:D + H], ALU.add).then_inc(S[x + "u"], 1)
                            v.wait_ge(S[x + "u"], nu * a.g + 1)
                            V.scalar_tensor_tensor(s_a, s_a, SLOPE, s_a, ALU.mult, ALU.max).then_inc(S[x + "u"], 1)
                        v.wait_ge(S[x + "u"], nu * (a.g + 1))
                        after(v, S[x + "st"], a.g - 1)
                        s3 = s_a.rearrange("p (t h) -> p t h", h=H)
                        r3 = rem[:, 0:wd].rearrange("p (t h) -> p t h", h=H)
                        p3 = [part[:, a.q].rearrange("p t k h -> p (t k h)")[:, 0:3 * wd].rearrange("p (t k h) -> p t k h", k=3, h=H)[:, :, k, :]
                              for k in range(3)]
                        V.tensor_copy(p3[0], s3).then_inc(S[x + "sp"], 1)
                        v.wait_ge(S[x + "sp"], 4 * a.g + 1)
                        V.tensor_tensor(r3, s3, p3[0], ALU.subtract).then_inc(S[x + "sp"], 1)
                        V.tensor_tensor(p3[1], s3, p3[0], ALU.subtract).then_inc(S[x + "sp"], 1)
                        v.wait_ge(S[x + "sp"], 4 * a.g + 3)
                        V.tensor_tensor(p3[2], r3, p3[1], ALU.subtract).then_inc(S[x + "sp"], 1)
                    if c and H == H3:
                        add_weights()
                    if b and H == H3:
                        maxima(range(3, H))
                        new_maximum(b)
                    if c and H == H3:
                        add_up()
                    if b:
                        v.wait_ge(S[x + "pm"], b.g + 1)
                        after(v, S[x + "ag"], b.g - 1)
                        after(v, S[x + "d"], 3 * b.g)
                        w_b = w[:, b.q, 0:wd]
                        pm = (accw if H == H0 else pu)[:, PM:PM + 3 * wd].rearrange("p (t k h) -> p t h k", k=3, h=H)
                        V.tensor_reduce(mne[:, 0:wd].rearrange("p (t h) -> p t h", h=H), pm, AX, ALU.add).then_inc(S[x + "d"], 1)
                        v.wait_ge(S[x + "d"], 3 * b.g + 1)
                        V.tensor_tensor(w_b, sc[:, b.q, 0:wd], mne[:, 0:wd], ALU.subtract).then_inc(S[x + "d"], 1)
                        v.wait_ge(S[x + "d"], 3 * b.g + 2)
                        V.tensor_scalar(w_b, w_b, 0.0, None, ALU.min).then_inc(S[x + "d"], 1)
                    if c and H == H0:
                        add_up()
                    if z and H == H0:
                        after(v, S[x + "tr"], z.g - 1)
                        after(v, S[x + "ohf"], z.g - 1)
                        onehots(ohb[:, z.q], S[x + "oh"], z)
                if H == H0:
                    pipe(v, n, step, MID, second_list)
                else:
                    pipe(v, n, step)
                v.wait_ge(S[x + "A"], 2 * n)
                if H == H3:
                    v.wait_ge(S["ddn"], 2 * n)

            attention("a", NG0, H0)
            A0v = A0[:].rearrange("p (c h e) -> p c h e", c=NC, h=H0)
            den = rden0[:, :, 0:H0]
            link(V.tensor_scalar(den, A0v[:, :, :, D // H0], 1e-16, None, ALU.add))
            link(V.reciprocal(den, den))
            for c in range(NC):
                last = V.tensor_tensor(CAT[:, c, 0:D].rearrange("p (h d) -> p h d", h=H0), A0v[:, c, :, 0:D // H0],
                                       rden0[:, c, 0:H0].unsqueeze(2).to_broadcast([P, H0, D // H0]), ALU.mult)
            last.then_inc(S["v"], 1)
            n[0] += 1
            V.tensor_copy(CAT[:, :, D:2 * D], Hn[:]).then_inc(S["ev"], 1)
            v.wait_ge(S["lin"], 3)
            link(V.tensor_tensor(X[:], X[:], acc_n, ALU.add))
            norm(Hn[:], X[:])
            V.memset(vdum[:, 0:1], 0.0).then_inc(S["tsrc"], 1)

            for r in range(3):
                def gathered(a):
                    after(v, S["cmm"], r * NG + a.g - 3)
                    onehots(oh[:, a.r], S["coh"], a)
                quads(v, NG, gathered)
                v.wait_ge(S["cmm"], (r + 1) * NG)
                link(V.tensor_copy(CAT[:, :, 0:D], Hn[:]))
                link(V.tensor_tensor(CAT[:, :, D:2 * D], acc_n, deg_b, ALU.mult))
                if r == 2:
                    link(V.tensor_tensor(CAT[:, :, D:2 * D], CAT[:, :, D:2 * D], Hn[:], ALU.subtract))
                V.memset(vdum[:, 0:1], 0.0).then_inc(S["ev"], 1)
                v.wait_ge(S["lin"], 4 + r)
                if r == 0:
                    V.tensor_scalar(Hn[:], acc_n, 0.0, None, ALU.max).then_inc(S["tsrc"], 1)
                    continue
                if r == 1:
                    link(V.tensor_scalar(XC, acc_n, 0.0, None, ALU.max))
                else:
                    link(V.tensor_tensor(XC, acc_n, hasin[:].unsqueeze(2).to_broadcast([P, NC, D]), ALU.mult))
                link(V.tensor_tensor(X[:], X[:], XC, ALU.add))
                norm(Hn[:], X[:])
                if r == 1:
                    V.memset(vdum[:, 0:1], 0.0).then_inc(S["tsrc"], 1)
            V.memset(vdum[:, 0:1], 0.0).then_inc(S["ev"], 1)

            v.wait_ge(S["lin"], 7)
            link(V.tensor_copy(AS[:], acc[:, 0:NC * 2 * H3].rearrange("p (c h) -> p c h", h=2 * H3)))
            link(V.tensor_copy(TB3[:, :, 0:D], Hn[:]))
            V.tensor_copy(TB3[:, :, D:D + H3], AS[:, :, 0:H3]).then_inc(S["tsrc"], 1)
            Mv = M[:].rearrange("p (c h) -> p c h", h=H3)
            parts_of(AS[:, :, H3:2 * H3], H3, H3)
            link(V.tensor_tensor(Mv, AS[:, :, 0:H3], AS[:, :, H3:2 * H3], ALU.add))
            link(V.scalar_tensor_tensor(Mv, Mv, SLOPE, Mv, ALU.mult, ALU.max))
            link(V.memset(Dn[:], 1.0))
            v.wait_ge(S["tb"], 16 * 5)
            for h in range(H3):
                last = V.tensor_copy(acc3.rearrange("p (c h d) -> p c h d", h=H3, d=D)[:, :, h, :], Hn[:])
            last.then_inc(S["init3"], 1)
            v.wait_ge(S["init3"], 1)
            attention("d", NG, H3)
            Dv = Dn[:].rearrange("p (c h) -> p c h", h=H3)
            link(V.tensor_scalar(rden[:], Dv, 1e-16, None, ALU.add))
            link(V.reciprocal(rden[:], rden[:]))
            link(V.tensor_scalar(rden[:], rden[:], 1.0 / H3, None, ALU.mult))
            for c in range(NC):
                o = acc3[:, c * H3 * D:(c + 1) * H3 * D].rearrange("p (h d) -> p h d", d=D)
                V.tensor_tensor(o, o, rden[:, c, :].unsqueeze(2).to_broadcast([P, H3, D]), ALU.mult).then_inc(S["fac"], 1)
            v.wait_ge(S["fmm"], NC)
            link(V.tensor_tensor(Hn[:], Hn[:], acc_n, ALU.add))
            link(V.tensor_tensor(Hn[:], Hn[:], lnb[:, 0, :].unsqueeze(1).to_broadcast([P, NC, D]), ALU.add))
            norm(Hn[:], Hn[:], 1, 2)
            V.memset(vdum[:, 0:1], 0.0).then_inc(S["ev"], 1)
            v.wait_ge(S["lin"], 8)
            link(V.tensor_tensor(Hn[:], Hn[:], acc_n, ALU.add))
            norm(Hn[:], Hn[:], 3, 4)
            V.tensor_tensor(OUTN, X[:], Hn[:], ALU.add).then_inc(S["xp"], 1)

        @block.tensor
        def _(pe):
            pe.wait_ge(S["cnt"], 2 * NC)
            pe.wait_ge(S["const"], 5)
            for l in range(2):
                last = nc.tensor.matmul(pu[0:NC, l:l + 1], cnt[l][:], ones[0:EP, 0:1], start=True, stop=True)
            last.then_inc(S["tot"], 1)
            pe.wait_ge(S["tcol"], 2)
            nc.tensor.matmul(pu[0:NC, 8:10], triinc[0:NC, 0:NC], tcol[:], start=True, stop=True)
            for l in range(2):
                o = pu[0:EP, 64 + 32 * l:64 + 32 * l + NC]
                nc.tensor.matmul(o, tri[0:EP, 0:EP], cnt[l][:], start=True, stop=False)
                last = nc.tensor.matmul(o, t128[:, l, :], tri[0:NC, 0:NC], start=False, stop=True)
            last.then_inc(S["end"], 1)
            pe.wait_ge(S["gm"], 2)
            last = nc.tensor.matmul(acc[0:1, 0:2 * NG], ones[0:NC, 0:1], gmat[:, :, :].rearrange("p l t -> p (l t)"), start=True, stop=True)
            last.then_inc(S["ct"], 1)

            pe.wait_ge(S["wts"], 16 * 31)
            at = 0
            for k, wd in enumerate((D, D, 2 * D, D, 2 * D)):
                last = nc.tensor.transpose(pt[0:wd, k * D:(k + 1) * D], wraw[:, at:at + wd], ident[0:D, 0:D])
                at += wd
            last.then_inc(S["wtp"], 1)
            pe.wait_ge(S["wtc"], 3)
            ntp, nln, nup = [0], [0], [0]

            def transposes(src, K):
                for b in range(-(-NC // 4)):
                    if ntp[0] >= 2:
                        pe.wait_ge(S["tc"], ntp[0] - 1)
                    bank = (ntp[0] % 2) * 512
                    for j in range(min(4, NC - 4 * b)):
                        last = nc.tensor.transpose(pt[0:K, bank + j * P:bank + (j + 1) * P], src[:, 4 * b + j, :], ident[:])
                    last.then_inc(S["tp"], 1)
                    ntp[0] += 1

            def product(parts, width, bk=None):
                pe.wait_ge(S["tc"], ntp[0])
                for c in range(NC):
                    o = acc[:, c * width:(c + 1) * width]
                    for n, (TL, K, R) in enumerate(parts):
                        last = nc.tensor.matmul(o, TL[0:K, c * P:(c + 1) * P], R, start=n == 0, stop=n == len(parts) - 1 and bk is None)
                    if bk is not None:
                        last = nc.tensor.matmul(o, ones[0:1, :], bias[:, bk, :], start=False, stop=True)
                last.then_inc(S["lin"], 1)

            def hidden(W, K, n0):
                pe.wait_ge(S["tc"], ntp[0])
                for g in range(8):
                    if g >= 2:
                        pe.wait_ge(S["upc"], n0 + g - 1)
                    nc.tensor.matmul((pu, accw)[g % 2][0:W.shape[1], 0:400], W, T[0:K, g * 400:(g + 1) * 400],
                                     start=True, stop=True).then_inc(S["up"], 1)
                pe.wait_ge(S["upc"], n0 + 8)

            def zero_acc():
                for k in range(4):
                    nc.tensor.matmul(acc[:, k * 512:(k + 1) * 512], zrow[0:1, 0:P], zrow[0:1, :], start=True, stop=True,
                                     skip_group_check=True)
                zero_accw()

            def zero_accw():
                nc.tensor.matmul(accw[:, :], zrow[0:1, 0:P], zrow[0:1, :], start=True, stop=True, skip_group_check=True)

            pe.wait_ge(S["ctab"], 1)
            pe.wait_ge(S["ev"], 1)
            transposes(Hn[:], D)
            product([(T, D, WT[0:D, 0, :])], D)
            pe.wait_ge(S["ev"], 2)
            product([(T, D, WT[0:D, 1, :])], D)
            pe.wait_ge(S["tsrc"], 1)

            def chunk_of(g):
                return nc.values_load(ctab[0:1, bass.ds(g, 1)], engines=[mybir.EngineType.PE], min_val=0, max_val=NC - 1,
                                      skip_runtime_bounds_check_because="the table is capped at the last chunk")

            zero_acc()

            def rec_mm(a):
                chunk = chunk_of(a.g)
                pe.wait_ge(S["rob"], a.g + 1)
                pe.wait_ge(S["roh"], a.g + 1)
                o, od = acc[:, bass.ds(chunk * D, D)], accw[:, bass.ds(chunk, 1)]
                for k in range(GT):
                    nc.tensor.matmul(o, oh[:, a.r, k, :], G[:, a.r, k, 0:D], start=False, stop=True, skip_group_check=True)
                    last = nc.tensor.matmul(od, ohb[:, a.q, k, :], onesb[:], start=False, stop=True, skip_group_check=True)
                last.then_inc(S["rmm"], 1)
            quads(pe, NG, rec_mm)

            def attention(x, n, H, width):
                sel = sel0 if H == H0 else sel3
                HD = D // H0 + 1 if H == H0 else D
                pmb = accw if H == H0 else pu

                def step(z, a, b, c):
                    def spread(h):
                        after(pe, S[x + "mx"], H * b.g + h - 1)
                        for j in range(2):
                            last = nc.tensor.matmul(acc[:, (h % 2) * 1024 + j * 512:(h % 2) * 1024 + j * 512 + 512], sel[:, h, :],
                                                    sT[0:3 * H, b.q, j * 512:(j + 1) * 512], start=True, stop=True)
                        last.then_inc(S[x + "bc"], 1)
                    def own_rows():
                        at = chunk_of(a.g) * (3 * width)
                        pe.wait_ge(S[x + "oht"], a.g + 1)
                        after(pe, S[x + "u"], (4 if H == H0 else 2) * (a.g - 1) + 1)
                        for k in range(GT):
                            for j in range(3):
                                last = nc.tensor.matmul(pu[:, k * width:(k + 1) * width], ohT[:, a.q, k, :],
                                                        own[H][:, bass.ds(at + j * width, width)], start=j == 0, stop=j == 2)
                        last.then_inc(S[x + "own"], 1)

                    def parts_transposed():
                        pe.wait_ge(S[x + "sp"], 4 * (a.g + 1))
                        after(pe, S[x + "sc"], a.g)
                        pa = part[:, a.q].rearrange("p t k h -> p (t k h)")
                        for k in range(GT):
                            last = nc.tensor.transpose(psT[0:3 * H, k * P:(k + 1) * P], pa[:, k * 3 * H:(k + 1) * 3 * H], identb[:])
                        last.then_inc(S[x + "st"], 1)

                    def gathered(k):
                        if H == H0:
                            left = V0[:, c.q, k].rearrange("p h e -> p (h e)")
                        else:
                            left = V3[:, k].rearrange("p h d -> p (h d)")
                            if k < GT - VA:
                                pe.wait_ge(S[x + "v"], (GT - VA) * c.g + k + 1)
                            else:
                                pe.wait_ge(S[x + "va"], VA * c.g + k - (GT - VA) + 1)
                        m = nc.tensor.matmul(accw[:, 0:H * HD], oh[:, c.r, k, :], left, start=k == 0, stop=k == GT - 1)
                        if k == GT - 1:
                            m.then_inc(S[x + "ag"], 1)

                    if b:
                        pe.wait_ge(S[x + "sc"], b.g + 1)
                        spread(0)
                        spread(1)
                    if a:
                        pe.wait_ge(S[x + "oh"], a.g + 1)
                        after(pe, S[x + "pen"], a.g)
                        after(pe, S[x + "oht"], a.g)
                        for k in range(GT):
                            last = nc.tensor.transpose(ptb[:, k * P:(k + 1) * P], ohb[:, a.q, k, :], identb[:])
                        last.then_inc(S[x + "tr"], 1)
                    if H == H0:
                        if b:
                            spread(2)
                            spread(3)
                        if a:
                            own_rows()
                    if c:
                        after(pe, S[x + "A"], 2 * c.g)
                        pe.wait_ge(S[x + "ohf"], c.g + 1)
                        if H == H0:
                            pe.wait_ge(S[x + "v"], c.g + 1)
                        else:
                            pe.wait_ge(S[x + "w"], c.g + 1)
                            after(pe, S["ddn"], 2 * c.g)
                            for k in range(GT):
                                last = nc.tensor.matmul(pu[:, DENC:DENC + H], oh[:, c.r, k, :], w[:, c.q, k * H:(k + 1) * H],
                                                        start=k == 0, stop=k == GT - 1)
                            last.then_inc(S["dden"], 1)
                    for k in range(GT):
                        if c:
                            gathered(k)
                        if b and H == H3 and k + 2 < H:
                            spread(k + 2)
                        if a and H == H3 and k == 0:
                            own_rows()
                        if a and H == H3 and k == 5:
                            parts_transposed()
                    if b:
                        pe.wait_ge(S[x + "mp"], 4 * (b.g + 1))
                        after(pe, S[x + "d"], 3 * b.g - 2)
                        if a and H == H3:
                            pe.wait_ge(S[x + "u"], 2 * a.g + 1)
                        for k in range(GT):
                            last = nc.tensor.matmul(pmb[:, PM + k * 3 * H:PM + (k + 1) * 3 * H], ohT[:, b.q, k, :], mnp[:, b.q, 0:3 * H],
                                                    start=True, stop=True)
                        last.then_inc(S[x + "pm"], 1)
                    if a and H == H0:
                        parts_transposed()
                pipe(pe, n, step)

            pe.wait_ge(S["ev"], 3)
            pe.wait_ge(S["jdone"], 1)
            pe.wait_ge(S["sel"], 8)

            attention("a", NG0, H0, D)
            pe.wait_ge(S["ev"], 4)
            transposes(CAT, 2 * D)
            hidden(WT[:, 2, :], 2 * D, 0)
            product([(T2, D, WT[0:D, 3, :])], D, 0)

            for r in range(3):
                pe.wait_ge(S["tsrc"], 2 + r)
                zero_acc()

                def mean_mm(a):
                    chunk = chunk_of(a.g)
                    pe.wait_ge(S["coh"], r * NG + a.g + 1)
                    pe.wait_ge(S[f"cg{a.r}"], (turns_before(r)[a.r] + a.turn + 1) * 16 * GT)
                    o = acc[:, bass.ds(chunk * D, D)]
                    for k in range(GT):
                        last = nc.tensor.matmul(o, oh[:, a.r, k, :], G[:, a.r, k, 0:D], start=False, stop=True, skip_group_check=True)
                    last.then_inc(S["cmm"], 1)
                quads(pe, NG, mean_mm)
                pe.wait_ge(S["ev"], 5 + r)
                transposes(CAT, 2 * D)
                if r == 0:
                    transposes(nbr_r[:], D)
                if r < 2:
                    product([(T, 2 * D, W1a[:, r, :]), (NRT, D, W1b[:, r, :])], D, 1 + r)
                else:
                    product([(T, 2 * D, WT[:, 4, :])], D, 3)

            pe.wait_ge(S["ev"], 8)
            transposes(Hn[:], D)
            product([(T, D, Asd[:].rearrange("p s h -> p (s h)"))], 2 * H3)
            pe.wait_ge(S["tsrc"], 5)

            pe.wait_ge(S["init3"], 1)
            attention("d", NG, H3, H3)
            for c in range(NC + 1):
                if c < NC:
                    pe.wait_ge(S["fac"], c + 1)
                    if c >= 2:
                        pe.wait_ge(S["ftc"], c - 1)
                    for j in range(4):
                        last = nc.tensor.transpose(pt[:, (c % 2) * 512 + j * P:(c % 2) * 512 + (j + 1) * P],
                                                   acc3[:, c * 512 + j * P:c * 512 + (j + 1) * P], ident[:])
                    last.then_inc(S["ftp"], 1)
                if c:
                    pe.wait_ge(S["ftc"], c)
                    for j in range(4):
                        last = nc.tensor.matmul(acc[:, (c - 1) * D:c * D], TT[(c - 1) % 2][:, j * P:(j + 1) * P], Wp[:, j, :],
                                                start=j == 0, stop=j == 3)
                    last.then_inc(S["fmm"], 1)
            pe.wait_ge(S["ev"], 9)
            transposes(Hn[:], D)
            hidden(F1[:], D, 8)
            product([(T2, 2 * D, F2[:])], D, 4)


_INS = ['x', 'src', 'dst', 'edge_attr_64', 'L0_gnn_Wl', 'L0_gnn_Wr', 'L0_gnn_att', 'L0_gnn_W1', 'L0_gnn_b1', 'L0_gnn_W2', 'L0_gnn_b2',
        'L1_gnn_W1', 'L1_gnn_b1', 'L1_gnn_W2', 'L1_gnn_b2', 'L2_gnn_W', 'L2_gnn_b', 'L3_gnn_W_att', 'L3_gnn_att_src',
        'L3_gnn_att_dst', 'L3_gnn_bias_att', 'L3_gnn_W1', 'L3_gnn_b1', 'L3_gnn_W2', 'L3_gnn_b2', 'L3_gnn_ln1_g', 'L3_gnn_ln1_b',
        'L3_gnn_ln2_g', 'L3_gnn_ln2_b']


def kernel(**inputs):
    import numpy as _np
    import concourse.bacc as _bacc
    from concourse import mybir as _mybir
    from concourse.bass_utils import run_bass_kernel_spmd as _run

    nc = _bacc.Bacc("TRN2", target_bir_lowering=False, num_devices=1)
    arrays, args = {}, {}
    for name in _INS:
        a = _np.ascontiguousarray(inputs[name])
        arrays[f"in_{name}_dram"] = a
        args[name] = nc.dram_tensor(f"in_{name}_dram", a.shape, _mybir.dt.from_np(a.dtype), kind="ExternalInput").ap()
    out = nc.dram_tensor("out_0_dram", (N, D), _mybir.dt.float32, kind="ExternalOutput").ap()
    build(nc, args, out)
    r = _run(nc, [arrays], core_ids=[0])
    return r.results[0]["out_0_dram"]
```
